# Optimizing a Trainium2 kernel written in Bass

```python
import numpy as np
import jax
import jax.numpy as jnp

def _softmax(x, axis=-1):
    return jax.nn.softmax(x, axis=axis)

def _gelu(x):
    return jax.nn.gelu(x, approximate=True)

def _silu(x):
    return jax.nn.silu(x)

def _sigmoid(x):
    return jax.nn.sigmoid(x)

def _layernorm(x, axis=-1, eps=1e-05):
    m = jnp.mean(x, axis=axis, keepdims=True)
    v = jnp.var(x, axis=axis, keepdims=True)
    return (x - m) / jnp.sqrt(v + eps)

def _scatter_add(tgt, idx, src, axis=0):
    return tgt.at[idx].add(src)

def _segment_sum(src, seg, n):
    return jax.ops.segment_sum(src, seg, n)
kernel_name = 'mk_prb_d2_jaxref_r8_aede1c'

def setup_inputs(seed: int=0):
    np.random.seed(seed)
    _w = jnp.asarray

    def _L0_attn_setup():
        import jax, jax.numpy as jnp
        import numpy as np
        D_MODEL, D_STATE, EXPAND = (128, 64, 2)
        D_INNER = EXPAND * D_MODEL
        BATCH, SEQ = (4, 256)

        def _scan_recurrence(a, b):

            def combine(e1, e2):
                a1, b1 = e1
                a2, b2 = e2
                return (a1 * a2, a2 * b1 + b2)
            _, h = jax.lax.associative_scan(combine, (a, b), axis=1)
            return h
        key = jax.random.key(seed)
        ks = jax.random.split(key, 7)
        s = lambda *d: 1.0 / np.sqrt(d[0])
        x = jax.random.normal(ks[0], (BATCH, SEQ, D_MODEL), dtype=jnp.float32)
        W_in = jax.random.normal(ks[1], (D_MODEL, 2 * D_INNER), dtype=jnp.float32) * s(D_MODEL)
        W_xp = jax.random.normal(ks[2], (D_INNER, 2 * D_STATE + 1), dtype=jnp.float32) * s(D_INNER)
        W_B = jax.random.normal(ks[3], (D_STATE, D_INNER), dtype=jnp.float32) * s(D_STATE)
        W_C = jax.random.normal(ks[4], (D_STATE, D_INNER), dtype=jnp.float32) * s(D_STATE)
        W_out = jax.random.normal(ks[5], (D_INNER, D_MODEL), dtype=jnp.float32) * s(D_INNER)
        D = jnp.ones((D_INNER,), dtype=jnp.float32)
        A_log = jnp.asarray(np.log(0.01), dtype=jnp.float32)
        return {'x': x, 'W_in': W_in, 'W_xp': W_xp, 'W_B': W_B, 'W_C': W_C, 'W_out': W_out, 'D': D, 'A_log': A_log}
    _L0_attn_in = _L0_attn_setup()

    def _L0_ffn_setup():
        import jax, jax.numpy as jnp
        import numpy as np
        B, T, D, E, H = (8, 256, 128, 8, 32)
        LN_EPS = 1e-05
        key = jax.random.key(seed)
        ks = jax.random.split(key, 4)
        return {'x': jax.random.normal(ks[0], (B, T, D), dtype=jnp.float32), 'Wg': jax.random.normal(ks[1], (E, D), dtype=jnp.float32) * 0.02, 'ln_scale': jnp.ones((E, D), dtype=jnp.float32), 'ln_bias': jnp.zeros((E, D), dtype=jnp.float32), 'W1': jax.random.normal(ks[2], (E, D, H), dtype=jnp.float32) * 0.02, 'b1': jnp.zeros((E, H), dtype=jnp.float32), 'W2': jax.random.normal(ks[3], (E, H, D), dtype=jnp.float32) * 0.02, 'b2': jnp.zeros((E, D), dtype=jnp.float32)}
    _L0_ffn_in = _L0_ffn_setup()

    def _L1_attn_setup():
        import jax, jax.numpy as jnp
        import numpy as np
        B, T, D = (1, 256, 128)
        H, S, LV = (16, 64, 12)
        HD = D // H
        NEG = -1e+30

        def _level_matrix(length, num_levels):
            t = np.arange(length)
            xor = t[:, None] ^ t[None, :]
            lv = np.zeros((length, length), dtype=np.int32)
            for k in range(num_levels - 1):
                lv += (xor >= 1 << k).astype(np.int32)
            return jnp.asarray(lv)

        def _forward(x, Wq, Wk, Wv, Wdl, Wdt, Wout, A_log, dt_bias, Lp, ln_g, ln_b):
            Bb, Tt, Dd = x.shape
            Q = (x @ Wq.T).reshape(Bb, Tt, H, S)
            K = (x @ Wk.T).reshape(Bb, Tt, H, S)
            V = (x @ Wv.T).reshape(Bb, Tt, H, HD)
            dl = (x @ Wdl.T).reshape(Bb, Tt, H, LV)
            A = -jnp.exp(A_log)
            dt = jax.nn.softplus(x @ Wdt.T + dt_bias)
            g = A[None, None, :] * dt
            Lam = jax.nn.softplus(Lp[None, None] * dl)
            cg = jnp.cumsum(g, axis=1)
            diff = cg[:, :, None, :] - cg[:, None, :, :]
            tri = np.tril(np.ones((Tt, Tt), dtype=bool))
            decay = jnp.exp(jnp.where(tri[None, :, :, None], diff, NEG))
            levels = _level_matrix(Tt, LV)
            lam_ts = jnp.take_along_axis(Lam[:, :, :, None, :], levels[None, :, None, :, None], axis=-1)[..., 0]
            scores = jnp.einsum('bthd,bshd->bhts', Q, K) * S ** (-0.5)
            Wmat = scores * jnp.transpose(decay, (0, 3, 1, 2)) * jnp.transpose(lam_ts, (0, 2, 1, 3))
            Y = jnp.einsum('bhts,bshd->bthd', Wmat, V).reshape(Bb, Tt, H * HD)
            o = Y @ Wout.T + x
            mu = o.mean(-1, keepdims=True)
            var = ((o - mu) ** 2).mean(-1, keepdims=True)
            return (o - mu) * jax.lax.rsqrt(var + 1e-05) * ln_g + ln_b
        ks = jax.random.split(jax.random.key(seed), 8)
        n = jax.random.normal
        w = 0.02
        return {'x': n(ks[0], (B, T, D), jnp.float32), 'Wq': n(ks[1], (H * S, D), jnp.float32) * w, 'Wk': n(ks[2], (H * S, D), jnp.float32) * w, 'Wv': n(ks[3], (H * HD, D), jnp.float32) * w, 'Wdl': n(ks[4], (H * LV, D), jnp.float32) * w, 'Wdt': n(ks[5], (H, D), jnp.float32) * w, 'Wout': n(ks[6], (D, H * HD), jnp.float32) * w, 'A_log': jnp.log(jnp.arange(1, H + 1, dtype=jnp.float32)), 'dt_bias': n(ks[7], (H,), jnp.float32), 'Lp': jnp.ones((H, LV), jnp.float32), 'ln_g': jnp.ones((D,), jnp.float32), 'ln_b': jnp.zeros((D,), jnp.float32)}
    _L1_attn_in = _L1_attn_setup()

    def _L1_ffn_setup():
        import jax, jax.numpy as jnp
        import numpy as np
        from jax import lax
        T, B, I, M, O = (32, 64, 128, 128, 128)

        def _xavier(key, shape):
            fan_out, fan_in = shape
            limit = float(np.sqrt(6.0 / (fan_in + fan_out)))
            return jax.random.uniform(key, shape, jnp.float32, -limit, limit)
        key = jax.random.key(seed)
        ks = jax.random.split(key, 9)
        x = jax.random.normal(ks[0], (T, B, I), jnp.float32)
        return {'x': x, 'wf': _xavier(ks[1], (M, I)), 'uf': _xavier(ks[2], (M, M)), 'bf': jnp.zeros((M,), jnp.float32), 'wi': _xavier(ks[3], (M, I)), 'ui': _xavier(ks[4], (M, M)), 'bi': jnp.zeros((M,), jnp.float32), 'wc': _xavier(ks[5], (M, I)), 'uc': _xavier(ks[6], (M, M)), 'bc': jnp.zeros((M,), jnp.float32), 'wo': _xavier(ks[7], (O, I)), 'uo': _xavier(ks[8], (O, M)), 'bo': jnp.zeros((O,), jnp.float32), 'in_c': jnp.zeros((M,), jnp.float32)}
    _L1_ffn_in = _L1_ffn_setup()
    _d = {'L0_attn_x': _L0_attn_in['x'], 'L0_attn_W_in': _L0_attn_in['W_in'], 'L0_attn_W_xp': _L0_attn_in['W_xp'], 'L0_attn_W_B': _L0_attn_in['W_B'], 'L0_attn_W_C': _L0_attn_in['W_C'], 'L0_attn_W_out': _L0_attn_in['W_out'], 'L0_attn_D': _L0_attn_in['D'], 'L0_attn_A_log': _L0_attn_in['A_log'], 'L0_ffn_Wg': _L0_ffn_in['Wg'], 'L0_ffn_ln_scale': _L0_ffn_in['ln_scale'], 'L0_ffn_ln_bias': _L0_ffn_in['ln_bias'], 'L0_ffn_W1': _L0_ffn_in['W1'], 'L0_ffn_b1': _L0_ffn_in['b1'], 'L0_ffn_W2': _L0_ffn_in['W2'], 'L0_ffn_b2': _L0_ffn_in['b2'], 'L1_attn_Wq': _L1_attn_in['Wq'], 'L1_attn_Wk': _L1_attn_in['Wk'], 'L1_attn_Wv': _L1_attn_in['Wv'], 'L1_attn_Wdl': _L1_attn_in['Wdl'], 'L1_attn_Wdt': _L1_attn_in['Wdt'], 'L1_attn_Wout': _L1_attn_in['Wout'], 'L1_attn_A_log': _L1_attn_in['A_log'], 'L1_attn_dt_bias': _L1_attn_in['dt_bias'], 'L1_attn_Lp': _L1_attn_in['Lp'], 'L1_attn_ln_g': _L1_attn_in['ln_g'], 'L1_attn_ln_b': _L1_attn_in['ln_b'], 'L1_ffn_wf': _L1_ffn_in['wf'], 'L1_ffn_uf': _L1_ffn_in['uf'], 'L1_ffn_bf': _L1_ffn_in['bf'], 'L1_ffn_wi': _L1_ffn_in['wi'], 'L1_ffn_ui': _L1_ffn_in['ui'], 'L1_ffn_bi': _L1_ffn_in['bi'], 'L1_ffn_wc': _L1_ffn_in['wc'], 'L1_ffn_uc': _L1_ffn_in['uc'], 'L1_ffn_bc': _L1_ffn_in['bc'], 'L1_ffn_wo': _L1_ffn_in['wo'], 'L1_ffn_uo': _L1_ffn_in['uo'], 'L1_ffn_bo': _L1_ffn_in['bo'], 'L1_ffn_in_c': _L1_ffn_in['in_c']}
    _x0 = _d['L0_attn_x']
    _d['L0_attn_x'] = jax.random.normal(jax.random.fold_in(jax.random.key(seed), 1), (16, 512, 128), dtype=_x0.dtype)
    del _x0
    return _d

def reference(L0_attn_x, L0_attn_W_in, L0_attn_W_xp, L0_attn_W_B, L0_attn_W_C, L0_attn_W_out, L0_attn_D, L0_attn_A_log, L0_ffn_Wg, L0_ffn_ln_scale, L0_ffn_ln_bias, L0_ffn_W1, L0_ffn_b1, L0_ffn_W2, L0_ffn_b2, L1_attn_Wq, L1_attn_Wk, L1_attn_Wv, L1_attn_Wdl, L1_attn_Wdt, L1_attn_Wout, L1_attn_A_log, L1_attn_dt_bias, L1_attn_Lp, L1_attn_ln_g, L1_attn_ln_b, L1_ffn_wf, L1_ffn_uf, L1_ffn_bf, L1_ffn_wi, L1_ffn_ui, L1_ffn_bi, L1_ffn_wc, L1_ffn_uc, L1_ffn_bc, L1_ffn_wo, L1_ffn_uo, L1_ffn_bo, L1_ffn_in_c):

    def _L0_attn_ref(x, W_in, W_xp, W_B, W_C, W_out, D, A_log):
        import jax, jax.numpy as jnp
        import numpy as np
        D_MODEL, D_STATE, EXPAND = (128, 64, 2)
        D_INNER = EXPAND * D_MODEL
        BATCH, SEQ = (4, 256)

        def _scan_recurrence(a, b):

            def combine(e1, e2):
                a1, b1 = e1
                a2, b2 = e2
                return (a1 * a2, a2 * b1 + b2)
            _, h = jax.lax.associative_scan(combine, (a, b), axis=1)
            return h
        xz = x @ W_in
        xi, z = jnp.split(xz, 2, axis=-1)
        proj = xi @ W_xp
        delta = jax.nn.softplus(proj[..., :1])
        B_raw = proj[..., 1:1 + D_STATE]
        C_raw = proj[..., 1 + D_STATE:]
        B = B_raw @ W_B
        C = C_raw @ W_C
        A = -jnp.exp(A_log)
        A_bar = jnp.exp(delta * A)
        a = jnp.broadcast_to(A_bar, B.shape)
        h = _scan_recurrence(a, B * xi)
        y = C * h + D * xi
        y = y * jax.nn.silu(z)
        return y @ W_out

    def _L0_ffn_ref(x, Wg, ln_scale, ln_bias, W1, b1, W2, b2):
        import jax, jax.numpy as jnp
        import numpy as np
        B, T, D, E, H = (8, 256, 128, 8, 32)
        LN_EPS = 1e-05
        Bs, Ts, Ds = x.shape
        xt = x.reshape(Bs * Ts, Ds)
        logits = xt @ Wg.T
        top1 = jnp.argmax(logits, axis=-1)
        mu = jnp.mean(xt, axis=-1, keepdims=True)
        var = jnp.mean(jnp.square(xt - mu), axis=-1, keepdims=True)
        xhat = (xt - mu) * jax.lax.rsqrt(var + LN_EPS)
        n_experts = Wg.shape[0]

        def body(y, p):
            s_e, b_e, w1, bb1, w2, bb2, eid = p
            h = jax.nn.gelu((xhat * s_e + b_e) @ w1 + bb1, approximate=False)
            out = h @ w2 + bb2
            mask = (top1 == eid)[:, None].astype(out.dtype)
            return (y + mask * out, None)
        y0 = jnp.zeros_like(xt)
        y, _ = jax.lax.scan(body, y0, (ln_scale, ln_bias, W1, b1, W2, b2, jnp.arange(n_experts)))
        return y.reshape(Bs, Ts, Ds)

    def _L1_attn_ref(x, Wq, Wk, Wv, Wdl, Wdt, Wout, A_log, dt_bias, Lp, ln_g, ln_b):
        import jax, jax.numpy as jnp
        import numpy as np
        B, T, D = (1, 256, 128)
        H, S, LV = (16, 64, 12)
        HD = D // H
        NEG = -1e+30

        def _level_matrix(length, num_levels):
            t = np.arange(length)
            xor = t[:, None] ^ t[None, :]
            lv = np.zeros((length, length), dtype=np.int32)
            for k in range(num_levels - 1):
                lv += (xor >= 1 << k).astype(np.int32)
            return jnp.asarray(lv)

        def _forward(x, Wq, Wk, Wv, Wdl, Wdt, Wout, A_log, dt_bias, Lp, ln_g, ln_b):
            Bb, Tt, Dd = x.shape
            Q = (x @ Wq.T).reshape(Bb, Tt, H, S)
            K = (x @ Wk.T).reshape(Bb, Tt, H, S)
            V = (x @ Wv.T).reshape(Bb, Tt, H, HD)
            dl = (x @ Wdl.T).reshape(Bb, Tt, H, LV)
            A = -jnp.exp(A_log)
            dt = jax.nn.softplus(x @ Wdt.T + dt_bias)
            g = A[None, None, :] * dt
            Lam = jax.nn.softplus(Lp[None, None] * dl)
            cg = jnp.cumsum(g, axis=1)
            diff = cg[:, :, None, :] - cg[:, None, :, :]
            tri = np.tril(np.ones((Tt, Tt), dtype=bool))
            decay = jnp.exp(jnp.where(tri[None, :, :, None], diff, NEG))
            levels = _level_matrix(Tt, LV)
            lam_ts = jnp.take_along_axis(Lam[:, :, :, None, :], levels[None, :, None, :, None], axis=-1)[..., 0]
            scores = jnp.einsum('bthd,bshd->bhts', Q, K) * S ** (-0.5)
            Wmat = scores * jnp.transpose(decay, (0, 3, 1, 2)) * jnp.transpose(lam_ts, (0, 2, 1, 3))
            Y = jnp.einsum('bhts,bshd->bthd', Wmat, V).reshape(Bb, Tt, H * HD)
            o = Y @ Wout.T + x
            mu = o.mean(-1, keepdims=True)
            var = ((o - mu) ** 2).mean(-1, keepdims=True)
            return (o - mu) * jax.lax.rsqrt(var + 1e-05) * ln_g + ln_b
        return _forward(x, Wq, Wk, Wv, Wdl, Wdt, Wout, A_log, dt_bias, Lp, ln_g, ln_b)

    def _L1_ffn_ref(x, wf, uf, bf, wi, ui, bi, wc, uc, bc, wo, uo, bo, in_c):
        import jax, jax.numpy as jnp
        import numpy as np
        from jax import lax
        T, B, I, M, O = (32, 64, 128, 128, 128)

        def _xavier(key, shape):
            fan_out, fan_in = shape
            limit = float(np.sqrt(6.0 / (fan_in + fan_out)))
            return jax.random.uniform(key, shape, jnp.float32, -limit, limit)
        batch = x.shape[1]
        c0 = jnp.broadcast_to(in_c, (batch, in_c.shape[0]))

        def step(c, xt):
            ft = jax.nn.sigmoid(xt @ wf.T + c @ uf.T + bf)
            it = jax.nn.sigmoid(xt @ wi.T + c @ ui.T + bi)
            gt = jnp.tanh(xt @ wc.T + c @ uc.T + bc)
            c = ft * c + it * gt
            return (c, None)
        c_final, _ = lax.scan(step, c0, x)
        h = jnp.tanh(jnp.einsum('tbi,oi->tbo', x, wo) + c_final @ uo.T + bo)
        return h
    x = L0_attn_x
    xn = _layernorm(x, axis=-1)
    x = x + _L0_attn_ref(xn, L0_attn_W_in, L0_attn_W_xp, L0_attn_W_B, L0_attn_W_C, L0_attn_W_out, L0_attn_D, L0_attn_A_log) + _L0_ffn_ref(xn, L0_ffn_Wg, L0_ffn_ln_scale, L0_ffn_ln_bias, L0_ffn_W1, L0_ffn_b1, L0_ffn_W2, L0_ffn_b2)
    xn = _layernorm(x, axis=-1)
    x = x + _L1_attn_ref(xn, L1_attn_Wq, L1_attn_Wk, L1_attn_Wv, L1_attn_Wdl, L1_attn_Wdt, L1_attn_Wout, L1_attn_A_log, L1_attn_dt_bias, L1_attn_Lp, L1_attn_ln_g, L1_attn_ln_b) + _L1_ffn_ref(xn, L1_ffn_wf, L1_ffn_uf, L1_ffn_bf, L1_ffn_wi, L1_ffn_ui, L1_ffn_bi, L1_ffn_wc, L1_ffn_uc, L1_ffn_bc, L1_ffn_wo, L1_ffn_uo, L1_ffn_bo, L1_ffn_in_c)
    return x

_drawn_inputs = setup_inputs


def setup_inputs(seed=0):
    import zlib

    import numpy as np

    out = dict(_drawn_inputs(seed))
    spreads = {'L0_attn_D': (1.0, 0.6),
     'L0_ffn_ln_scale': (1.0, 0.6),
     'L0_ffn_ln_bias': (0.0, 0.8),
     'L0_ffn_b1': (0.0, 0.8),
     'L0_ffn_b2': (0.0, 0.632),
     'L1_attn_Lp': (1.0, 0.6),
     'L1_attn_ln_g': (1.0, 0.6),
     'L1_attn_ln_b': (0.0, 0.76),
     'L1_ffn_bf': (0.0, 0.8),
     'L1_ffn_bi': (0.0, 0.8),
     'L1_ffn_bc': (0.0, 0.8),
     'L1_ffn_bo': (0.0, 0.8),
     'L1_ffn_in_c': (0.0, 0.8)}
    factors = {'L0_ffn_Wg': 4.702,
     'L0_ffn_W1': 8.0,
     'L0_ffn_W2': 8.0,
     'L1_attn_Wq': 8.0,
     'L1_attn_Wk': 8.0,
     'L1_attn_Wv': 8.0,
     'L1_attn_Wdl': 8.0,
     'L1_attn_Wdt': 8.0,
     'L1_attn_Wout': 8.0,
     'L1_attn_A_log': 8.0,
     'L1_attn_dt_bias': 8.0,
     'L1_ffn_wf': 5.826,
     'L1_ffn_uf': 8.0,
     'L1_ffn_wi': 3.948,
     'L1_ffn_ui': 7.964,
     'L1_ffn_uc': 3.235}
    for name, (base, spread) in spreads.items():
        noise = np.random.default_rng([zlib.crc32(name.encode()), seed]).standard_normal(out[name].shape)
        drawn = base * np.exp(spread * noise) if base else spread * noise
        out[name] = jnp.asarray(drawn.astype(out[name].dtype))
    for name, factor in factors.items():
        out[name] = (out[name] * factor).astype(out[name].dtype)
    return out
```

```python
import numpy as np

B, T, D = 16, 512, 128
TILES = T // 128
INNER, STATE = 256, 64
E, HID = 8, 32
H, HS, HD = 16, 64, 8
LEVELS = 10
CHUNK = 32
NODES = 32
EPS = 1e-5
BIG = 1e30


def _weight_columns():
    return {
        "Win": 2 * INNER, "wdelta": 2, "Dskip": 2, "A0": 1, "WgT": 32, "W1": E * HID,
        "lns": E, "lnb": E, "b1": 2, "Wout0": 2 * D, "W2": 2 * D, "b2": D,
        "Wvdw": 128 + 160 + 16 + 128, "dtb": H, "A1": H, "lng": D, "lnbias": D,
        "WoutT": D, "gates_x": 3 * D, "gates_c": 3 * D, "gate_b": 3, "uo": D, "bo": D, "c0": 1,
        "WinT": 2 * D, "WxpT": INNER, "WBC": INNER, "Lp": 160, "Wq": H * D, "Wk": H * D,
    }


def _const_columns():
    return {
        "ident": 128, "sel6": 128, "sel7": 128, "sel_last": 128, "left": 128, "right": NODES,
        "diag": CHUNK, "own_chunk": 4, "own_head": 4, "sum_heads": CHUNK,
        "alpha_mask": 4 * 64, "beta_mask": TILES * 5 * H, "rank": E, "expert": E * HID, "b2_part": 3,
    }


def _offsets(columns):
    at, out = 0, {}
    for name, width in columns.items():
        out[name] = (at, width)
        at += width
    return out, at


def build(nc, x, weights, consts, out):
    import concourse.bass as bass
    from concourse import mybir
    from contextlib import ExitStack

    fp32, bf16 = mybir.dt.float32, mybir.dt.bfloat16
    ACT, ALU, AX = mybir.ActivationFunctionType, mybir.AluOpType, mybir.AxisListType
    wat, wwidth = _offsets(_weight_columns())
    cat, cwidth = _offsets(_const_columns())

    with ExitStack() as ctx:
        def sb(name, cols, dt=fp32, rows=128):
            return ctx.enter_context(nc.sbuf_tensor(name, [rows, cols], dt))

        def psum(name):
            return ctx.enter_context(nc.psum_tensor(name, [128, 512], fp32))

        def sem(name):
            return ctx.enter_context(nc.semaphore(name))

        kept = wat["WinT"][0]
        W = sb("W", kept)
        K = sb("K", cwidth)

        def w(name, a=0, b=None, rows=128):
            at, width = wat[name]
            t = W if at < kept else gx
            at -= 0 if at < kept else kept
            return t[0:rows, at + a:at + (width if b is None else b)]

        def k(name, a=0, b=None, rows=128):
            at, width = cat[name]
            return K[0:rows, at + a:at + (width if b is None else b)]

        ident = k("ident")
        MB = sb("MB", INNER)
        MC = sb("MC", INNER)
        Mdelta = sb("Mdelta", 128)
        G = sb("G", H * 128)
        GT = sb("GT", H * 128)
        bias_u = sb("bias_u", 2)
        neg_a0 = sb("neg_a0", 1)
        neg_a1 = sb("neg_a1", H)
        expert_b = sb("expert_b", E * HID, bf16, 32)
        b2_b = sb("b2_b", D, bf16, 32)
        ones = sb("ones", T, fp32, 16)
        xin = sb("xin", T)
        st0 = sb("st0", TILES * 6)
        mv0 = sb("mv0", TILES * 2)
        sm0 = sb("sm0", 8 * TILES)
        xn = sb("xn", T)
        xh = sb("xh", T)
        xnT = sb("xnT", T)
        xhT = sb("xhT", T)
        sp0 = sb("sp0", T)
        decay0 = sb("decay0", T)
        xi = sb("xi", 2 * T)
        y = sb("y", 2 * T)
        th = sb("th", 2 * T)
        gelu = sb("gelu", 2 * T)
        lgT = sb("lgT", T, fp32, 32)
        oh = sb("oh", T, fp32, 32)
        ohT = lgT
        am = sb("am", 4 * 128 + 64, fp32, 32)
        mask_b = sb("mask_b", T, bf16, 32)
        oh_b = sb("oh_b", T, bf16, 32)
        x1 = sb("x1", T)
        st1 = sb("st1", TILES * 6)
        mv1 = sb("mv1", TILES * 2)
        sm1 = sb("sm1", 4 * TILES)
        xn1 = sb("xn1", T)
        x1T = sb("x1T", T)
        VDW = 432
        vdw = sb("vdw", TILES * VDW)
        lam = sb("lam", TILES * 160)
        dts = sb("dts", 10 * 64)
        cgC = sb("cgC", T, fp32, 16)
        cgt = sb("cgt", 64)
        lev = sb("lev", 256)
        e4 = sb("e4", 256)
        alpha = sb("alpha", 256)
        beta = sb("beta", TILES * 5 * H)
        gx = sb("gx", H * T)
        pair = sb("pair", TILES * 512)
        nodesT = sb("nodesT", TILES * 512)
        self_lam = sb("self_lam", TILES * 512)
        vp = sb("vp", 2048)
        nodes = vp
        vbd = sb("vbd", TILES * 512)
        rs = sb("rs", 2048)
        ms = sb("ms", 2048)
        yt, ytT, ob = rs[:, 0:T], rs[:, T:2 * T], rs[:, 2 * T:3 * T]
        tf, ti, tg = nodesT[:, 0:T], nodesT[:, T:2 * T], nodesT[:, 2 * T:3 * T]
        ym = sb("ym", 2 * 512)
        lv = sb("lv", 512)
        lvs = sb("lvs", 128)
        c2 = sb("c2", T)
        hx_dram = nc.dram_tensor("hx_scratch", (B, 128, T), fp32, kind="Internal").ap()
        res_dram = nc.dram_tensor("res_scratch", (B, 128, T), fp32, kind="Internal").ap()
        res = sb("res", T)
        WQ, WK = w("Wq"), w("Wk")

        P0 = [psum(f"p0_{n}") for n in range(3)]
        P1 = [psum(f"p1_{n}") for n in range(5)]

        names = """loaded folded setup_ps setup_ev setup_done
            x_loaded st0_ready mv0_ready ln0_steps r0_ready vr_steps q0_ready rr_ready xn_ready xh_ready
            xnT_ps xhT_ps xnT_ready xhT_ready logit_ps top1_steps ohT_ready delta_ps sp0_steps delta_ready decay0_ready
            xi0_ps xi1_ps xi0_ready xi1_ready b0_ps b1_ps bx0_ready bx1_ready h0_ready h1_ready
            c0_ps c1_ps ch0_ready ch1_ready yd0_ready yd1_ready z0_ps z1_ps th0_ready th1_ready
            sz0_ready sz1_ready y0_ready y1_ready u0_ps u1_ps g0_ready g1_ready out0_ps x1_ready
            st1_ready mv1_ready ln1_ready r1_ready xn1_ready x1T_ps x1T_ready vdw_ps vdw_ready hx_stored
            lam_steps lam_ready dt_in dt_act dt_steps g_ready gT_ps cgC_ready cgT_ps cgt_ready cgc_ps
            lev_diff lev_neg e4_ready alpha_steps beta_ready vp_ready r_ps r_copied m_ps m_copied
            gx_ps gx_copied cgrow_ready diff_ready diff_min decay_ready nodes_ready nodesT_ready self_ready
            s_ps lam_ps dlam_ready w_ready vbd_ready y1_ps ym_ready y2_ps lev_ps lev_ready levsum_ready
            yt_ready ytT_ps ytT_ready wo_ps ob_ready st2_ready mv2_ready ln2_ready r2_ready n_ready
            res_init ng_ready res_ready res_stored f_ps i_ps g_ps tf_ready ti_ready tg_ready fa_ready ib_ready c_ready
            cp_ps cp_ready fin_loaded0 fin_loaded1 fin_sum fin_tanh fin_add fin_stored""".split()
        R = {n: sem(n) for n in names}

        def later(i, n=0):
            return not (isinstance(i, int) and i == 0 and n == 0)

        def tile(t, n, width=128):
            return t[:, n * width:(n + 1) * width]

        def view(ap, spec, **sizes):
            return ap.rearrange(spec, **sizes)

        def spread(ap, shape):
            return ap.broadcast_to(shape)

        block = ctx.enter_context(nc.Block())

        def schedule(eng, stages, before, after):
            before()
            stages(None, 0)
            stages(0, 1)
            with eng.Fori(1, B - 1) as i:
                stages(i, i + 1)
            stages(B - 1, None)
            after()

        @block.sync
        def _(sp):
            def before():
                sp.dma_start(W[:, :], weights[:, 0:kept]).then_inc(R["loaded"], 16)
                sp.dma_start(gx[:, 0:wwidth - kept], weights[:, kept:wwidth]).then_inc(R["loaded"], 16)
                sp.dma_start(K[:, :], consts).then_inc(R["loaded"], 16)

            def load_x(j):
                if later(j):
                    sp.wait_ge(R["x1_ready"], j)
                src = x[j:j + 1] if isinstance(j, int) else x[bass.ds(j, 1)]
                sp.dma_start(view(xin[:, :], "p (a k d) -> p a k d", a=1, d=D),
                             view(src, "a (k p) d -> p a k d", p=128)).then_inc(R["x_loaded"], 16)

            def row(dram, b):
                return view(dram[b:b + 1] if isinstance(b, int) else dram[bass.ds(b, 1)], "a p n -> p (a n)")

            def store_hx(i):
                sp.wait_ge(R["vdw_ready"], 4 * i + 4)
                sp.dma_start(view(row(hx_dram, i), "p (k d) -> p k d", d=D),
                             view(vdw[:, :], "p (k c) -> p k c", k=TILES)[:, :, 304:432]).then_inc(R["hx_stored"], 16)

            def store_res(i):
                sp.wait_ge(R["res_ready"], i + 1)
                sp.dma_start(row(res_dram, i), res[:, :]).then_inc(R["res_stored"], 16)

            def stages(i, j):
                if j is not None:
                    load_x(j)
                if i is not None:
                    store_hx(i)
                    store_res(i)

            def after():
                sp.wait_ge(R["res_stored"], 16 * B)
                sp.wait_ge(R["hx_stored"], 16 * B)
                sp.wait_ge(R["out0_ps"], B)

                def load(b, buf):
                    sp.dma_start(tile(y, buf, T), row(res_dram, b)).then_inc(R[f"fin_loaded{buf}"], 16)
                    sp.dma_start(tile(gelu, buf, T), row(hx_dram, b)).then_inc(R[f"fin_loaded{buf}"], 16)

                load(0, 0)
                load(1, 1)
                for b in range(B):
                    sp.wait_ge(R["fin_add"], b + 1)
                    sp.dma_start(view(out[b], "(k p) d -> p k d", p=128),
                                 view(tile(y, b % 2, T), "p (k d) -> p k d", d=D)).then_inc(R["fin_stored"], 16)
                    if b + 2 < B:
                        sp.wait_ge(R["fin_stored"], 16 * (b + 1))
                        load(b + 2, b % 2)
                sp.wait_ge(R["fin_stored"], 16 * B)
            schedule(sp, stages, before, after)

        @block.tensor
        def _(pe):
            def before():
                pe.wait_ge(R["loaded"], 48)
                for n, half in enumerate(("B", "C")):
                    rows = slice(64 * n, 64 * n + 64)
                    for q in range(2):
                        mm = pe.matmul(P0[n][:, 256 * q:256 * q + 256],
                                       w("WxpT", 128 * q, 128 * q + 128)[rows, :], w("WBC")[rows, :],
                                       start=True, stop=True)
                mm.then_inc(R["setup_ps"], 1)
                for e in range(E):
                    mm = pe.matmul(P1[0][32 * (e % 4):32 * (e % 4) + 32, e // 4:e // 4 + 1],
                                   w("W1", HID * e, HID * e + HID), w("lnb", e, e + 1), start=True, stop=True)
                mm.then_inc(R["setup_ps"], 1)
                for q in range(2):
                    mm = pe.matmul(P1[1][:, 0:128], w("WinT", 128 * q, 128 * q + 128),
                                   spread(w("wdelta", q, q + 1), [128, 128]), start=(q == 0), stop=(q == 1))
                mm.then_inc(R["setup_ps"], 1)
                pe.wait_ge(R["setup_ev"], 2)
                for n in range(2):
                    for q in range(2):
                        mm = pe.matmul(P1[2][:, 256 * n:256 * n + 256], w("WinT", 128 * q, 128 * q + 128),
                                       tile(xi, n, 512)[:, 256 * q:256 * q + 256], start=(q == 0), stop=(q == 1))
                mm.then_inc(R["setup_ps"], 1)
                for g in range(4):
                    for n, (lhs, rhs) in enumerate(((WQ, WK), (WK, WQ))):
                        bank = (P1[3], P1[4])[n] if g % 2 == 0 else (P0[2], P0[1])[n]
                        if g >= 2:
                            pe.wait_ge(R["setup_ev"], 6 + 2 * (g - 2) + n + 1)
                        for a in range(4):
                            h = 4 * g + a
                            rows, cols = slice(0, HS), slice(D * h, D * h + D)
                            mm = pe.matmul(bank[:, 128 * a:128 * a + 128], lhs[rows, cols], rhs[rows, cols],
                                           start=True, stop=True)
                        mm.then_inc(R["setup_ps"], 1)
                pe.wait_ge(R["setup_done"], 3)

            def turn_x(j):
                if later(j):
                    pe.wait_ge(R["g0_ready"], j)
                pe.wait_ge(R["xn_ready"], j + 1)
                for n in range(TILES):
                    mm = pe.transpose(tile(P0[0], n), tile(xn, n), ident)
                mm.then_inc(R["xnT_ps"], 1)
                if later(j):
                    pe.wait_ge(R["g1_ready"], j)
                pe.wait_ge(R["xh_ready"], j + 1)
                for n in range(TILES):
                    mm = pe.transpose(tile(P0[1], n), tile(xh, n), ident)
                mm.then_inc(R["xhT_ps"], 1)

            def logits(j):
                if later(j):
                    pe.wait_ge(R["x1_ready"], j)
                pe.wait_ge(R["xnT_ready"], j + 1)
                pe.matmul(P0[2][0:32, :], w("WgT"), xnT[:, :], start=True, stop=True).then_inc(R["logit_ps"], 1)
                pe.matmul(P0[0][:, :], Mdelta[:, :], xnT[:, :], start=True, stop=True).then_inc(R["delta_ps"], 1)

            def project(j, bank, free, value, lhs, done):
                pe.wait_ge(R[free], value)
                pe.matmul(P0[bank][:, :], lhs, xnT[:, :], start=True, stop=True).then_inc(R[done], 1)

            def scan_in(j):
                project(j, 1, "xhT_ready", j + 1, w("Win", 0, 128), "xi0_ps")
                project(j, 2, "top1_steps", 7 * j + 1, w("Win", 128, 256), "xi1_ps")
                project(j, 0, "delta_ready", j + 1, MB[:, 0:128], "b0_ps")
                project(j, 1, "xi0_ready", j + 1, MB[:, 128:256], "b1_ps")
                project(j, 2, "xi1_ready", j + 1, MC[:, 0:128], "c0_ps")
                project(j, 0, "bx0_ready", j + 1, MC[:, 128:256], "c1_ps")

            def gate_in(j):
                project(j, 1, "bx1_ready", j + 1, w("Win", 256, 384), "z0_ps")
                project(j, 2, "ch0_ready", j + 1, w("Win", 384, 512), "z1_ps")
                pe.wait_ge(R["top1_steps"], 7 * j + 7)
                for q, bank, free, done in ((0, 0, "ch1_ready", "u0_ps"), (1, 1, "sz0_ready", "u1_ps")):
                    pe.wait_ge(R[free], j + 1)
                    pe.matmul(P0[bank][:, :], expert_b[0:8, 128 * q:128 * q + 128], mask_b[0:8, :],
                              start=True, stop=False)
                    pe.matmul(P0[bank][:, :], w("W1", 128 * q, 128 * q + 128), xhT[:, :],
                              start=False, stop=True).then_inc(R[done], 1)

            def out0(j):
                pe.wait_ge(R["sz1_ready"], j + 1)
                for name in ("y0_ready", "y1_ready", "g0_ready", "g1_ready"):
                    pe.wait_ge(R[name], j + 1)
                for n in range(TILES):
                    o, t = tile(P0[2], n), slice(128 * n, 128 * n + 128)
                    pe.matmul(o, y[:, t], w("Wout0", 0, D), start=True, stop=False)
                    pe.matmul(o, y[:, 128 * n + T:128 * n + T + 128], w("Wout0", D), start=False, stop=False)
                    pe.matmul(o, gelu[:, t], w("W2", 0, D), start=False, stop=False)
                    pe.matmul(o, gelu[:, 128 * n + T:128 * n + T + 128], w("W2", D), start=False, stop=False)
                    mm = pe.matmul(o, oh_b[0:24, t], b2_b[0:24, :], start=False, stop=True)
                mm.then_inc(R["out0_ps"], 1)

            def turn_x1(i):
                if later(i):
                    pe.wait_ge(R["lev_ready"], 4 * i)
                pe.wait_ge(R["xn1_ready"], i + 1)
                for n in range(TILES):
                    mm = pe.transpose(tile(P1[0], n), tile(xn1, n), ident)
                mm.then_inc(R["x1T_ps"], 1)

            def values(i):
                pe.wait_ge(R["x1T_ready"], i + 1)
                for n, free in enumerate(("ob_ready", "tf_ready", "ti_ready", "tg_ready")):
                    if later(i):
                        pe.wait_ge(R[free], i)
                    pe.matmul(P1[1 + n][:, 0:VDW], tile(x1T, n), w("Wvdw"), start=True, stop=True)\
                        .then_inc(R["vdw_ps"], 1)

            def heads(i, a, b):
                for h in range(a, b):
                    if h == 0:
                        pe.wait_ge(R["x1T_ready"], i + 1)
                    elif h < 5:
                        pe.wait_ge(R["vdw_ready"], 4 * i + h)
                    else:
                        pe.wait_ge(R["gx_copied"], 16 * i + h - 4)
                    pe.matmul(P1[h % 5][:, :], tile(G, h), x1T[:, :], start=True, stop=True).then_inc(R["gx_ps"], 1)

            def gates_to_rows(i):
                pe.wait_ge(R["gx_copied"], 16 * i + 13)
                pe.wait_ge(R["g_ready"], i + 1)
                for n in range(TILES):
                    mm = pe.transpose(P1[1][0:16, 128 * n:128 * n + 128],
                                      dts[:, 576 + 16 * n:576 + 16 * n + 16], ident)
                mm.then_inc(R["gT_ps"], 1)

            def sums_to_tokens(i):
                pe.wait_ge(R["loaded"], 48)
                pe.wait_ge(R["cgC_ready"], i + 1)
                for n in range(TILES):
                    mm = pe.transpose(P1[2][:, 16 * n:16 * n + 16], cgC[:, 128 * n:128 * n + 128], k("ident", 0, 16, 16))
                mm.then_inc(R["cgT_ps"], 1)
                pe.wait_ge(R["cgt_ready"], i + 1)
                pe.matmul(P1[2][:, 64:128], k("sel6"), cgt[:, :], start=True, stop=True)
                pe.matmul(P1[2][:, 128:192], k("sel7"), cgt[:, :], start=True, stop=True)
                pe.matmul(P1[2][:, 192:224], k("sel_last"),
                          view(cgt[:, :], "p (a b h) -> p a b h", a=2, b=2)[:, :, 0, :], start=True, stop=True)
                pe.matmul(P1[2][:, 224:240], k("sel_last"), cgt[:, 16:32], start=True, stop=True)\
                    .then_inc(R["cgc_ps"], 1)

            def left_halves(i):
                pe.wait_ge(R["vp_ready"], i + 1)
                for n in range(TILES):
                    if n < 3:
                        pe.wait_ge(R["gx_copied"], 16 * i + 14 + n)
                    else:
                        pe.wait_ge(R["cgC_ready"], i + 1)
                    bank = P1[(3 + n) % 5]
                    if n == 1:
                        pe.matmul(bank[:, 384:512], tile(xn1, 0), vp[:, 512:640], start=True, stop=False)
                        pe.matmul(bank[:, 384:512], tile(xn1, 1), vp[:, 1024:1152], start=False, stop=True)
                    at = (0, 640, 1152, 1664)[n]
                    cols = 512 if n in (0, 2) else 384
                    pe.matmul(bank[:, 0:cols], tile(xn1, n), vp[:, at:at + cols], start=True, stop=True)\
                        .then_inc(R["r_ps"], 1)

            def node_matrices(i):
                pe.wait_ge(R["r_copied"], 4 * i + 4)
                pe.wait_ge(R["lev_diff"], i + 1)
                for g in range(4):
                    bank = P1[(2 + g) % 5]
                    for a in range(4):
                        h = 4 * g + a
                        mm = pe.matmul(bank[:, 120 * a:120 * a + 120], tile(GT, h),
                                       view(rs[:, 0:1920], "p (n c) -> p n c", c=128)[:, :, HD * h:HD * h + HD],
                                       start=True, stop=True)
                    mm.then_inc(R["m_ps"], 1)

            def pairs(i, n):
                if n == 0:
                    pe.wait_ge(R["m_copied"], 4 * i + 4)
                    pe.wait_ge(R["gx_copied"], 16 * i + 16)
                else:
                    pe.wait_ge(R["w_ready"], 4 * i + n)
                for c in range(4):
                    mm = pe.matmul(P1[1][32 * c:32 * c + 32, :], x1T[:, 128 * n + 32 * c:128 * n + 32 * c + 32],
                                   view(gx[:, :], "p (h t) -> p h t", h=H)[:, :, 128 * n + 32 * c:128 * n + 32 * c + 32],
                                   start=True, stop=True)
                mm.then_inc(R["s_ps"], 1)
                if n == 0:
                    pe.wait_ge(R["nodesT_ready"], i + 1)
                    pe.wait_ge(R["self_ready"], i + 1)
                else:
                    pe.wait_ge(R["dlam_ready"], 4 * i + n)
                pe.matmul(P1[2][:, :], k("left"), tile(nodesT, n, 512), start=True, stop=False)
                pe.matmul(P1[2][:, :], ident, tile(self_lam, n, 512), start=False, stop=True).then_inc(R["lam_ps"], 1)

            def levels(i, n):
                pe.wait_ge(R["m_copied"], 4 * i + 4)
                if later(i, n):
                    pe.wait_ge(R["lev_ready"], 4 * i + n)
                node = lambda a: tile(ms, a)
                bank = P1[0]
                for c in range(2):
                    pe.matmul(bank[64 * c:64 * c + 64, 0:128], x1T[:, 128 * n + 64 * c:128 * n + 64 * c + 64],
                              node(4 * n + c), start=True, stop=True)
                full = [4 * n + 2] + [[], [3], [7], [11, 7]][n]
                for a, m in enumerate(full):
                    mm = pe.matmul(bank[:, 128 * (a + 1):128 * (a + 2)], tile(x1T, n), node(m), start=True, stop=True)
                mm.then_inc(R["lev_ps"], 1)

            def chunk_values(i, n):
                if later(i, n):
                    pe.wait_ge(R["ym_ready"], 4 * i + n)
                pe.wait_ge(R["w_ready"], 4 * i + n + 1)
                pe.wait_ge(R["vbd_ready"], 4 * i + n + 1)
                for g in range(4):
                    at = 512 * n + 128 * g
                    mm = pe.matmul(tile(P1[3], g), pair[:, at:at + 128], vbd[:, at:at + 128], start=True, stop=True)
                mm.then_inc(R["y1_ps"], 1)

            def chunk_sums(i, n):
                if later(i, n):
                    pe.wait_ge(R["yt_ready"], 4 * i + n)
                pe.wait_ge(R["ym_ready"], 4 * i + n + 1)
                for c in range(4):
                    mm = pe.matmul(P1[4][32 * c:32 * c + 32, 0:128], k("sum_heads"),
                                   view(tile(ym, n % 2, 512), "p (g c v) -> p g c v", g=4, c=4)[:, :, c, :],
                                   start=True, stop=True)
                mm.then_inc(R["y2_ps"], 1)

            def project_out(i):
                pe.wait_ge(R["w_ready"], 4 * i + 4)
                pe.wait_ge(R["yt_ready"], 4 * i + 4)
                for n in range(TILES):
                    mm = pe.transpose(tile(P1[1], n), tile(yt, n), ident)
                mm.then_inc(R["ytT_ps"], 1)
                pe.wait_ge(R["ytT_ready"], i + 1)
                for n in range(TILES):
                    mm = pe.matmul(tile(P1[1], n), tile(ytT, n), w("WoutT"), start=True, stop=True)
                mm.then_inc(R["wo_ps"], 1)

            def recurrence(i):
                if later(i):
                    pe.wait_ge(R["c_ready"], i)
                for n, (free, value, done) in enumerate((("dlam_ready", 4 * i + 4, "f_ps"), ("ym_ready", 4 * i + 4, "i_ps"),
                                                         ("yt_ready", 4 * i + 4, "g_ps"))):
                    pe.wait_ge(R[free], value)
                    pe.matmul(P1[2 + n][:, :], w("gates_x", 128 * n, 128 * n + 128), x1T[:, :], start=True, stop=False)
                    pe.matmul(P1[2 + n][:, :], w("gates_c", 128 * n, 128 * n + 128), c2[:, :],
                              start=False, stop=True).then_inc(R[done], 1)

            def stages(i, j):
                if i is not None:
                    turn_x1(i)
                    values(i)
                    heads(i, 0, 8)
                if j is not None:
                    turn_x(j)
                    logits(j)
                if i is not None:
                    heads(i, 8, H)
                    gates_to_rows(i)
                    sums_to_tokens(i)
                if j is not None:
                    scan_in(j)
                if i is not None:
                    left_halves(i)
                    node_matrices(i)
                    for n in range(TILES):
                        pairs(i, n)
                        levels(i, n)
                        chunk_values(i, n)
                        chunk_sums(i, n)
                    project_out(i)
                    recurrence(i)
                if j is not None:
                    gate_in(j)
                    out0(j)

            def after():
                pe.wait_ge(R["c_ready"], B)
                pe.wait_ge(R["lev_ready"], 4 * B)
                for n in range(TILES):
                    mm = pe.matmul(tile(P1[0], n), tile(c2, n), w("uo"), start=True, stop=True)
                mm.then_inc(R["cp_ps"], 1)
            schedule(pe, stages, before, after)

        @block.scalar
        def _(act):
            def logs():
                act.preload_act_table_set("natural_log_exp_and_others")

            def gelus():
                act.preload_act_table_set("gelu_and_others")

            def before():
                logs()
                act.wait_ge(R["loaded"], 48)
                act.activation(neg_a0[:, :], w("A0"), ACT.Exp).then_inc(R["setup_ev"], 1)
                act.activation(neg_a1[:, :], w("A1"), ACT.Exp).then_inc(R["setup_done"], 1)
                act.wait_ge(R["setup_ps"], 1)
                for n in range(2):
                    cp = act.activation(tile(xi, n, 512), P0[n][:, :], ACT.Copy)
                cp.then_inc(R["setup_ev"], 1)
                act.wait_ge(R["setup_ps"], 3)
                act.activation(Mdelta[:, :], P1[1][:, 0:128], ACT.Copy).then_inc(R["setup_ev"], 1)
                act.wait_ge(R["setup_ps"], 4)
                act.activation(MB[:, :], P1[2][:, 0:256], ACT.Copy).then_inc(R["setup_ev"], 1)
                act.activation(MC[:, :], P1[2][:, 256:512], ACT.Copy).then_inc(R["setup_ev"], 1)
                act.mul(w("uo"), w("uo"), 0.5).then_inc(R["setup_ev"], 1)
                for g in range(4):
                    for n, dst in enumerate((G, GT)):
                        bank = (P1[3], P1[4])[n] if g % 2 == 0 else (P0[2], P0[1])[n]
                        act.wait_ge(R["setup_ps"], 5 + 2 * g + n)
                        act.activation(tile(dst, g, 512), bank[:, :], ACT.Copy, scale=HS ** -0.5)\
                            .then_inc(R["setup_ev"], 1)
                act.wait_ge(R["setup_ev"], 14)
                act.mul(neg_a0[:, :], neg_a0[:, :], -1.0).then_inc(R["setup_done"], 1)

            def rstd0(j):
                act.wait_ge(R["mv0_ready"], j + 1)
                act.activation(sm0[:, 0:4], view(mv0[:, :], "p (k s) -> p k s", s=2)[:, :, 1], ACT.Ln, bias=EPS_COL)\
                    .then_inc(R["ln0_steps"], 1)
                act.wait_ge(R["ln0_steps"], 2 * j + 1)
                act.activation(sm0[:, 4:8], sm0[:, 0:4], ACT.Exp, scale=-0.5).then_inc(R["r0_ready"], 1)
                act.wait_ge(R["vr_steps"], 2 * j + 2)
                act.activation(sm0[:, 16:20], sm0[:, 12:16], ACT.Ln, bias=EPS_COL).then_inc(R["ln0_steps"], 1)
                act.wait_ge(R["ln0_steps"], 2 * j + 2)
                act.activation(sm0[:, 20:24], sm0[:, 16:20], ACT.Exp, scale=-0.5).then_inc(R["q0_ready"], 1)

            def turned(j):
                if later(j):
                    act.wait_ge(R["z1_ps"], j)
                act.wait_ge(R["xnT_ps"], j + 1)
                act.activation(xnT[:, :], P0[0][:, :], ACT.Copy).then_inc(R["xnT_ready"], 1)
                if later(j):
                    act.wait_ge(R["u1_ps"], j)
                act.wait_ge(R["xhT_ps"], j + 1)
                act.activation(xhT[:, :], P0[1][:, :], ACT.Copy).then_inc(R["xhT_ready"], 1)

            def delta(j):
                act.wait_ge(R["delta_ps"], j + 1)
                if later(j):
                    act.wait_ge(R["delta_ready"], j)
                act.activation(sp0[:, :], P0[0][:, :], ACT.Abs).then_inc(R["sp0_steps"], 1)
                act.wait_ge(R["sp0_steps"], 3 * j + 1)
                act.activation(sp0[:, :], sp0[:, :], ACT.Exp, scale=-1.0).then_inc(R["sp0_steps"], 1)
                act.wait_ge(R["sp0_steps"], 3 * j + 2)
                act.activation(sp0[:, :], sp0[:, :], ACT.Ln, bias=1.0).then_inc(R["sp0_steps"], 1)
                act.wait_ge(R["delta_ready"], j + 1)
                act.activation(decay0[:, :], decay0[:, :], ACT.Exp, scale=neg_a0[:, 0:1]).then_inc(R["decay0_ready"], 1)

            def xi_copy(j):
                if later(j):
                    act.wait_ge(R["yd1_ready"], j)
                for q, bank in ((0, 1), (1, 2)):
                    act.wait_ge(R[f"xi{q}_ps"], j + 1)
                    act.activation(tile(xi, q, T), P0[bank][:, :], ACT.Copy).then_inc(R[f"xi{q}_ready"], 1)

            def gates0(j):
                for q, bank in ((0, 1), (1, 2)):
                    if later(j):
                        act.wait_ge(R[f"y{q}_ready"], j)
                    act.wait_ge(R[f"z{q}_ps"], j + 1)
                    act.activation(tile(th, q, T), P0[bank][:, :], ACT.Tanh, scale=0.5).then_inc(R[f"th{q}_ready"], 1)
                if later(j):
                    act.wait_ge(R["out0_ps"], j)
                for q in range(2):
                    act.wait_ge(R[f"u{q}_ps"], j + 1)
                    act.activation(tile(gelu, q, T), P0[q][:, :], ACT.Gelu, bias=bias_u[:, q:q + 1])\
                        .then_inc(R[f"g{q}_ready"], 1)

            def rstd(i, mv, ready, ln, done):
                act.wait_ge(R[ready], i + 1)
                act.activation(sm1[:, 0:4], view(mv, "p (k s) -> p k s", s=2)[:, :, 1], ACT.Ln, bias=EPS_COL)\
                    .then_inc(R[ln], 1)
                act.wait_ge(R[ln], i + 1)
                act.activation(sm1[:, 4:8], sm1[:, 0:4], ACT.Exp, scale=-0.5).then_inc(R[done], 1)

            def turned1(i):
                if later(i):
                    act.wait_ge(R["g_ps"], i)
                act.wait_ge(R["x1T_ps"], i + 1)
                act.activation(x1T[:, :], P1[0][:, :], ACT.Copy).then_inc(R["x1T_ready"], 1)

            def values(i):
                if later(i):
                    act.wait_ge(R["vbd_ready"], 4 * i)
                if later(i):
                    act.wait_ge(R["vp_ready"], i)
                if later(i):
                    act.wait_ge(R["hx_stored"], 16 * i)
                for n in range(TILES):
                    act.wait_ge(R["vdw_ps"], 4 * i + n + 1)
                    act.activation(tile(vdw, n, VDW), P1[1 + n][:, 0:VDW], ACT.Copy).then_inc(R["vdw_ready"], 1)

            def heads(i, a, b):
                for h in range(a, b):
                    if h == 0:
                        if later(i):
                            act.wait_ge(R["s_ps"], 4 * i)
                    act.wait_ge(R["gx_ps"], 16 * i + h + 1)
                    act.activation(tile(gx, h, T), P1[h % 5][:, :], ACT.Copy).then_inc(R["gx_copied"], 1)

            def gate_logs(i):
                act.wait_ge(R["dt_in"], i + 1)
                act.activation(dts[:, 64:128], dts[:, 0:64], ACT.Abs).then_inc(R["dt_act"], 1)
                act.wait_ge(R["dt_act"], 3 * i + 1)
                act.activation(dts[:, 128:192], dts[:, 64:128], ACT.Exp, scale=-1.0).then_inc(R["dt_act"], 1)
                act.wait_ge(R["dt_act"], 3 * i + 2)
                act.activation(dts[:, 192:256], dts[:, 128:192], ACT.Ln, bias=1.0).then_inc(R["dt_act"], 1)

            def lam_logs(i):
                if later(i):
                    act.wait_ge(R["nodes_ready"], i)
                if later(i):
                    act.wait_ge(R["self_ready"], i)
                if later(i):
                    act.wait_ge(R["alpha_steps"], 2 * i)
                act.wait_ge(R["vdw_ready"], 4 * i + 4)
                act.activation(view(lam[:, :], "p (k c) -> p k c", k=TILES),
                               view(vdw[:, :], "p (k c) -> p k c", k=TILES)[:, :, 128:288], ACT.Abs)\
                    .then_inc(R["lam_steps"], 1)
                act.wait_ge(R["lam_steps"], 3 * i + 1)
                act.activation(lam[:, :], lam[:, :], ACT.Exp, scale=-1.0).then_inc(R["lam_steps"], 1)
                act.wait_ge(R["lam_steps"], 3 * i + 2)
                act.activation(lam[:, :], lam[:, :], ACT.Ln, bias=1.0).then_inc(R["lam_steps"], 1)

            def level_decay(i):
                act.wait_ge(R["lev_neg"], i + 1)
                act.activation(e4[:, :], lev[:, :], ACT.Exp).then_inc(R["e4_ready"], 1)

            def pair_decay(i):
                act.wait_ge(R["diff_min"], i + 1)
                act.activation(pair[:, :], pair[:, :], ACT.Exp).then_inc(R["decay_ready"], 1)

            def left_halves(i):
                if later(i):
                    act.wait_ge(R["m_ps"], 4 * i)
                for n in range(TILES):
                    cols = 384 if n == 3 else 512
                    act.wait_ge(R["r_ps"], 4 * i + n + 1)
                    act.activation(rs[:, 512 * n:512 * n + cols], P1[(3 + n) % 5][:, 0:cols], ACT.Copy)\
                        .then_inc(R["r_copied"], 1)

            def node_matrices(i):
                if later(i):
                    act.wait_ge(R["lev_ps"], 4 * i)
                for g in range(4):
                    act.wait_ge(R["m_ps"], 4 * i + g + 1)
                    src = view(P1[(2 + g) % 5][:, 0:480], "p (a n e) -> p a n e", a=4, e=HD)
                    dst = view(ms[:, 0:1920], "p (n g a e) -> p g a n e", g=4, a=4, e=HD)[:, g]
                    for a in range(4):
                        cp = act.activation(dst[:, a], src[:, a], ACT.Copy)
                    cp.then_inc(R["m_copied"], 1)

            def project_out(i):
                act.wait_ge(R["ytT_ps"], i + 1)
                act.activation(ytT[:, :], P1[1][:, :], ACT.Copy).then_inc(R["ytT_ready"], 1)

            def recurrence(i):
                for n, (ps, dst, done, scale) in enumerate((("f_ps", tf, "tf_ready", 0.5), ("i_ps", ti, "ti_ready", 0.5),
                                                            ("g_ps", tg, "tg_ready", 1.0))):
                    act.wait_ge(R[ps], i + 1)
                    act.activation(dst[:, :], P1[2 + n][:, :], ACT.Tanh, bias=w("gate_b", n, n + 1), scale=scale)\
                        .then_inc(R[done], 1)

            def stages(i, j):
                logs()
                if i is not None:
                    rstd(i, mv1[:, :], "mv1_ready", "ln1_ready", "r1_ready")
                    turned1(i)
                    values(i)
                    gate_logs(i)
                    lam_logs(i)
                    heads(i, 0, 8)
                if j is not None:
                    rstd0(j)
                    turned(j)
                    delta(j)
                if i is not None:
                    heads(i, 8, H)
                if j is not None:
                    xi_copy(j)
                if i is not None:
                    level_decay(i)
                    pair_decay(i)
                    left_halves(i)
                    node_matrices(i)
                    project_out(i)
                    rstd(i, mv1[:, :], "mv2_ready", "ln2_ready", "r2_ready")
                gelus()
                if i is not None:
                    recurrence(i)
                if j is not None:
                    gates0(j)

            def after():
                for b in range(B):
                    act.wait_ge(R["fin_sum"], b + 1)
                    act.activation(tile(gelu, b % 2, T), tile(gelu, b % 2, T), ACT.Tanh).then_inc(R["fin_tanh"], 1)
            EPS_COL = EPS
            schedule(act, stages, before, after)

        @block.vector
        def _(dve):
            def before():
                dve.wait_ge(R["loaded"], 48)
                b2 = w("b2", rows=32)
                steps = [0]

                def step(ins):
                    steps[0] += 1
                    ins.then_inc(R["folded"], 1)
                    dve.wait_ge(R["folded"], steps[0])

                part, rest = am[:, 0:128], am[:, 128:256]
                step(dve.memset(am[:, 256:384], 0.0))
                for n in range(3):
                    step(dve.tensor_copy(b2_b[:, :], b2 if n == 0 else rest))
                    step(dve.tensor_copy(part, b2_b[:, :]))
                    step(dve.tensor_tensor(rest, b2 if n == 0 else rest, part, ALU.subtract))
                    step(dve.scalar_tensor_tensor(am[:, 256:384], part, k("b2_part", n, n + 1, 32), am[:, 256:384],
                                                  ALU.mult, ALU.add))
                step(dve.tensor_copy(b2_b[:, :], am[:, 256:384]))
                step(dve.tensor_copy(expert_b[:, :], k("expert", rows=32)))
                step(dve.memset(oh[:, :], 0.0))
                step(dve.memset(ones[:, :], 1.0))
                dve.wait_ge(R["setup_ps"], 2)
                step(dve.tensor_tensor(bias_u[:, :], P1[0][:, 0:2], w("b1"), ALU.add))
                w1 = view(w("W1"), "p (e h) -> p e h", e=E)
                step(dve.tensor_tensor(w1, w1, spread(w("lns").unsqueeze(2), [128, E, HID]), ALU.mult))
                dl = w("Wvdw", 128, 288)
                step(dve.tensor_tensor(dl, dl, w("Lp"), ALU.mult))
                step(dve.tensor_scalar(w("Wout0"), w("Wout0"), 0.5, None, ALU.mult))
                step(dve.tensor_scalar(w("gates_c"), w("gates_c"), 0.5, None, ALU.mult))
                step(dve.tensor_scalar(w("gate_b", 0, 2), w("gate_b", 0, 2), 0.5, None, ALU.mult))
                step(dve.tensor_scalar(c2[:, :], spread(w("c0"), [128, T]), 2.0, None, ALU.mult))
                dve.wait_ge(R["setup_done"], 1)
                step(dve.tensor_scalar(neg_a1[:, :], neg_a1[:, :], -1.0, None, ALU.mult))
                dve.sem_inc(R["setup_done"], 1)
                dve.wait_ge(R["setup_done"], 3)

            def stats(src, st, mv, st_ready, mv_ready, i):
                for n in range(TILES):
                    last = dve.bn_stats(st[:, 6 * n:6 * n + 6], tile(src, n))
                last.then_inc(R[st_ready], 1)
                dve.wait_ge(R["loaded"], 48)
                dve.wait_ge(R[st_ready], i + 1)
                for n in range(TILES):
                    last = dve.bn_aggr(mv[:, 2 * n:2 * n + 2], st[:, 6 * n:6 * n + 6])
                last.then_inc(R[mv_ready], 1)

            def normalise(dst, src, mv, r):
                for n in range(TILES):
                    last = dve.tensor_scalar(tile(dst, n), tile(src, n), mv[:, 2 * n:2 * n + 1], r[:, n:n + 1],
                                             ALU.subtract, ALU.mult)
                return last

            def norm0(j):
                dve.wait_ge(R["x_loaded"], 16 * (j + 1))
                stats(xin, st0, mv0, "st0_ready", "mv0_ready", j)
                dve.wait_ge(R["r0_ready"], j + 1)
                var, r = view(mv0[:, :], "p (k s) -> p k s", s=2)[:, :, 1], sm0[:, 4:8]
                dve.tensor_tensor(sm0[:, 8:12], var, r, ALU.mult).then_inc(R["vr_steps"], 1)
                if later(j):
                    dve.wait_ge(R["xnT_ps"], j)
                dve.wait_ge(R["vr_steps"], 2 * j + 1)
                dve.tensor_tensor(sm0[:, 12:16], sm0[:, 8:12], r, ALU.mult).then_inc(R["vr_steps"], 1)
                normalise(xn, xin, mv0, r).then_inc(R["xn_ready"], 1)
                dve.wait_ge(R["q0_ready"], j + 1)
                dve.tensor_tensor(sm0[:, 24:28], sm0[:, 20:24], r, ALU.mult).then_inc(R["rr_ready"], 1)
                if later(j):
                    dve.wait_ge(R["xhT_ps"], j)
                dve.wait_ge(R["rr_ready"], j + 1)
                normalise(xh, xin, mv0, sm0[:, 24:28]).then_inc(R["xh_ready"], 1)

            def top1(j):
                dve.wait_ge(R["logit_ps"], j + 1)
                dve.transpose(lgT[:, :], P0[2][0:32, :]).then_inc(R["top1_steps"], 1)
                lg = view(lgT[:, :], "p (c e) -> p c e", e=32)[:, :, 0:E]
                eq = view(am[:, 0:128], "p (c e) -> p c e", e=E)
                val = view(am[:, 128:256], "p (c e) -> p c e", e=E)
                mx, mx2 = am[:, 512:528], am[:, 528:544]
                dve.wait_ge(R["top1_steps"], 7 * j + 1)
                dve.tensor_reduce(mx, lg, AX.X, ALU.max).then_inc(R["top1_steps"], 1)
                dve.wait_ge(R["top1_steps"], 7 * j + 2)
                dve.tensor_tensor(eq, lg, spread(mx.unsqueeze(2), [32, 16, E]), ALU.is_ge).then_inc(R["top1_steps"], 1)
                dve.wait_ge(R["top1_steps"], 7 * j + 3)
                dve.tensor_tensor(val, eq, spread(k("rank", rows=32).unsqueeze(1), [32, 16, E]), ALU.mult)\
                    .then_inc(R["top1_steps"], 1)
                dve.wait_ge(R["top1_steps"], 7 * j + 4)
                dve.tensor_reduce(mx2, val, AX.X, ALU.max).then_inc(R["top1_steps"], 1)
                dve.wait_ge(R["top1_steps"], 7 * j + 5)
                rows = view(oh[:, :], "p (c r e) -> p c r e", c=16, e=E)
                for r in range(3):
                    last = dve.tensor_tensor(rows[:, :, r], val, spread(mx2.unsqueeze(2), [32, 16, E]), ALU.is_equal)
                last.then_inc(R["top1_steps"], 1)
                dve.wait_ge(R["top1_steps"], 7 * j + 6)
                dve.transpose(ohT[:, :], oh[:, :]).then_inc(R["ohT_ready"], 1)
                dve.wait_ge(R["ohT_ready"], j + 1)
                if later(j):
                    dve.wait_ge(R["out0_ps"], j)
                dve.tensor_copy(oh_b[:, :], ohT[:, :])
                dve.tensor_scalar(mask_b[:, :], ohT[:, :], 1.0, BIG, ALU.subtract, ALU.mult)\
                    .then_inc(R["top1_steps"], 1)

            def delta(j):
                dve.wait_ge(R["sp0_steps"], 3 * j + 3)
                if later(j):
                    dve.wait_ge(R["h1_ready"], j)
                dve.scalar_tensor_tensor(decay0[:, :], P0[0][:, :], 0.0, sp0[:, :], ALU.max, ALU.add)\
                    .then_inc(R["delta_ready"], 1)

            def scans(j):
                if later(j):
                    dve.wait_ge(R["out0_ps"], j)
                for q, bank in ((0, 0), (1, 1)):
                    dve.wait_ge(R[f"b{q}_ps"], j + 1)
                    dve.wait_ge(R[f"xi{q}_ready"], j + 1)
                    dve.tensor_tensor(tile(y, q, T), P0[bank][:, :], tile(xi, q, T), ALU.mult)\
                        .then_inc(R[f"bx{q}_ready"], 1)
                dve.wait_ge(R["decay0_ready"], j + 1)
                for q in range(2):
                    dve.wait_ge(R[f"bx{q}_ready"], j + 1)
                    dve.tensor_tensor_scan(tile(y, q, T), decay0[:, :], tile(y, q, T), 0.0, ALU.mult, ALU.add)\
                        .then_inc(R[f"h{q}_ready"], 1)
                for q, bank in ((0, 2), (1, 0)):
                    dve.wait_ge(R[f"c{q}_ps"], j + 1)
                    dve.wait_ge(R[f"h{q}_ready"], j + 1)
                    dve.tensor_tensor(tile(y, q, T), P0[bank][:, :], tile(y, q, T), ALU.mult)\
                        .then_inc(R[f"ch{q}_ready"], 1)
                for q in range(2):
                    dve.wait_ge(R[f"ch{q}_ready"], j + 1)
                    dve.scalar_tensor_tensor(tile(y, q, T), tile(xi, q, T), w("Dskip", q, q + 1), tile(y, q, T),
                                             ALU.mult, ALU.add).then_inc(R[f"yd{q}_ready"], 1)

            def gates0(j):
                for q, bank in ((0, 1), (1, 2)):
                    dve.wait_ge(R[f"th{q}_ready"], j + 1)
                    dve.scalar_tensor_tensor(tile(th, q, T), tile(th, q, T), 1.0, P0[bank][:, :], ALU.add, ALU.mult)\
                        .then_inc(R[f"sz{q}_ready"], 1)
                for q in range(2):
                    dve.wait_ge(R[f"sz{q}_ready"], j + 1)
                    dve.wait_ge(R[f"yd{q}_ready"], j + 1)
                    dve.tensor_tensor(tile(y, q, T), tile(y, q, T), tile(th, q, T), ALU.mult)\
                        .then_inc(R[f"y{q}_ready"], 1)

            def sum0(j):
                dve.wait_ge(R["out0_ps"], j + 1)
                if later(j):
                    dve.wait_ge(R["res_init"], j)
                dve.tensor_tensor(x1[:, :], P0[2][:, :], xin[:, :], ALU.add).then_inc(R["x1_ready"], 1)

            def norm1(i):
                dve.wait_ge(R["x1_ready"], i + 1)
                stats(x1, st1, mv1, "st1_ready", "mv1_ready", i)
                dve.wait_ge(R["r1_ready"], i + 1)
                if later(i):
                    dve.wait_ge(R["ob_ready"], i)
                if later(i):
                    dve.wait_ge(R["r_ps"], 4 * i)
                normalise(xn1, x1, mv1, sm1[:, 4:8]).then_inc(R["xn1_ready"], 1)

            def gates1(i):
                c = lambda n: dts[:, 64 * n:64 * n + 64]
                heads = lambda ap: view(ap, "p (k h) -> p k h", k=TILES)
                dve.wait_ge(R["vdw_ready"], 4 * i + 4)
                dve.tensor_tensor(heads(c(0)), view(vdw[:, :], "p (k c) -> p k c", k=TILES)[:, :, 288:304],
                                  spread(w("dtb").unsqueeze(1), [128, TILES, H]), ALU.add).then_inc(R["dt_in"], 1)
                dve.wait_ge(R["dt_act"], 3 * i + 2)
                dve.tensor_scalar(c(4), c(2), 1.0, 1.0, ALU.add, ALU.subtract).then_inc(R["dt_steps"], 1)
                dve.wait_ge(R["dt_act"], 3 * i + 3)
                dve.wait_ge(R["dt_steps"], 6 * i + 1)
                dve.scalar_tensor_tensor(c(5), c(4), 0.0, c(4), ALU.is_equal, ALU.add).then_inc(R["dt_steps"], 1)
                dve.scalar_tensor_tensor(c(6), c(4), 0.0, c(3), ALU.is_equal, ALU.add)
                dve.wait_ge(R["dt_steps"], 6 * i + 2)
                dve.reciprocal(c(7), c(5)).then_inc(R["dt_steps"], 1)
                dve.wait_ge(R["dt_steps"], 6 * i + 3)
                dve.tensor_tensor(c(7), c(7), c(2), ALU.mult).then_inc(R["dt_steps"], 1)
                dve.wait_ge(R["dt_steps"], 6 * i + 4)
                dve.tensor_tensor(c(7), c(7), c(6), ALU.mult).then_inc(R["dt_steps"], 1)
                dve.wait_ge(R["dt_steps"], 6 * i + 5)
                dve.scalar_tensor_tensor(c(8), c(0), 0.0, c(7), ALU.max, ALU.add).then_inc(R["dt_steps"], 1)
                dve.wait_ge(R["dt_steps"], 6 * i + 6)
                dve.tensor_tensor(heads(c(9)), heads(c(8)), spread(neg_a1[:, :].unsqueeze(1), [128, TILES, H]), ALU.mult)\
                    .then_inc(R["g_ready"], 1)

            def lam_sum(i):
                dve.wait_ge(R["lam_steps"], 3 * i + 3)
                l = view(lam[:, :], "p (k c) -> p k c", k=TILES)
                dve.scalar_tensor_tensor(l, view(vdw[:, :], "p (k c) -> p k c", k=TILES)[:, :, 128:288], 0.0, l,
                                         ALU.max, ALU.add).then_inc(R["lam_ready"], 1)

            def node_rows(i):
                dve.wait_ge(R["lam_ready"], i + 1)
                if later(i):
                    dve.wait_ge(R["r_ps"], 4 * i)
                l = view(lam[:, :], "p (m l) -> p m l", l=LEVELS)
                nd = view(nodes[:, :], "p (m n) -> p m n", n=NODES)
                at = 0
                for level in range(5, 0, -1):
                    count = (CHUNK >> level) + (level == 1)
                    last = dve.tensor_tensor(nd[:, :, at:at + count], spread(l[:, :, level:level + 1], [128, 64, count]),
                                             spread(k("right", at, at + count).unsqueeze(1), [128, 64, count]), ALU.mult)
                    at += count
                last.then_inc(R["nodes_ready"], 1)
                dve.wait_ge(R["nodes_ready"], i + 1)
                if later(i):
                    dve.wait_ge(R["lam_ps"], 4 * i)
                if later(i):
                    dve.wait_ge(R["c_ready"], i)
                dve.transpose(nodesT[:, :], nodes[:, :]).then_inc(R["nodesT_ready"], 1)

            def sums(i):
                dve.wait_ge(R["gT_ps"], i + 1)
                dve.tensor_tensor_scan(cgC[:, :], ones[:, :], P1[1][0:16, :], 0.0, ALU.mult, ALU.add)\
                    .then_inc(R["cgC_ready"], 1)
                dve.wait_ge(R["cgT_ps"], i + 1)
                if later(i):
                    dve.wait_ge(R["diff_ready"], i)
                dve.tensor_copy(cgt[:, :], P1[2][:, 0:64]).then_inc(R["cgt_ready"], 1)
                dve.wait_ge(R["cgt_ready"], i + 1)
                if later(i):
                    dve.wait_ge(R["y1_ps"], 4 * i)
                dve.transpose(view(pair[:, :], "p (m t) -> p m t", t=CHUNK), spread(cgt[:, :].unsqueeze(2), [128, 64, CHUNK]))\
                    .then_inc(R["cgrow_ready"], 1)

            def level_factors(i):
                dve.wait_ge(R["cgc_ps"], i + 1)
                P = P1[2]
                dve.tensor_tensor(view(lev[:, 0:128], "p (a m) -> p a m", a=2), view(P[:, 64:192], "p (a m) -> p a m", a=2),
                                  spread(cgt[:, :].unsqueeze(1), [128, 2, 64]), ALU.subtract)
                dve.tensor_tensor(view(lev[:, 128:192], "p (a b h) -> p a b h", a=2, b=2),
                                  spread(view(P[:, 192:224], "p (a h) -> p a h", a=2).unsqueeze(2), [128, 2, 2, H]),
                                  view(cgt[:, :], "p (a b h) -> p a b h", a=2, b=2), ALU.subtract)
                dve.tensor_tensor(view(lev[:, 192:256], "p (a h) -> p a h", a=TILES),
                                  spread(P[:, 224:240].unsqueeze(1), [128, TILES, H]),
                                  view(cgt[:, :], "p (a h) -> p a h", a=TILES), ALU.subtract).then_inc(R["lev_diff"], 1)
                dve.wait_ge(R["lev_diff"], i + 1)
                dve.scalar_tensor_tensor(lev[:, :], lev[:, :], -1.0, lev[:, :], ALU.mult, ALU.min)\
                    .then_inc(R["lev_neg"], 1)
                dve.wait_ge(R["lam_ready"], i + 1)
                dve.tensor_tensor(view(alpha[:, :], "p (l m) -> p l m", l=4),
                                  view(lam[:, :], "p (m l) -> p l m", l=LEVELS)[:, 6:10],
                                  view(k("alpha_mask"), "p (l m) -> p l m", l=4), ALU.mult).then_inc(R["alpha_steps"], 1)
                dve.wait_ge(R["e4_ready"], i + 1)
                dve.wait_ge(R["alpha_steps"], 2 * i + 1)
                dve.tensor_tensor(alpha[:, :], alpha[:, :], e4[:, :], ALU.mult).then_inc(R["alpha_steps"], 1)
                bt = view(beta[:, :], "p (k s h) -> p k s h", k=TILES, s=5)
                bm = view(k("beta_mask"), "p (k s h) -> p k s h", k=TILES, s=5)
                e = view(e4[:, :], "p (l k h) -> p k l h", l=4, k=TILES)
                if later(i):
                    dve.wait_ge(R["vp_ready"], i)
                dve.tensor_tensor(bt[:, :, 0:2], spread(e[:, :, 0:1], [128, TILES, 2, H]), bm[:, :, 0:2], ALU.mult)
                dve.tensor_tensor(bt[:, :, 2:5], e[:, :, 1:4], bm[:, :, 2:5], ALU.mult).then_inc(R["beta_ready"], 1)

            def pair_min(i):
                dve.wait_ge(R["diff_ready"], i + 1)
                dve.tensor_scalar(pair[:, :], pair[:, :], 0.0, None, ALU.min).then_inc(R["diff_min"], 1)

            def decay_lam(i, n):
                if n == 0:
                    dve.wait_ge(R["decay_ready"], i + 1)
                dve.wait_ge(R["lam_ps"], 4 * i + n + 1)
                dve.tensor_tensor(tile(pair, n, 512), tile(pair, n, 512), P1[2][:, :], ALU.mult)\
                    .then_inc(R["dlam_ready"], 1)
                dve.wait_ge(R["s_ps"], 4 * i + n + 1)
                dve.wait_ge(R["dlam_ready"], 4 * i + n + 1)
                dve.tensor_tensor(tile(pair, n, 512), tile(pair, n, 512), P1[1][:, :], ALU.mult)\
                    .then_inc(R["w_ready"], 1)

            def level_sum(i, n):
                dve.wait_ge(R["lev_ps"], 4 * i + n + 1)
                al = view(alpha[:, :], "p (l k h) -> p k l h", l=4, k=TILES)[:, n]
                runs = [[(0, 0, 2)], [(0, 0, 3)], [(0, 0, 2), (2, 3, 1)], [(0, 0, 4)]][n]
                for at, level, count in runs:
                    o = view(lv[:, 128 * at:128 * (at + count)], "p (l h e) -> p l h e", l=count, e=HD)
                    p = view(P1[0][:, 128 * at:128 * (at + count)], "p (l h e) -> p l h e", l=count, e=HD)
                    last = dve.tensor_tensor(o, p, spread(al[:, level:level + count].unsqueeze(3), [128, count, H, HD]),
                                             ALU.mult)
                last.then_inc(R["lev_ready"], 1)
                dve.wait_ge(R["lev_ready"], 4 * i + n + 1)
                count = sum(r[2] for r in runs)
                dve.tensor_reduce(lvs[:, :], view(lv[:, 0:128 * count], "p (l v) -> p v l", l=count), AX.X, ALU.add)\
                    .then_inc(R["levsum_ready"], 1)

            def own_heads(i, n):
                dve.wait_ge(R["y1_ps"], 4 * i + n + 1)
                if later(i, n // 2):
                    dve.wait_ge(R["y2_ps"], 4 * i + n - 1)
                dve.tensor_tensor(view(tile(ym, n % 2, 512), "p (m a e) -> p m a e", m=16, a=4),
                                  view(P1[3][:, :], "p (m a e) -> p m a e", m=16, a=4),
                                  spread(k("own_head").unsqueeze(1).unsqueeze(3), [128, 16, 4, HD]), ALU.mult)\
                    .then_inc(R["ym_ready"], 1)

            def tile_sum(i, n):
                dve.wait_ge(R["y2_ps"], 4 * i + n + 1)
                dve.wait_ge(R["levsum_ready"], 4 * i + n + 1)
                if n == 0:
                    if later(i):
                        dve.wait_ge(R["ytT_ps"], i)
                dve.tensor_tensor(tile(yt, n), lvs[:, :], P1[4][:, 0:128], ALU.add).then_inc(R["yt_ready"], 1)

            def norm2(i):
                dve.wait_ge(R["wo_ps"], i + 1)
                if later(i):
                    dve.wait_ge(R["ng_ready"], i)
                dve.tensor_tensor(ob[:, :], P1[1][:, :], xn1[:, :], ALU.add).then_inc(R["ob_ready"], 1)
                dve.wait_ge(R["ob_ready"], i + 1)
                stats(ob, st1, mv1, "st2_ready", "mv2_ready", i)
                dve.wait_ge(R["r2_ready"], i + 1)
                normalise(ob, ob, mv1, sm1[:, 4:8]).then_inc(R["n_ready"], 1)

            def recurrence(i):
                dve.wait_ge(R["tf_ready"], i + 1)
                if later(i):
                    dve.wait_ge(R["c_ready"], i)
                dve.scalar_tensor_tensor(tf[:, :], tf[:, :], 1.0, c2[:, :], ALU.add, ALU.mult).then_inc(R["fa_ready"], 1)
                dve.wait_ge(R["tg_ready"], i + 1)
                dve.wait_ge(R["ti_ready"], i + 1)
                dve.scalar_tensor_tensor(ti[:, :], ti[:, :], 1.0, tg[:, :], ALU.add, ALU.mult).then_inc(R["ib_ready"], 1)
                dve.wait_ge(R["fa_ready"], i + 1)
                dve.wait_ge(R["ib_ready"], i + 1)
                dve.wait_ge(R["g_ps"], i + 1)
                dve.scalar_tensor_tensor(c2[:, :], tf[:, :], 0.5, ti[:, :], ALU.mult, ALU.add).then_inc(R["c_ready"], 1)

            def stages(i, j):
                if i is not None:
                    norm1(i)
                    gates1(i)
                    lam_sum(i)
                    node_rows(i)
                if j is not None:
                    norm0(j)
                    top1(j)
                    delta(j)
                if i is not None:
                    sums(i)
                    level_factors(i)
                    pair_min(i)
                if j is not None:
                    scans(j)
                if i is not None:
                    for n in range(TILES):
                        decay_lam(i, n)
                        level_sum(i, n)
                        own_heads(i, n)
                        tile_sum(i, n)
                    norm2(i)
                    recurrence(i)
                if j is not None:
                    gates0(j)
                    sum0(j)

            def after():
                dve.wait_ge(R["cp_ps"], 1)
                dve.tensor_tensor(view(xi[:, 0:T], "p (k d) -> p k d", d=D), view(P1[0][:, :], "p (k d) -> p k d", d=D),
                                  spread(w("bo").unsqueeze(1), [128, TILES, D]), ALU.add).then_inc(R["cp_ready"], 1)
                dve.wait_ge(R["cp_ready"], 1)

                def add_tanh(b):
                    dve.wait_ge(R["fin_tanh"], b + 1)
                    t = tile(y, b % 2, T)
                    dve.tensor_tensor(t, t, tile(gelu, b % 2, T), ALU.add).then_inc(R["fin_add"], 1)

                for b in range(B):
                    dve.wait_ge(R[f"fin_loaded{b % 2}"], 32 * (b // 2 + 1))
                    t = tile(gelu, b % 2, T)
                    dve.tensor_tensor(t, t, xi[:, 0:T], ALU.add).then_inc(R["fin_sum"], 1)
                    if b >= 1:
                        add_tanh(b - 1)
                add_tanh(B - 1)
            schedule(dve, stages, before, after)

        @block.gpsimd
        def _(pool):
            def stages(i, j):
                if i is None:
                    return
                pool.wait_ge(R["x1_ready"], i + 1)
                if later(i):
                    pool.wait_ge(R["res_stored"], 16 * i)
                pool.tensor_tensor(view(res[:, :], "p (k d) -> p k d", d=D), view(x1[:, :], "p (k d) -> p k d", d=D),
                                   spread(w("lnbias").unsqueeze(1), [128, TILES, D]), ALU.add).then_inc(R["res_init"], 1)
                pool.wait_ge(R["lam_ready"], i + 1)
                if later(i):
                    pool.wait_ge(R["lam_ps"], 4 * i)
                pool.tensor_tensor(view(self_lam[:, :], "p (m t) -> p m t", t=CHUNK),
                                   spread(view(lam[:, :], "p (m l) -> p m l", l=LEVELS)[:, :, 0:1], [128, 64, CHUNK]),
                                   spread(k("diag").unsqueeze(1), [128, 64, CHUNK]), ALU.mult).then_inc(R["self_ready"], 1)
                pool.wait_ge(R["cgrow_ready"], i + 1)
                pw = view(pair[:, :], "p (m t) -> p m t", t=CHUNK)
                pool.tensor_tensor(pw, pw, spread(cgt[:, :].unsqueeze(2), [128, 64, CHUNK]), ALU.subtract)\
                    .then_inc(R["diff_ready"], 1)
                pool.wait_ge(R["beta_ready"], i + 1)
                if later(i):
                    pool.wait_ge(R["r_ps"], 4 * i)
                at = 0
                for n, runs in enumerate((((0, 5),), ((0, 3), (4, 1)), ((0, 4),), ((0, 3),))):
                    v = view(vdw[:, VDW * n:VDW * n + 128], "p (h e) -> p h e", e=HD)
                    bt = view(beta[:, 80 * n:80 * n + 80], "p (s h) -> p s h", h=H)
                    for slot, count in runs:
                        last = pool.tensor_tensor(view(vp[:, at:at + 128 * count], "p (s h e) -> p s h e", s=count, e=HD),
                                                  spread(v.unsqueeze(1), [128, count, H, HD]),
                                                  spread(bt[:, slot:slot + count].unsqueeze(3), [128, count, H, HD]),
                                                  ALU.mult)
                        at += 128 * count
                last.then_inc(R["vp_ready"], 1)
                if later(i):
                    pool.wait_ge(R["y1_ps"], 4 * i)
                for n in range(TILES):
                    v = view(vdw[:, VDW * n:VDW * n + 128], "p (g v) -> p g v", g=4)
                    pool.tensor_tensor(view(tile(vbd, n, 512), "p (g c v) -> p g c v", g=4, c=4),
                                       spread(v.unsqueeze(2), [128, 4, 4, 32]),
                                       spread(k("own_chunk").unsqueeze(1).unsqueeze(3), [128, 4, 4, 32]), ALU.mult)\
                        .then_inc(R["vbd_ready"], 1)
                pool.wait_ge(R["n_ready"], i + 1)
                pool.tensor_tensor(view(ob[:, :], "p (k d) -> p k d", d=D), view(ob[:, :], "p (k d) -> p k d", d=D),
                                   spread(w("lng").unsqueeze(1), [128, TILES, D]), ALU.mult).then_inc(R["ng_ready"], 1)
                pool.wait_ge(R["ng_ready"], i + 1)
                pool.tensor_tensor(res[:, :], res[:, :], ob[:, :], ALU.add).then_inc(R["res_ready"], 1)

            schedule(pool, stages, lambda: None, lambda: None)


def _columns_of(a, rows=128):
    n = a.shape[0] // rows
    return a.reshape(n, rows, -1).transpose(1, 0, 2).reshape(rows, -1)


def _pack(columns, parts):
    at, width = _offsets(columns)
    out = np.zeros((128, width), np.float32)
    for name, a in parts.items():
        out[:a.shape[0], at[name][0]:at[name][0] + a.shape[1]] = a
    return out


def _consts():
    p = np.arange(128)
    q, c = p % CHUNK, p // CHUNK
    ident = np.eye(128, dtype=np.float32)
    end6, end7 = 64 * (p // 64) + 31, np.full(128, 63)
    left = np.zeros((128, 128), np.float32)
    right = np.zeros((128, NODES), np.float32)
    at = 0
    for level in range(5, 0, -1):
        size = 1 << level
        for m in range(CHUNK // size):
            inside = (q // size == m)
            first = q % size < size // 2
            right[:, at] = inside & ~first
            for chunk in range(4):
                left[32 * chunk + at, :] = inside & first & (c == chunk)
            at += 1
    alpha = np.zeros((128, 4, TILES, H), np.float32)
    alpha[:, 0] = (p % 64 >= 32)[:, None, None]
    alpha[:, 1] = (p >= 64)[:, None, None]
    alpha[:, 2, 1::2] = 1
    alpha[:, 3, 2:] = 1
    beta = np.zeros((128, TILES, 5, H), np.float32)
    beta[:, :, 0] = (p < 32)[:, None, None]
    beta[:, :, 1] = ((p >= 64) & (p < 96))[:, None, None]
    beta[:, :, 2] = (p < 64)[:, None, None]
    beta[:, 0::2, 3] = 1
    beta[:, 0:2, 4] = 1
    expert = np.zeros((8, E * HID), np.float32)
    for e in range(E):
        expert[e, HID * e:HID * e + HID] = 1
    parts = {
        "ident": ident, "sel6": (p[:, None] == end6[None]).astype(np.float32),
        "sel7": (p[:, None] == end7[None]).astype(np.float32),
        "sel_last": np.repeat((p == 127)[:, None], 128, 1).astype(np.float32),
        "left": left, "right": right, "diag": (q[:, None] == np.arange(CHUNK)).astype(np.float32),
        "own_chunk": (c[:, None] == np.arange(4)).astype(np.float32),
        "own_head": (c[:, None] == np.arange(4)).astype(np.float32),
        "sum_heads": (q[:, None] == np.arange(CHUNK)).astype(np.float32),
        "alpha_mask": alpha.reshape(128, -1), "beta_mask": beta.reshape(128, -1),
        "rank": np.repeat((E - np.arange(E, dtype=np.float32))[None], 32, 0), "expert": expert,
        "b2_part": (np.arange(24)[:, None] // 8 == np.arange(3)).astype(np.float32),
    }
    return _pack(_const_columns(), parts)


def kernel(**inputs):
    import numpy as _np
    import concourse.bacc as _bacc
    from concourse import mybir as _mybir
    from concourse.bass_utils import run_bass_kernel_spmd as _run

    a = {n: _np.asarray(v) for n, v in inputs.items()}
    rows = lambda v, n=128: _np.repeat(v.reshape(1, -1), n, 0)
    w_xp = a["L0_attn_W_xp"]
    parts = {
        "Win": a["L0_attn_W_in"], "wdelta": _columns_of(w_xp[:, 0:1]), "Dskip": _columns_of(a["L0_attn_D"][:, None]),
        "A0": rows(a["L0_attn_A_log"]), "WgT": a["L0_ffn_Wg"].T,
        "W1": a["L0_ffn_W1"].transpose(1, 0, 2).reshape(D, -1), "lns": a["L0_ffn_ln_scale"].T,
        "lnb": a["L0_ffn_ln_bias"].T, "b1": _columns_of(a["L0_ffn_b1"].reshape(-1, 1)),
        "Wout0": _columns_of(a["L0_attn_W_out"]), "W2": _columns_of(a["L0_ffn_W2"].reshape(E * HID, D)),
        "b2": _np.concatenate([a["L0_ffn_b2"]] * 3, 0),
        "WinT": _columns_of(a["L0_attn_W_in"][:, :INNER].T), "WxpT": w_xp[:, 1:].T,
        "WBC": _np.concatenate([a["L0_attn_W_B"], a["L0_attn_W_C"]], 0),
        "Wvdw": _np.concatenate([a["L1_attn_Wv"].T,
                                 a["L1_attn_Wdl"].reshape(H, 12, D)[:, :LEVELS].reshape(-1, D).T,
                                 a["L1_attn_Wdt"].T, a["L1_ffn_wo"].T], 1),
        "Lp": rows(a["L1_attn_Lp"][:, :LEVELS]), "dtb": rows(a["L1_attn_dt_bias"]), "A1": rows(a["L1_attn_A_log"]),
        "lng": rows(a["L1_attn_ln_g"]), "lnbias": rows(a["L1_attn_ln_b"]), "WoutT": a["L1_attn_Wout"].T,
        "gates_x": _np.concatenate([a["L1_ffn_wf"].T, a["L1_ffn_wi"].T, a["L1_ffn_wc"].T], 1),
        "gates_c": _np.concatenate([a["L1_ffn_uf"].T, a["L1_ffn_ui"].T, a["L1_ffn_uc"].T], 1),
        "gate_b": _np.stack([a["L1_ffn_bf"], a["L1_ffn_bi"], a["L1_ffn_bc"]], 1),
        "uo": a["L1_ffn_uo"].T, "bo": rows(a["L1_ffn_bo"]), "c0": a["L1_ffn_in_c"][:, None],
        "Wq": _columns_of(a["L1_attn_Wq"], HS), "Wk": _columns_of(a["L1_attn_Wk"], HS),
    }
    arrays = {
        "in_x": _np.ascontiguousarray(a["L0_attn_x"]),
        "in_weights": _pack(_weight_columns(), parts),
        "in_consts": _consts(),
    }
    nc = _bacc.Bacc("TRN2", target_bir_lowering=False, num_devices=1)
    fp32 = _mybir.dt.float32
    args = [nc.dram_tensor(name, v.shape, fp32, kind="ExternalInput").ap() for name, v in arrays.items()]
    args.append(nc.dram_tensor("out_0", (B, T, D), fp32, kind="ExternalOutput").ap())
    build(nc, *args)
    r = _run(nc, [arrays], core_ids=[0])
    return r.results[0]["out_0"]
```

```python
import numpy as np

B, T, D = 16, 512, 128
TILES = T // 128
INNER, STATE = 256, 64
E, HID = 8, 32
H, HS, HD = 16, 64, 8
LEVELS = 10
CHUNK = 32
NODES = 32
EPS = 1e-5
BIG = 1e30


def _weight_columns():
    return {
        "Win": 2 * INNER, "wdelta": 2, "Dskip": 2, "A0": 1, "WgT": 32, "W1": E * HID,
        "lns": E, "lnb": E, "b1": 2, "Wout0": 2 * D, "W2": 2 * D, "b2": D,
        "Wvdw": 128 + 160 + 16 + 128, "dtb": H, "A1": H, "lng": D, "lnbias": D,
        "WoutT": D, "gates_x": 3 * D, "gates_c": 3 * D, "gate_b": 3, "uo": D, "bo": D, "c0": 1,
        "WinT": 2 * D, "WxpT": INNER, "WBC": INNER, "Lp": 160, "Wq": H * D, "Wk": H * D,
    }


def _const_columns():
    return {
        "ident": 128, "sel6": 128, "sel7": 128, "sel_last": 128, "left": 128, "right": NODES,
        "diag": CHUNK, "own_chunk": 4, "own_head": 4, "sum_heads": CHUNK,
        "alpha_mask": 4 * 64, "beta_mask": TILES * 5 * H, "rank": E, "expert": E * HID, "b2_part": 3,
    }


def _offsets(columns):
    at, out = 0, {}
    for name, width in columns.items():
        out[name] = (at, width)
        at += width
    return out, at


def build(nc, x, weights, consts, out):
    import concourse.bass as bass
    from concourse import mybir
    from contextlib import ExitStack

    fp32, bf16 = mybir.dt.float32, mybir.dt.bfloat16
    ACT, ALU, AX = mybir.ActivationFunctionType, mybir.AluOpType, mybir.AxisListType
    wat, wwidth = _offsets(_weight_columns())
    cat, cwidth = _offsets(_const_columns())

    with ExitStack() as ctx:
        def sb(name, cols, dt=fp32, rows=128):
            return ctx.enter_context(nc.sbuf_tensor(name, [rows, cols], dt))

        def psum(name):
            return ctx.enter_context(nc.psum_tensor(name, [128, 512], fp32))

        def sem(name):
            return ctx.enter_context(nc.semaphore(name))

        kept = wat["WinT"][0]
        W = sb("W", kept)
        K = sb("K", cwidth)

        def w(name, a=0, b=None, rows=128):
            at, width = wat[name]
            t = W if at < kept else gx
            at -= 0 if at < kept else kept
            return t[0:rows, at + a:at + (width if b is None else b)]

        def k(name, a=0, b=None, rows=128):
            at, width = cat[name]
            return K[0:rows, at + a:at + (width if b is None else b)]

        def tile(t, n, width=128):
            return t[:, n * width:(n + 1) * width]

        ident = k("ident")
        MB = sb("MB", INNER)
        MC = sb("MC", INNER)
        Mdelta = sb("Mdelta", 128)
        G = sb("G", H * 128)
        GT = sb("GT", H * 128)
        bias_u = sb("bias_u", 2)
        neg_a0 = sb("neg_a0", 1)
        neg_a1 = sb("neg_a1", H)
        expert_b = sb("expert_b", E * HID, bf16, 32)
        b2_b = sb("b2_b", D, bf16, 32)
        ones = sb("ones", T, fp32, 16)
        xin = sb("xin", T)
        st0 = sb("st0", TILES * 6)
        mv0 = sb("mv0", TILES * 2)
        sm0 = sb("sm0", 8 * TILES)
        xn = sb("xn", T)
        xh = sb("xh", T)
        xnT = sb("xnT", T)
        xhT = sb("xhT", T)
        sp0 = sb("sp0", T)
        decay0 = sb("decay0", T)
        xi = sb("xi", 2 * T)
        y = sb("y", 2 * T)
        th = sb("th", 2 * T)
        gelu = sb("gelu", 2 * T)
        lgT = sb("lgT", T, fp32, 32)
        oh = sb("oh", T, fp32, 32)
        ohT = lgT
        am = sb("am", 4 * 128 + 64, fp32, 32)
        mask_b = sb("mask_b", T, bf16, 32)
        oh_b = sb("oh_b", T, bf16, 32)
        x1 = sb("x1", T)
        st1 = sb("st1", TILES * 6)
        mv1 = sb("mv1", TILES * 2)
        sm1 = sb("sm1", 2 * TILES)
        st2 = sb("st2", TILES * 6)
        mv2 = sb("mv2", TILES * 2)
        sm2 = sb("sm2", 2 * TILES)
        skip = sb("skip", T)
        xn1 = sb("xn1", T)
        x1T = sb("x1T", T)
        VDW = 432
        vdw = sb("vdw", TILES * VDW)
        lam = sb("lam", TILES * 160)
        dts = sb("dts", 10 * 64)
        cgC = sb("cgC", T, fp32, 16)
        cgt = sb("cgt", 64)
        lev = sb("lev", 256)
        e4 = sb("e4", 256)
        alpha = sb("alpha", 256)
        beta = sb("beta", TILES * 5 * H)
        gx = sb("gx", H * T)
        pair = sb("pair", TILES * 512)
        nodesT = sb("nodesT", TILES * 512)
        self_lam = sb("self_lam", TILES * 512)
        vp = sb("vp", 2048)
        nodes = vp
        vbd = sb("vbd", TILES * 512)
        rs = sb("rs", 2048)
        ms = sb("ms", 2048)
        yt, ytT, ob = rs[:, 0:T], rs[:, T:2 * T], rs[:, 2 * T:3 * T]
        tf, ti, tg = sp0, decay0, rs[:, 3 * T:4 * T]
        ym = sb("ym", 2 * 512)
        lv = sb("lv", 512)
        lvs = sb("lvs", 128)
        cell = sb("cell", T)
        hx_dram = nc.dram_tensor("hx_scratch", (B, 128, T), fp32, kind="Internal").ap()
        res_dram = nc.dram_tensor("res_scratch", (B, 128, T), fp32, kind="Internal").ap()
        res = sb("res", T)
        WQ, WK = w("Wq"), w("Wk")

        FIRST = B // 2
        end_hx = [tile(t, n, T) for t in (y, gelu, th, xi) for n in range(2)] + [tile(gx, n, T) for n in range(FIRST)]
        end_res = [xnT[:, :], xhT[:, :], xn[:, :], xh[:, :], xin[:, :]] + [tile(G, n, T) for n in range(3)] \
            + [tile(gx, n, T) for n in range(FIRST, B - 1)] + [res[:, :]]
        c_out = x1

        P0 = [psum(f"p0_{n}") for n in range(3)]
        P1 = [psum(f"p1_{n}") for n in range(5)]

        names = """loaded folded setup_ps setup_ev setup_done
            x_loaded st0_ready mv0_ready ln0_steps r0_ready vr_steps q0_ready rr_ready xn_ready xh_ready
            xnT_ps xhT_ps xnT_ready xhT_ready logit_ps top1_steps ohT_ready delta_ps sp0_steps delta_ready decay0_ready
            xi0_ps xi1_ps xi0_ready xi1_ready b0_ps b1_ps bx0_ready bx1_ready h0_ready h1_ready
            c0_ps c1_ps ch0_ready ch1_ready yd0_ready yd1_ready z0_ps z1_ps th0_ready th1_ready
            sz0_ready sz1_ready y0_ready y1_ready u0_ps u1_ps g0_ready g1_ready out0_ps x1_ready
            st1_ready mv1_ready ln1_ready r1_ready xn1_ready x1T_ps x1T_ready vdw_ps vdw_ready hx_stored
            lam_steps lam_ready dt_in dt_act dt_steps g_ready gT_ps cgC_ready cgT_ps cgt_ready cgc_ps
            lev_diff lev_neg e4_ready alpha_steps beta_ready vp_ready r_ps r_copied m_ps m_copied
            gx_ps gx_copied cgrow_ready diff_ready diff_min decay_ready nodes_ready nodesT_ready self_ready
            s_ps lam_ps dlam_ready w_ready vbd_ready y1_ps ym_ready y2_ps lev_ps lev_ready levsum_ready
            yt_ready ytT_ps ytT_ready wo_ps ob_ready st2_ready mv2_ready ln2_ready r2_ready n_ready
            res_init skip_ready ng_ready res_ready res_stored f_ps i_ps g_ps tf_ready ti_ready tg_ready fc_ready ig_ready c_ready
            cp_ps cp_ready end_loaded0 end_loaded1 end_sum end_tanh end_add end_stored""".split()
        R = {n: sem(n) for n in names}

        def later(i, n=0):
            return not (isinstance(i, int) and i == 0 and n == 0)

        def view(ap, spec, **sizes):
            return ap.rearrange(spec, **sizes)

        def spread(ap, shape):
            return ap.broadcast_to(shape)

        def head_bank(h):
            return P1[(2 + h) % 5] if h < 4 else P1[(3, 4, 0)[(h - 4) % 3]]

        block = ctx.enter_context(nc.Block())

        def schedule(eng, stages, before, after):
            before()
            stages(None, 0)
            stages(0, 1)
            with eng.Fori(1, B - 1) as i:
                stages(i, i + 1)
            stages(B - 1, None)
            after()

        @block.sync
        def _(sp):
            def before():
                sp.dma_start(W[:, :], weights[:, 0:kept]).then_inc(R["loaded"], 16)
                sp.dma_start(gx[:, 0:wwidth - kept], weights[:, kept:wwidth]).then_inc(R["loaded"], 16)
                sp.dma_start(K[:, :], consts).then_inc(R["loaded"], 16)

            def load_x(j):
                if later(j):
                    sp.wait_ge(R["x1_ready"], j)
                src = x[j:j + 1] if isinstance(j, int) else x[bass.ds(j, 1)]
                sp.dma_start(view(xin[:, :], "p (a k d) -> p a k d", a=1, d=D),
                             view(src, "a (k p) d -> p a k d", p=128)).then_inc(R["x_loaded"], 16)

            def row(dram, b):
                return view(dram[b:b + 1] if isinstance(b, int) else dram[bass.ds(b, 1)], "a p n -> p (a n)")

            def store_hx(i):
                sp.wait_ge(R["vdw_ready"], 4 * i + 4)
                sp.dma_start(view(row(hx_dram, i), "p (k d) -> p k d", d=D),
                             view(vdw[:, :], "p (k c) -> p k c", k=TILES)[:, :, 304:432]).then_inc(R["hx_stored"], 16)

            def store_res(i):
                sp.wait_ge(R["res_ready"], i + 1)
                sp.dma_start(row(res_dram, i), res[:, :]).then_inc(R["res_stored"], 16)

            def stages(i, j):
                if j is not None:
                    load_x(j)
                if i is not None:
                    if later(i):
                        store_res(i - 1)
                    store_hx(i)

            def after():
                def load(b):
                    half = R[f"end_loaded{b // FIRST}"]
                    sp.dma_start(end_hx[b], row(hx_dram, b)).then_inc(half, 16)
                    if b < B - 1:
                        sp.dma_start(end_res[b], row(res_dram, b)).then_inc(half, 16)

                def store(b):
                    sp.wait_ge(R["end_add"], b + 1)
                    sp.dma_start(view(out[b], "(k p) d -> p k d", p=128),
                                 view(end_hx[b], "p (k d) -> p k d", d=D)).then_inc(R["end_stored"], 16)

                sp.wait_ge(R["res_stored"], 16 * (B - 1))
                sp.wait_ge(R["hx_stored"], 16 * B)
                sp.wait_ge(R["x1_ready"], B)
                sp.wait_ge(R["u1_ps"], B)
                for b in range(5):
                    load(b)
                sp.wait_ge(R["gx_ps"], 16 * B)
                for b in range(5, FIRST):
                    load(b)
                for b in range(FIRST):
                    store(b)
                sp.wait_ge(R["s_ps"], 4 * B)
                for b in range(FIRST, B):
                    load(b)
                for b in range(FIRST, B):
                    store(b)
                sp.wait_ge(R["end_stored"], 16 * B)
            schedule(sp, stages, before, after)

        @block.tensor
        def _(pe):
            def before():
                pe.wait_ge(R["loaded"], 48)
                for n, half in enumerate(("B", "C")):
                    rows = slice(64 * n, 64 * n + 64)
                    for q in range(2):
                        mm = pe.matmul(P0[n][:, 256 * q:256 * q + 256],
                                       w("WxpT", 128 * q, 128 * q + 128)[rows, :], w("WBC")[rows, :],
                                       start=True, stop=True)
                mm.then_inc(R["setup_ps"], 1)
                for e in range(E):
                    mm = pe.matmul(P1[0][32 * (e % 4):32 * (e % 4) + 32, e // 4:e // 4 + 1],
                                   w("W1", HID * e, HID * e + HID), w("lnb", e, e + 1), start=True, stop=True)
                mm.then_inc(R["setup_ps"], 1)
                for q in range(2):
                    mm = pe.matmul(P1[1][:, 0:128], w("WinT", 128 * q, 128 * q + 128),
                                   spread(w("wdelta", q, q + 1), [128, 128]), start=(q == 0), stop=(q == 1))
                mm.then_inc(R["setup_ps"], 1)
                pe.wait_ge(R["setup_ev"], 2)
                for n in range(2):
                    for q in range(2):
                        mm = pe.matmul(P1[2][:, 256 * n:256 * n + 256], w("WinT", 128 * q, 128 * q + 128),
                                       tile(xi, n, 512)[:, 256 * q:256 * q + 256], start=(q == 0), stop=(q == 1))
                mm.then_inc(R["setup_ps"], 1)
                for g in range(4):
                    for n, (lhs, rhs) in enumerate(((WQ, WK), (WK, WQ))):
                        bank = (P1[3], P1[4])[n] if g % 2 == 0 else (P0[2], P0[1])[n]
                        if g >= 2:
                            pe.wait_ge(R["setup_ev"], 6 + 2 * (g - 2) + n + 1)
                        for a in range(4):
                            h = 4 * g + a
                            rows, cols = slice(0, HS), slice(D * h, D * h + D)
                            mm = pe.matmul(bank[:, 128 * a:128 * a + 128], lhs[rows, cols], rhs[rows, cols],
                                           start=True, stop=True)
                        mm.then_inc(R["setup_ps"], 1)
                pe.wait_ge(R["setup_done"], 3)

            def turn_x(j):
                if not isinstance(j, int):
                    pe.wait_ge(R["tf_ready"], j - 1)
                elif j == 1:
                    pe.wait_ge(R["g0_ready"], 1)
                pe.wait_ge(R["xn_ready"], j + 1)
                for n in range(TILES):
                    mm = pe.transpose(tile(P0[0], n), tile(xn, n), ident)
                mm.then_inc(R["xnT_ps"], 1)
                if not isinstance(j, int):
                    pe.wait_ge(R["ti_ready"], j - 1)
                elif j == 1:
                    pe.wait_ge(R["g1_ready"], 1)
                pe.wait_ge(R["xh_ready"], j + 1)
                for n in range(TILES):
                    mm = pe.transpose(tile(P0[1], n), tile(xh, n), ident)
                mm.then_inc(R["xhT_ps"], 1)

            def logits(j):
                if not isinstance(j, int):
                    pe.wait_ge(R["tg_ready"], j - 1)
                elif j == 1:
                    pe.wait_ge(R["x1_ready"], 1)
                pe.wait_ge(R["xnT_ready"], j + 1)
                pe.matmul(P0[2][0:32, :], w("WgT"), xnT[:, :], start=True, stop=True).then_inc(R["logit_ps"], 1)
                pe.matmul(P0[0][:, :], Mdelta[:, :], xnT[:, :], start=True, stop=True).then_inc(R["delta_ps"], 1)

            def project(j, bank, free, value, lhs, done):
                pe.wait_ge(R[free], value)
                pe.matmul(P0[bank][:, :], lhs, xnT[:, :], start=True, stop=True).then_inc(R[done], 1)

            def scan_x(j):
                project(j, 1, "xhT_ready", j + 1, w("Win", 0, 128), "xi0_ps")
                project(j, 2, "top1_steps", 7 * j + 1, w("Win", 128, 256), "xi1_ps")

            def scan_b(j):
                project(j, 0, "delta_ready", j + 1, MB[:, 0:128], "b0_ps")
                project(j, 1, "xi0_ready", j + 1, MB[:, 128:256], "b1_ps")

            def scan_c(j):
                project(j, 2, "xi1_ready", j + 1, MC[:, 0:128], "c0_ps")
                project(j, 0, "bx0_ready", j + 1, MC[:, 128:256], "c1_ps")

            def gate_z(j, q):
                if q == 0:
                    project(j, 1, "bx1_ready", j + 1, w("Win", 256, 384), "z0_ps")
                else:
                    project(j, 2, "ch0_ready", j + 1, w("Win", 384, 512), "z1_ps")

            def gate_u(j, q):
                pe.wait_ge(R["top1_steps"], 7 * j + 7)
                if q == 0:
                    pe.wait_ge(R["ch1_ready"], j + 1)
                else:
                    pe.wait_ge(R["sz0_ready"], j + 1)
                pe.matmul(P0[q][:, :], expert_b[0:8, 128 * q:128 * q + 128], mask_b[0:8, :],
                          start=True, stop=False)
                pe.matmul(P0[q][:, :], w("W1", 128 * q, 128 * q + 128), xhT[:, :],
                          start=False, stop=True).then_inc(R[f"u{q}_ps"], 1)

            def out0(j):
                pe.wait_ge(R["sz1_ready"], j + 1)
                for name in ("y0_ready", "y1_ready", "g0_ready", "g1_ready"):
                    pe.wait_ge(R[name], j + 1)
                for n in range(TILES):
                    o, t = tile(P0[2], n), slice(128 * n, 128 * n + 128)
                    pe.matmul(o, y[:, t], w("Wout0", 0, D), start=True, stop=False)
                    pe.matmul(o, y[:, 128 * n + T:128 * n + T + 128], w("Wout0", D), start=False, stop=False)
                    pe.matmul(o, gelu[:, t], w("W2", 0, D), start=False, stop=False)
                    pe.matmul(o, gelu[:, 128 * n + T:128 * n + T + 128], w("W2", D), start=False, stop=False)
                    mm = pe.matmul(o, oh_b[0:24, t], b2_b[0:24, :], start=False, stop=True)
                mm.then_inc(R["out0_ps"], 1)

            def turn_x1(j):
                if later(j):
                    pe.wait_ge(R["lev_ready"], 4 * j)
                pe.wait_ge(R["xn1_ready"], j + 1)
                for n in range(TILES):
                    mm = pe.transpose(tile(P1[0], n), tile(xn1, n), ident)
                mm.then_inc(R["x1T_ps"], 1)

            def values(j):
                pe.wait_ge(R["x1T_ready"], j + 1)
                for n, free in enumerate(("dlam_ready", "ym_ready", "yt_ready", "x1T_ready")):
                    if n < 3 and later(j):
                        pe.wait_ge(R[free], 4 * j)
                    pe.matmul(P1[(2 + n) % 5][:, 0:VDW], tile(x1T, n), w("Wvdw"), start=True, stop=True)\
                        .then_inc(R["vdw_ps"], 1)

            def heads(i, a, b):
                for h in range(a, b):
                    if h < 4:
                        pe.wait_ge(R["vdw_ready"], 4 * i + h + 1)
                    else:
                        pe.wait_ge(R["gx_copied"], 16 * i + h - 2)
                    pe.matmul(head_bank(h)[:, :], tile(G, h), x1T[:, :], start=True, stop=True).then_inc(R["gx_ps"], 1)

            def gates_to_rows(i):
                if later(i):
                    pe.wait_ge(R["ob_ready"], i)
                pe.wait_ge(R["g_ready"], i + 1)
                for n in range(TILES):
                    mm = pe.transpose(P1[1][0:16, 128 * n:128 * n + 128],
                                      dts[:, 576 + 16 * n:576 + 16 * n + 16], ident)
                mm.then_inc(R["gT_ps"], 1)

            def sums_to_tokens(i):
                pe.wait_ge(R["loaded"], 48)
                pe.wait_ge(R["cgC_ready"], i + 1)
                for n in range(TILES):
                    mm = pe.transpose(P1[2][:, 16 * n:16 * n + 16], cgC[:, 128 * n:128 * n + 128], k("ident", 0, 16, 16))
                mm.then_inc(R["cgT_ps"], 1)

            def left_ends(i):
                pe.wait_ge(R["cgt_ready"], i + 1)
                pe.matmul(P1[2][:, 64:128], k("sel6"), cgt[:, :], start=True, stop=True)
                pe.matmul(P1[2][:, 128:192], k("sel7"), cgt[:, :], start=True, stop=True)
                pe.matmul(P1[2][:, 192:224], k("sel_last"),
                          view(cgt[:, :], "p (a b h) -> p a b h", a=2, b=2)[:, :, 0, :], start=True, stop=True)
                pe.matmul(P1[2][:, 224:240], k("sel_last"), cgt[:, 16:32], start=True, stop=True)\
                    .then_inc(R["cgc_ps"], 1)

            def left_halves(i):
                pe.wait_ge(R["vp_ready"], i + 1)
                for n in range(TILES):
                    if n < 3:
                        pe.wait_ge(R["gx_copied"], 16 * i + 14 + n)
                    else:
                        pe.wait_ge(R["r_copied"], 4 * i + 1)
                    bank = P1[(3, 4, 0, 3)[n]]
                    if n == 1:
                        pe.matmul(bank[:, 384:512], tile(xn1, 0), vp[:, 512:640], start=True, stop=False)
                        pe.matmul(bank[:, 384:512], tile(xn1, 1), vp[:, 1024:1152], start=False, stop=True)
                    at = (0, 640, 1152, 1664)[n]
                    cols = 512 if n in (0, 2) else 384
                    pe.matmul(bank[:, 0:cols], tile(xn1, n), vp[:, at:at + cols], start=True, stop=True)\
                        .then_inc(R["r_ps"], 1)

            def node_matrices(i):
                pe.wait_ge(R["r_copied"], 4 * i + 4)
                for g in range(4):
                    if g == 3:
                        pe.wait_ge(R["m_copied"], 4 * i + 1)
                    bank = P1[(4, 0, 3, 4)[g]]
                    for a in range(4):
                        h = 4 * g + a
                        mm = pe.matmul(bank[:, 120 * a:120 * a + 120], tile(GT, h),
                                       view(rs[:, 0:1920], "p (n c) -> p n c", c=128)[:, :, HD * h:HD * h + HD],
                                       start=True, stop=True)
                    mm.then_inc(R["m_ps"], 1)

            def pair_scores(i, n):
                if n == 0:
                    pe.wait_ge(R["cgC_ready"], i + 1)
                    pe.wait_ge(R["gx_copied"], 16 * i + 16)
                else:
                    pe.wait_ge(R["w_ready"], 4 * i + n)
                for c in range(4):
                    mm = pe.matmul(P1[1][32 * c:32 * c + 32, :], x1T[:, 128 * n + 32 * c:128 * n + 32 * c + 32],
                                   view(gx[:, :], "p (h t) -> p h t", h=H)[:, :, 128 * n + 32 * c:128 * n + 32 * c + 32],
                                   start=True, stop=True)
                mm.then_inc(R["s_ps"], 1)

            def pair_levels(i, n):
                if n == 0:
                    pe.wait_ge(R["lev_diff"], i + 1)
                    pe.wait_ge(R["nodesT_ready"], i + 1)
                    pe.wait_ge(R["self_ready"], i + 1)
                else:
                    pe.wait_ge(R["dlam_ready"], 4 * i + n)
                pe.matmul(P1[2][:, :], k("left"), tile(nodesT, n, 512), start=True, stop=False)
                pe.matmul(P1[2][:, :], ident, tile(self_lam, n, 512), start=False, stop=True).then_inc(R["lam_ps"], 1)

            def levels(i, n):
                pe.wait_ge(R["m_copied"], 4 * i + 4)
                if n > 0:
                    pe.wait_ge(R["lev_ready"], 4 * i + n)
                node = lambda a: tile(ms, a)
                bank = P1[0]
                for c in range(2):
                    pe.matmul(bank[64 * c:64 * c + 64, 0:128], x1T[:, 128 * n + 64 * c:128 * n + 64 * c + 64],
                              node(4 * n + c), start=True, stop=True)
                full = [4 * n + 2] + [[], [3], [7], [11, 7]][n]
                for a, m in enumerate(full):
                    mm = pe.matmul(bank[:, 128 * (a + 1):128 * (a + 2)], tile(x1T, n), node(m), start=True, stop=True)
                mm.then_inc(R["lev_ps"], 1)

            def chunk_values(i, n):
                if n > 0:
                    pe.wait_ge(R["ym_ready"], 4 * i + n)
                pe.wait_ge(R["m_copied"], 4 * i + 4)
                pe.wait_ge(R["w_ready"], 4 * i + n + 1)
                pe.wait_ge(R["vbd_ready"], 4 * i + n + 1)
                for g in range(4):
                    at = 512 * n + 128 * g
                    mm = pe.matmul(tile(P1[3], g), pair[:, at:at + 128], vbd[:, at:at + 128], start=True, stop=True)
                mm.then_inc(R["y1_ps"], 1)

            def chunk_sums(i, n):
                if n > 0:
                    pe.wait_ge(R["yt_ready"], 4 * i + n)
                pe.wait_ge(R["ym_ready"], 4 * i + n + 1)
                for c in range(4):
                    mm = pe.matmul(P1[4][32 * c:32 * c + 32, 0:128], k("sum_heads"),
                                   view(tile(ym, n % 2, 512), "p (g c v) -> p g c v", g=4, c=4)[:, :, c, :],
                                   start=True, stop=True)
                mm.then_inc(R["y2_ps"], 1)

            def turn_out(i):
                pe.wait_ge(R["w_ready"], 4 * i + 4)
                pe.wait_ge(R["yt_ready"], 4 * i + 4)
                for n in range(TILES):
                    mm = pe.transpose(tile(P1[1], n), tile(yt, n), ident)
                mm.then_inc(R["ytT_ps"], 1)

            def project_out(i):
                pe.wait_ge(R["ytT_ready"], i + 1)
                for n in range(TILES):
                    mm = pe.matmul(tile(P1[1], n), tile(ytT, n), w("WoutT"), start=True, stop=True)
                mm.then_inc(R["wo_ps"], 1)

            def recurrence(i, j, n):
                if n == 0:
                    if later(i):
                        pe.wait_ge(R["c_ready"], i)
                free, done = ("g0_ready", "g1_ready", "x1_ready")[n], ("f_ps", "i_ps", "g_ps")[n]
                pe.wait_ge(R[free], B if j is None else j + 1)
                pe.matmul(P0[n][:, :], w("gates_x", 128 * n, 128 * n + 128), x1T[:, :], start=True, stop=False)
                pe.matmul(P0[n][:, :], w("gates_c", 128 * n, 128 * n + 128), cell[:, :],
                          start=False, stop=True).then_inc(R[done], 1)

            def stages(i, j):
                if j is None:
                    for n in range(3):
                        recurrence(i, j, n)
                if i is not None:
                    heads(i, 0, 4)
                if j is not None:
                    turn_x(j)
                if i is not None:
                    gates_to_rows(i)
                    heads(i, 4, 6)
                    sums_to_tokens(i)
                    heads(i, 6, 8)
                if j is not None:
                    logits(j)
                if i is not None:
                    left_ends(i)
                    heads(i, 8, 12)
                if j is not None:
                    scan_x(j)
                else:
                    cell_out()
                if i is not None:
                    heads(i, 12, 14)
                if j is not None:
                    scan_b(j)
                if i is not None:
                    heads(i, 14, H)
                if j is not None:
                    scan_c(j)
                if i is not None:
                    pair_scores(i, 0)
                    left_halves(i)
                    pair_levels(i, 0)
                    node_matrices(i)
                    pair_scores(i, 1)
                    levels(i, 0)
                    pair_levels(i, 1)
                    chunk_values(i, 0)
                if j is not None:
                    gate_z(j, 0)
                if i is not None:
                    levels(i, 1)
                    chunk_sums(i, 0)
                if j is not None:
                    gate_z(j, 1)
                if i is not None:
                    pair_scores(i, 2)
                    pair_levels(i, 2)
                    chunk_values(i, 1)
                if j is not None:
                    gate_u(j, 0)
                if i is not None:
                    chunk_sums(i, 1)
                    levels(i, 2)
                if j is not None:
                    gate_u(j, 1)
                if i is not None:
                    pair_scores(i, 3)
                    pair_levels(i, 3)
                    chunk_values(i, 2)
                    levels(i, 3)
                    chunk_sums(i, 2)
                    chunk_values(i, 3)
                if j is not None:
                    out0(j)
                    if i is not None:
                        for n in range(3):
                            recurrence(i, j, n)
                    turn_x1(j)
                if i is not None:
                    chunk_sums(i, 3)
                    turn_out(i)
                if j is not None:
                    values(j)
                if i is not None:
                    project_out(i)

            def cell_out():
                pe.wait_ge(R["c_ready"], B)
                pe.wait_ge(R["tf_ready"], B)
                for n in range(TILES):
                    mm = pe.matmul(tile(P0[0], n), tile(cell, n), w("uo"), start=True, stop=True)
                mm.then_inc(R["cp_ps"], 1)
            schedule(pe, stages, before, lambda: None)

        @block.scalar
        def _(act):
            def logs():
                act.preload_act_table_set("natural_log_exp_and_others")

            def gelus():
                act.preload_act_table_set("gelu_and_others")

            def before():
                logs()
                act.wait_ge(R["loaded"], 48)
                act.activation(neg_a0[:, :], w("A0"), ACT.Exp).then_inc(R["setup_ev"], 1)
                act.activation(neg_a1[:, :], w("A1"), ACT.Exp).then_inc(R["setup_done"], 1)
                act.wait_ge(R["setup_ps"], 1)
                for n in range(2):
                    cp = act.activation(tile(xi, n, 512), P0[n][:, :], ACT.Copy)
                cp.then_inc(R["setup_ev"], 1)
                act.wait_ge(R["setup_ps"], 3)
                act.activation(Mdelta[:, :], P1[1][:, 0:128], ACT.Copy).then_inc(R["setup_ev"], 1)
                act.wait_ge(R["setup_ps"], 4)
                act.activation(MB[:, :], P1[2][:, 0:256], ACT.Copy).then_inc(R["setup_ev"], 1)
                act.activation(MC[:, :], P1[2][:, 256:512], ACT.Copy).then_inc(R["setup_ev"], 1)
                act.mul(w("uo"), w("uo"), 0.5).then_inc(R["setup_ev"], 1)
                for g in range(4):
                    for n, dst in enumerate((G, GT)):
                        bank = (P1[3], P1[4])[n] if g % 2 == 0 else (P0[2], P0[1])[n]
                        act.wait_ge(R["setup_ps"], 5 + 2 * g + n)
                        act.activation(tile(dst, g, 512), bank[:, :], ACT.Copy, scale=HS ** -0.5)\
                            .then_inc(R["setup_ev"], 1)
                act.wait_ge(R["setup_ev"], 14)
                act.mul(neg_a0[:, :], neg_a0[:, :], -1.0).then_inc(R["setup_done"], 1)

            def rstd0(j):
                act.wait_ge(R["mv0_ready"], j + 1)
                act.activation(sm0[:, 0:4], view(mv0[:, :], "p (k s) -> p k s", s=2)[:, :, 1], ACT.Ln, bias=EPS)\
                    .then_inc(R["ln0_steps"], 1)
                act.wait_ge(R["ln0_steps"], 2 * j + 1)
                act.activation(sm0[:, 4:8], sm0[:, 0:4], ACT.Exp, scale=-0.5).then_inc(R["r0_ready"], 1)
                act.wait_ge(R["vr_steps"], 2 * j + 2)
                act.activation(sm0[:, 16:20], sm0[:, 12:16], ACT.Ln, bias=EPS).then_inc(R["ln0_steps"], 1)
                act.wait_ge(R["ln0_steps"], 2 * j + 2)
                act.activation(sm0[:, 20:24], sm0[:, 16:20], ACT.Exp, scale=-0.5).then_inc(R["q0_ready"], 1)

            def turned(j):
                if later(j):
                    act.wait_ge(R["z1_ps"], j)
                act.wait_ge(R["xnT_ps"], j + 1)
                act.activation(xnT[:, :], P0[0][:, :], ACT.Copy).then_inc(R["xnT_ready"], 1)
                if later(j):
                    act.wait_ge(R["u1_ps"], j)
                act.wait_ge(R["xhT_ps"], j + 1)
                act.activation(xhT[:, :], P0[1][:, :], ACT.Copy).then_inc(R["xhT_ready"], 1)

            def delta(j):
                act.wait_ge(R["delta_ps"], j + 1)
                if not isinstance(j, int):
                    act.wait_ge(R["fc_ready"], j - 1)
                act.activation(sp0[:, :], P0[0][:, :], ACT.Abs).then_inc(R["sp0_steps"], 1)
                act.wait_ge(R["sp0_steps"], 3 * j + 1)
                act.activation(sp0[:, :], sp0[:, :], ACT.Exp, scale=-1.0).then_inc(R["sp0_steps"], 1)
                act.wait_ge(R["sp0_steps"], 3 * j + 2)
                act.activation(sp0[:, :], sp0[:, :], ACT.Ln, bias=1.0).then_inc(R["sp0_steps"], 1)

            def decay(j):
                act.wait_ge(R["delta_ready"], j + 1)
                act.activation(decay0[:, :], decay0[:, :], ACT.Exp, scale=neg_a0[:, 0:1]).then_inc(R["decay0_ready"], 1)

            def xi_copy(j):
                if later(j):
                    act.wait_ge(R["yd1_ready"], j)
                for q, bank in ((0, 1), (1, 2)):
                    act.wait_ge(R[f"xi{q}_ps"], j + 1)
                    act.activation(tile(xi, q, T), P0[bank][:, :], ACT.Copy).then_inc(R[f"xi{q}_ready"], 1)

            def gates0(j):
                for q, bank in ((0, 1), (1, 2)):
                    if later(j):
                        act.wait_ge(R[f"y{q}_ready"], j)
                    act.wait_ge(R[f"z{q}_ps"], j + 1)
                    act.activation(tile(th, q, T), P0[bank][:, :], ACT.Tanh, scale=0.5).then_inc(R[f"th{q}_ready"], 1)
                if later(j):
                    act.wait_ge(R["out0_ps"], j)
                for q in range(2):
                    act.wait_ge(R[f"u{q}_ps"], j + 1)
                    act.activation(tile(gelu, q, T), P0[q][:, :], ACT.Gelu, bias=bias_u[:, q:q + 1])\
                        .then_inc(R[f"g{q}_ready"], 1)

            def rstd(i, mv, sm, ready, ln, done):
                act.wait_ge(R[ready], i + 1)
                act.activation(sm[:, 0:4], view(mv, "p (k s) -> p k s", s=2)[:, :, 1], ACT.Ln, bias=EPS)\
                    .then_inc(R[ln], 1)
                act.wait_ge(R[ln], i + 1)
                act.activation(sm[:, 4:8], sm[:, 0:4], ACT.Exp, scale=-0.5).then_inc(R[done], 1)

            def rstd2(i):
                rstd(i, mv2[:, :], sm2, "mv2_ready", "ln2_ready", "r2_ready")

            def turned1(i):
                if later(i):
                    act.wait_ge(R["g_ps"], i)
                    act.wait_ge(R["lev_ps"], 4 * i)
                act.wait_ge(R["x1T_ps"], i + 1)
                act.activation(x1T[:, :], P1[0][:, :], ACT.Copy).then_inc(R["x1T_ready"], 1)

            def values(i):
                if later(i):
                    act.wait_ge(R["vbd_ready"], 4 * i)
                if later(i):
                    act.wait_ge(R["vp_ready"], i)
                if later(i):
                    act.wait_ge(R["hx_stored"], 16 * i)
                for n in range(TILES):
                    act.wait_ge(R["vdw_ps"], 4 * i + n + 1)
                    act.activation(tile(vdw, n, VDW), P1[(2 + n) % 5][:, 0:VDW], ACT.Copy)\
                        .then_inc(R["vdw_ready"], 1)

            def heads(i, a, b):
                for h in range(a, b):
                    if h == 0:
                        if later(i):
                            act.wait_ge(R["s_ps"], 4 * i)
                    act.wait_ge(R["gx_ps"], 16 * i + h + 1)
                    act.activation(tile(gx, h, T), head_bank(h)[:, :], ACT.Copy).then_inc(R["gx_copied"], 1)

            def gate_logs(i):
                act.wait_ge(R["dt_in"], i + 1)
                act.activation(dts[:, 64:128], dts[:, 0:64], ACT.Abs).then_inc(R["dt_act"], 1)
                act.wait_ge(R["dt_act"], 3 * i + 1)
                act.activation(dts[:, 128:192], dts[:, 64:128], ACT.Exp, scale=-1.0).then_inc(R["dt_act"], 1)
                act.wait_ge(R["dt_act"], 3 * i + 2)
                act.activation(dts[:, 192:256], dts[:, 128:192], ACT.Ln, bias=1.0).then_inc(R["dt_act"], 1)

            def lam_logs(i):
                if later(i):
                    act.wait_ge(R["nodes_ready"], i)
                if later(i):
                    act.wait_ge(R["self_ready"], i)
                if later(i):
                    act.wait_ge(R["alpha_steps"], 2 * i)
                act.wait_ge(R["vdw_ready"], 4 * i + 4)
                act.activation(view(lam[:, :], "p (k c) -> p k c", k=TILES),
                               view(vdw[:, :], "p (k c) -> p k c", k=TILES)[:, :, 128:288], ACT.Abs)\
                    .then_inc(R["lam_steps"], 1)
                act.wait_ge(R["lam_steps"], 3 * i + 1)
                act.activation(lam[:, :], lam[:, :], ACT.Exp, scale=-1.0).then_inc(R["lam_steps"], 1)
                act.wait_ge(R["lam_steps"], 3 * i + 2)
                act.activation(lam[:, :], lam[:, :], ACT.Ln, bias=1.0).then_inc(R["lam_steps"], 1)

            def level_decay(i):
                act.wait_ge(R["lev_neg"], i + 1)
                act.activation(e4[:, :], lev[:, :], ACT.Exp).then_inc(R["e4_ready"], 1)

            def pair_decay(i):
                act.wait_ge(R["diff_min"], i + 1)
                act.activation(pair[:, :], pair[:, :], ACT.Exp).then_inc(R["decay_ready"], 1)

            def left_halves(i):
                if later(i):
                    act.wait_ge(R["m_ps"], 4 * i)
                for n in range(TILES):
                    cols = 384 if n == 3 else 512
                    act.wait_ge(R["r_ps"], 4 * i + n + 1)
                    act.activation(rs[:, 512 * n:512 * n + cols], P1[(3, 4, 0, 3)[n]][:, 0:cols], ACT.Copy)\
                        .then_inc(R["r_copied"], 1)

            def node_matrices(i):
                if later(i):
                    act.wait_ge(R["lev_ps"], 4 * i)
                for g in range(4):
                    act.wait_ge(R["m_ps"], 4 * i + g + 1)
                    src = view(P1[(4, 0, 3, 4)[g]][:, 0:480], "p (a n e) -> p a n e", a=4, e=HD)
                    dst = view(ms[:, 0:1920], "p (n g a e) -> p g a n e", g=4, a=4, e=HD)[:, g]
                    for a in range(4):
                        cp = act.activation(dst[:, a], src[:, a], ACT.Copy)
                    cp.then_inc(R["m_copied"], 1)

            def project_out(i):
                act.wait_ge(R["ytT_ps"], i + 1)
                act.activation(ytT[:, :], P1[1][:, :], ACT.Copy).then_inc(R["ytT_ready"], 1)

            def recurrence(i, n):
                ps, done = (("f_ps", "tf_ready"), ("i_ps", "ti_ready"), ("g_ps", "tg_ready"))[n]
                act.wait_ge(R[ps], i + 1)
                act.activation((tf, ti, tg)[n][:, :], P0[n][:, :], ACT.Tanh, bias=w("gate_b", n, n + 1),
                               scale=(0.5, 0.5, 1.0)[n]).then_inc(R[done], 1)

            def end_tanh(b):
                act.wait_ge(R["end_sum"], b + 1)
                act.activation(end_hx[b], end_hx[b], ACT.Tanh).then_inc(R["end_tanh"], 1)

            def stages(i, j):
                if j is not None:
                    rstd0(j)
                if i is not None:
                    values(i)
                    if j is None:
                        gate_logs(i)
                    heads(i, 0, 2)
                    if j is not None:
                        gate_logs(i)
                    heads(i, 2, 4)
                if j is not None:
                    turned(j)
                if i is not None:
                    lam_logs(i)
                if j is None:
                    gelus()
                    for n in range(3):
                        recurrence(i, n)
                    logs()
                if i is not None:
                    heads(i, 4, 6)
                    if later(i):
                        rstd2(i - 1)
                    heads(i, 6, 8)
                if j is not None:
                    delta(j)
                if i is not None:
                    heads(i, 8, 10)
                    level_decay(i)
                    heads(i, 10, 12)
                if j is not None:
                    xi_copy(j)
                if i is not None:
                    heads(i, 12, 14)
                if j is not None:
                    decay(j)
                if i is not None:
                    heads(i, 14, H)
                    left_halves(i)
                    pair_decay(i)
                    node_matrices(i)
                gelus()
                if j is not None:
                    gates0(j)
                else:
                    for b in range(FIRST):
                        end_tanh(b)
                logs()
                if j is not None:
                    rstd(j, mv1[:, :], sm1, "mv1_ready", "ln1_ready", "r1_ready")
                    if i is not None:
                        gelus()
                        for n in range(3):
                            recurrence(i, n)
                    turned1(j)
                    if i is not None:
                        logs()
                if i is not None:
                    project_out(i)

            def after():
                rstd2(B - 1)
                gelus()
                for b in range(FIRST, B):
                    end_tanh(b)
            schedule(act, stages, before, after)

        @block.vector
        def _(dve):
            def before():
                dve.wait_ge(R["loaded"], 48)
                b2 = w("b2", rows=32)
                steps = [0]

                def step(ins):
                    steps[0] += 1
                    ins.then_inc(R["folded"], 1)
                    dve.wait_ge(R["folded"], steps[0])

                part, rest = am[:, 0:128], am[:, 128:256]
                step(dve.memset(am[:, 256:384], 0.0))
                for n in range(3):
                    step(dve.tensor_copy(b2_b[:, :], b2 if n == 0 else rest))
                    step(dve.tensor_copy(part, b2_b[:, :]))
                    step(dve.tensor_tensor(rest, b2 if n == 0 else rest, part, ALU.subtract))
                    step(dve.scalar_tensor_tensor(am[:, 256:384], part, k("b2_part", n, n + 1, 32), am[:, 256:384],
                                                  ALU.mult, ALU.add))
                step(dve.tensor_copy(b2_b[:, :], am[:, 256:384]))
                step(dve.tensor_copy(expert_b[:, :], k("expert", rows=32)))
                step(dve.memset(oh[:, :], 0.0))
                step(dve.memset(ones[:, :], 1.0))
                dve.wait_ge(R["setup_ps"], 2)
                step(dve.tensor_tensor(bias_u[:, :], P1[0][:, 0:2], w("b1"), ALU.add))
                w1 = view(w("W1"), "p (e h) -> p e h", e=E)
                step(dve.tensor_tensor(w1, w1, spread(w("lns").unsqueeze(2), [128, E, HID]), ALU.mult))
                dl = w("Wvdw", 128, 288)
                step(dve.tensor_tensor(dl, dl, w("Lp"), ALU.mult))
                step(dve.tensor_scalar(w("Wout0"), w("Wout0"), 0.5, None, ALU.mult))
                step(dve.tensor_scalar(w("gates_c"), w("gates_c"), 0.5, None, ALU.mult))
                step(dve.tensor_scalar(w("gate_b", 0, 2), w("gate_b", 0, 2), 0.5, None, ALU.mult))
                step(dve.tensor_scalar(cell[:, :], spread(w("c0"), [128, T]), 2.0, None, ALU.mult))
                dve.wait_ge(R["setup_done"], 1)
                step(dve.tensor_scalar(neg_a1[:, :], neg_a1[:, :], -1.0, None, ALU.mult))
                dve.sem_inc(R["setup_done"], 1)
                dve.wait_ge(R["setup_done"], 3)

            def stats(src, st, mv, st_ready, mv_ready, i):
                for n in range(TILES):
                    last = dve.bn_stats(st[:, 6 * n:6 * n + 6], tile(src, n))
                last.then_inc(R[st_ready], 1)
                dve.wait_ge(R["loaded"], 48)
                dve.wait_ge(R[st_ready], i + 1)
                for n in range(TILES):
                    last = dve.bn_aggr(mv[:, 2 * n:2 * n + 2], st[:, 6 * n:6 * n + 6])
                last.then_inc(R[mv_ready], 1)

            def normalise(dst, src, mv, r):
                for n in range(TILES):
                    last = dve.tensor_scalar(tile(dst, n), tile(src, n), mv[:, 2 * n:2 * n + 1], r[:, n:n + 1],
                                             ALU.subtract, ALU.mult)
                return last

            def norm0(j):
                dve.wait_ge(R["x_loaded"], 16 * (j + 1))
                stats(xin, st0, mv0, "st0_ready", "mv0_ready", j)
                dve.wait_ge(R["r0_ready"], j + 1)
                var, r = view(mv0[:, :], "p (k s) -> p k s", s=2)[:, :, 1], sm0[:, 4:8]
                dve.tensor_tensor(sm0[:, 8:12], var, r, ALU.mult).then_inc(R["vr_steps"], 1)
                if later(j):
                    dve.wait_ge(R["xnT_ps"], j)
                dve.wait_ge(R["vr_steps"], 2 * j + 1)
                dve.tensor_tensor(sm0[:, 12:16], sm0[:, 8:12], r, ALU.mult).then_inc(R["vr_steps"], 1)
                normalise(xn, xin, mv0, r).then_inc(R["xn_ready"], 1)
                dve.wait_ge(R["q0_ready"], j + 1)
                dve.tensor_tensor(sm0[:, 24:28], sm0[:, 20:24], r, ALU.mult).then_inc(R["rr_ready"], 1)
                if later(j):
                    dve.wait_ge(R["xhT_ps"], j)
                dve.wait_ge(R["rr_ready"], j + 1)
                normalise(xh, xin, mv0, sm0[:, 24:28]).then_inc(R["xh_ready"], 1)

            def turn_logits(j):
                dve.wait_ge(R["logit_ps"], j + 1)
                dve.transpose(lgT[:, :], P0[2][0:32, :]).then_inc(R["top1_steps"], 1)

            def top1(j):
                lg = view(lgT[:, :], "p (c e) -> p c e", e=32)[:, :, 0:E]
                eq = view(am[:, 0:128], "p (c e) -> p c e", e=E)
                val = view(am[:, 128:256], "p (c e) -> p c e", e=E)
                mx, mx2 = am[:, 512:528], am[:, 528:544]
                dve.wait_ge(R["top1_steps"], 7 * j + 1)
                dve.tensor_reduce(mx, lg, AX.X, ALU.max).then_inc(R["top1_steps"], 1)
                dve.wait_ge(R["top1_steps"], 7 * j + 2)
                dve.tensor_tensor(eq, lg, spread(mx.unsqueeze(2), [32, 16, E]), ALU.is_ge).then_inc(R["top1_steps"], 1)
                dve.wait_ge(R["top1_steps"], 7 * j + 3)
                dve.tensor_tensor(val, eq, spread(k("rank", rows=32).unsqueeze(1), [32, 16, E]), ALU.mult)\
                    .then_inc(R["top1_steps"], 1)
                dve.wait_ge(R["top1_steps"], 7 * j + 4)
                dve.tensor_reduce(mx2, val, AX.X, ALU.max).then_inc(R["top1_steps"], 1)
                dve.wait_ge(R["top1_steps"], 7 * j + 5)
                rows = view(oh[:, :], "p (c r e) -> p c r e", c=16, e=E)
                for r in range(3):
                    last = dve.tensor_tensor(rows[:, :, r], val, spread(mx2.unsqueeze(2), [32, 16, E]), ALU.is_equal)
                last.then_inc(R["top1_steps"], 1)
                dve.wait_ge(R["top1_steps"], 7 * j + 6)
                dve.transpose(ohT[:, :], oh[:, :]).then_inc(R["ohT_ready"], 1)
                dve.wait_ge(R["ohT_ready"], j + 1)
                if later(j):
                    dve.wait_ge(R["out0_ps"], j)
                dve.tensor_copy(oh_b[:, :], ohT[:, :])
                dve.tensor_scalar(mask_b[:, :], ohT[:, :], 1.0, BIG, ALU.subtract, ALU.mult)\
                    .then_inc(R["top1_steps"], 1)

            def delta(j):
                dve.wait_ge(R["sp0_steps"], 3 * j + 3)
                if later(j):
                    dve.wait_ge(R["h1_ready"], j)
                dve.scalar_tensor_tensor(decay0[:, :], P0[0][:, :], 0.0, sp0[:, :], ALU.max, ALU.add)\
                    .then_inc(R["delta_ready"], 1)

            def scan_inputs(j):
                if later(j):
                    dve.wait_ge(R["out0_ps"], j)
                for q, bank in ((0, 0), (1, 1)):
                    dve.wait_ge(R[f"b{q}_ps"], j + 1)
                    dve.wait_ge(R[f"xi{q}_ready"], j + 1)
                    dve.tensor_tensor(tile(y, q, T), P0[bank][:, :], tile(xi, q, T), ALU.mult)\
                        .then_inc(R[f"bx{q}_ready"], 1)

            def scans(j):
                dve.wait_ge(R["decay0_ready"], j + 1)
                for q in range(2):
                    dve.wait_ge(R[f"bx{q}_ready"], j + 1)
                    dve.tensor_tensor_scan(tile(y, q, T), decay0[:, :], tile(y, q, T), 0.0, ALU.mult, ALU.add)\
                        .then_inc(R[f"h{q}_ready"], 1)
                for q, bank in ((0, 2), (1, 0)):
                    dve.wait_ge(R[f"c{q}_ps"], j + 1)
                    dve.wait_ge(R[f"h{q}_ready"], j + 1)
                    dve.tensor_tensor(tile(y, q, T), P0[bank][:, :], tile(y, q, T), ALU.mult)\
                        .then_inc(R[f"ch{q}_ready"], 1)
                for q in range(2):
                    dve.wait_ge(R[f"ch{q}_ready"], j + 1)
                    dve.scalar_tensor_tensor(tile(y, q, T), tile(xi, q, T), w("Dskip", q, q + 1), tile(y, q, T),
                                             ALU.mult, ALU.add).then_inc(R[f"yd{q}_ready"], 1)

            def gate0(j, q):
                dve.wait_ge(R[f"th{q}_ready"], j + 1)
                dve.scalar_tensor_tensor(tile(th, q, T), tile(th, q, T), 1.0, P0[1 + q][:, :], ALU.add, ALU.mult)\
                    .then_inc(R[f"sz{q}_ready"], 1)
                dve.wait_ge(R[f"sz{q}_ready"], j + 1)
                dve.wait_ge(R[f"yd{q}_ready"], j + 1)
                dve.tensor_tensor(tile(y, q, T), tile(y, q, T), tile(th, q, T), ALU.mult)\
                    .then_inc(R[f"y{q}_ready"], 1)

            def sum0(j):
                dve.wait_ge(R["out0_ps"], j + 1)
                if later(j):
                    dve.wait_ge(R["res_init"], j)
                dve.tensor_tensor(x1[:, :], P0[2][:, :], xin[:, :], ALU.add).then_inc(R["x1_ready"], 1)

            def norm1(i):
                dve.wait_ge(R["x1_ready"], i + 1)
                stats(x1, st1, mv1, "st1_ready", "mv1_ready", i)
                dve.wait_ge(R["r1_ready"], i + 1)
                if later(i):
                    dve.wait_ge(R["skip_ready"], i)
                    dve.wait_ge(R["r_ps"], 4 * i)
                normalise(xn1, x1, mv1, sm1[:, 4:8]).then_inc(R["xn1_ready"], 1)

            def gates1(i):
                c = lambda n: dts[:, 64 * n:64 * n + 64]
                heads = lambda ap: view(ap, "p (k h) -> p k h", k=TILES)
                dve.wait_ge(R["vdw_ready"], 4 * i + 4)
                dve.tensor_tensor(heads(c(0)), view(vdw[:, :], "p (k c) -> p k c", k=TILES)[:, :, 288:304],
                                  spread(w("dtb").unsqueeze(1), [128, TILES, H]), ALU.add).then_inc(R["dt_in"], 1)
                dve.wait_ge(R["dt_act"], 3 * i + 2)
                dve.tensor_scalar(c(4), c(2), 1.0, 1.0, ALU.add, ALU.subtract).then_inc(R["dt_steps"], 1)
                dve.wait_ge(R["dt_act"], 3 * i + 3)
                dve.wait_ge(R["dt_steps"], 6 * i + 1)
                dve.scalar_tensor_tensor(c(5), c(4), 0.0, c(4), ALU.is_equal, ALU.add).then_inc(R["dt_steps"], 1)
                dve.scalar_tensor_tensor(c(6), c(4), 0.0, c(3), ALU.is_equal, ALU.add)
                dve.wait_ge(R["dt_steps"], 6 * i + 2)
                dve.reciprocal(c(7), c(5)).then_inc(R["dt_steps"], 1)
                dve.wait_ge(R["dt_steps"], 6 * i + 3)
                dve.tensor_tensor(c(7), c(7), c(2), ALU.mult).then_inc(R["dt_steps"], 1)
                dve.wait_ge(R["dt_steps"], 6 * i + 4)
                dve.tensor_tensor(c(7), c(7), c(6), ALU.mult).then_inc(R["dt_steps"], 1)
                dve.wait_ge(R["dt_steps"], 6 * i + 5)
                dve.scalar_tensor_tensor(c(8), c(0), 0.0, c(7), ALU.max, ALU.add).then_inc(R["dt_steps"], 1)
                dve.wait_ge(R["dt_steps"], 6 * i + 6)
                dve.tensor_tensor(heads(c(9)), heads(c(8)), spread(neg_a1[:, :].unsqueeze(1), [128, TILES, H]), ALU.mult)\
                    .then_inc(R["g_ready"], 1)

            def lam_sum(i):
                dve.wait_ge(R["lam_steps"], 3 * i + 3)
                l = view(lam[:, :], "p (k c) -> p k c", k=TILES)
                dve.scalar_tensor_tensor(l, view(vdw[:, :], "p (k c) -> p k c", k=TILES)[:, :, 128:288], 0.0, l,
                                         ALU.max, ALU.add).then_inc(R["lam_ready"], 1)

            def node_lams(i):
                dve.wait_ge(R["lam_ready"], i + 1)
                if later(i):
                    dve.wait_ge(R["r_ps"], 4 * i)
                l = view(lam[:, :], "p (m l) -> p m l", l=LEVELS)
                nd = view(nodes[:, :], "p (m n) -> p m n", n=NODES)
                at = 0
                for level in range(5, 0, -1):
                    count = (CHUNK >> level) + (level == 1)
                    last = dve.tensor_tensor(nd[:, :, at:at + count], spread(l[:, :, level:level + 1], [128, 64, count]),
                                             spread(k("right", at, at + count).unsqueeze(1), [128, 64, count]), ALU.mult)
                    at += count
                last.then_inc(R["nodes_ready"], 1)

            def node_rows(i):
                dve.wait_ge(R["nodes_ready"], i + 1)
                if later(i):
                    dve.wait_ge(R["lam_ps"], 4 * i)
                dve.transpose(nodesT[:, :], nodes[:, :]).then_inc(R["nodesT_ready"], 1)

            def sums(i):
                dve.wait_ge(R["gT_ps"], i + 1)
                dve.tensor_tensor_scan(cgC[:, :], ones[:, :], P1[1][0:16, :], 0.0, ALU.mult, ALU.add)\
                    .then_inc(R["cgC_ready"], 1)

            def token_sums(i):
                dve.wait_ge(R["cgT_ps"], i + 1)
                if later(i):
                    dve.wait_ge(R["diff_ready"], i)
                dve.tensor_copy(cgt[:, :], P1[2][:, 0:64]).then_inc(R["cgt_ready"], 1)

            def level_factors(i):
                dve.wait_ge(R["cgc_ps"], i + 1)
                P = P1[2]
                dve.tensor_tensor(view(lev[:, 0:128], "p (a m) -> p a m", a=2), view(P[:, 64:192], "p (a m) -> p a m", a=2),
                                  spread(cgt[:, :].unsqueeze(1), [128, 2, 64]), ALU.subtract)
                dve.tensor_tensor(view(lev[:, 128:192], "p (a b h) -> p a b h", a=2, b=2),
                                  spread(view(P[:, 192:224], "p (a h) -> p a h", a=2).unsqueeze(2), [128, 2, 2, H]),
                                  view(cgt[:, :], "p (a b h) -> p a b h", a=2, b=2), ALU.subtract)
                dve.tensor_tensor(view(lev[:, 192:256], "p (a h) -> p a h", a=TILES),
                                  spread(P[:, 224:240].unsqueeze(1), [128, TILES, H]),
                                  view(cgt[:, :], "p (a h) -> p a h", a=TILES), ALU.subtract).then_inc(R["lev_diff"], 1)
                dve.wait_ge(R["lev_diff"], i + 1)
                dve.scalar_tensor_tensor(lev[:, :], lev[:, :], -1.0, lev[:, :], ALU.mult, ALU.min)\
                    .then_inc(R["lev_neg"], 1)

            def level_weights(i):
                dve.wait_ge(R["lam_ready"], i + 1)
                dve.tensor_tensor(view(alpha[:, :], "p (l m) -> p l m", l=4),
                                  view(lam[:, :], "p (m l) -> p l m", l=LEVELS)[:, 6:10],
                                  view(k("alpha_mask"), "p (l m) -> p l m", l=4), ALU.mult).then_inc(R["alpha_steps"], 1)
                dve.wait_ge(R["e4_ready"], i + 1)
                dve.wait_ge(R["alpha_steps"], 2 * i + 1)
                dve.tensor_tensor(alpha[:, :], alpha[:, :], e4[:, :], ALU.mult).then_inc(R["alpha_steps"], 1)
                bt = view(beta[:, :], "p (k s h) -> p k s h", k=TILES, s=5)
                bm = view(k("beta_mask"), "p (k s h) -> p k s h", k=TILES, s=5)
                e = view(e4[:, :], "p (l k h) -> p k l h", l=4, k=TILES)
                if later(i):
                    dve.wait_ge(R["vp_ready"], i)
                dve.tensor_tensor(bt[:, :, 0:2], spread(e[:, :, 0:1], [128, TILES, 2, H]), bm[:, :, 0:2], ALU.mult)
                dve.tensor_tensor(bt[:, :, 2:5], e[:, :, 1:4], bm[:, :, 2:5], ALU.mult).then_inc(R["beta_ready"], 1)

            def pair_exponents(i):
                dve.wait_ge(R["cgt_ready"], i + 1)
                if later(i):
                    dve.wait_ge(R["y1_ps"], 4 * i)
                dve.transpose(view(pair[:, :], "p (m t) -> p m t", t=CHUNK), spread(cgt[:, :].unsqueeze(2), [128, 64, CHUNK]))\
                    .then_inc(R["cgrow_ready"], 1)
                pw = view(pair[:, :], "p (m t) -> p m t", t=CHUNK)
                dve.wait_ge(R["cgrow_ready"], i + 1)
                dve.tensor_tensor(pw, pw, spread(cgt[:, :].unsqueeze(2), [128, 64, CHUNK]), ALU.subtract)\
                    .then_inc(R["diff_ready"], 1)
                dve.wait_ge(R["diff_ready"], i + 1)
                dve.tensor_scalar(pair[:, :], pair[:, :], 0.0, None, ALU.min).then_inc(R["diff_min"], 1)

            def pair_weights(i, n):
                if n == 0:
                    dve.wait_ge(R["decay_ready"], i + 1)
                dve.wait_ge(R["lam_ps"], 4 * i + n + 1)
                dve.tensor_tensor(tile(pair, n, 512), tile(pair, n, 512), P1[2][:, :], ALU.mult)\
                    .then_inc(R["dlam_ready"], 1)
                dve.wait_ge(R["s_ps"], 4 * i + n + 1)
                dve.wait_ge(R["dlam_ready"], 4 * i + n + 1)
                dve.tensor_tensor(tile(pair, n, 512), tile(pair, n, 512), P1[1][:, :], ALU.mult)\
                    .then_inc(R["w_ready"], 1)

            def level_sum(i, n):
                dve.wait_ge(R["lev_ps"], 4 * i + n + 1)
                al = view(alpha[:, :], "p (l k h) -> p k l h", l=4, k=TILES)[:, n]
                runs = [[(0, 0, 2)], [(0, 0, 3)], [(0, 0, 2), (2, 3, 1)], [(0, 0, 4)]][n]
                for at, level, count in runs:
                    o = view(lv[:, 128 * at:128 * (at + count)], "p (l h e) -> p l h e", l=count, e=HD)
                    p = view(P1[0][:, 128 * at:128 * (at + count)], "p (l h e) -> p l h e", l=count, e=HD)
                    last = dve.tensor_tensor(o, p, spread(al[:, level:level + count].unsqueeze(3), [128, count, H, HD]),
                                             ALU.mult)
                last.then_inc(R["lev_ready"], 1)
                dve.wait_ge(R["lev_ready"], 4 * i + n + 1)
                count = sum(r[2] for r in runs)
                dve.tensor_reduce(lvs[:, :], view(lv[:, 0:128 * count], "p (l v) -> p v l", l=count), AX.X, ALU.add)\
                    .then_inc(R["levsum_ready"], 1)

            def own_heads(i, n):
                dve.wait_ge(R["y1_ps"], 4 * i + n + 1)
                if later(i, n // 2):
                    dve.wait_ge(R["y2_ps"], 4 * i + n - 1)
                dve.tensor_tensor(view(tile(ym, n % 2, 512), "p (m a e) -> p m a e", m=16, a=4),
                                  view(P1[3][:, :], "p (m a e) -> p m a e", m=16, a=4),
                                  spread(k("own_head").unsqueeze(1).unsqueeze(3), [128, 16, 4, HD]), ALU.mult)\
                    .then_inc(R["ym_ready"], 1)

            def tile_sum(i, n):
                dve.wait_ge(R["y2_ps"], 4 * i + n + 1)
                dve.wait_ge(R["levsum_ready"], 4 * i + n + 1)
                if n == 0:
                    if later(i):
                        dve.wait_ge(R["ytT_ps"], i)
                dve.tensor_tensor(tile(yt, n), lvs[:, :], P1[4][:, 0:128], ALU.add).then_inc(R["yt_ready"], 1)

            def attention_out(i):
                dve.wait_ge(R["wo_ps"], i + 1)
                if later(i):
                    dve.wait_ge(R["ng_ready"], i)
                dve.tensor_tensor(ob[:, :], P1[1][:, :], skip[:, :], ALU.add).then_inc(R["ob_ready"], 1)

            def norm2(i):
                dve.wait_ge(R["ob_ready"], i + 1)
                stats(ob, st2, mv2, "st2_ready", "mv2_ready", i)
                dve.wait_ge(R["r2_ready"], i + 1)
                normalise(ob, ob, mv2, sm2[:, 4:8]).then_inc(R["n_ready"], 1)

            def recurrence(i):
                dve.wait_ge(R["tf_ready"], i + 1)
                if later(i):
                    dve.wait_ge(R["c_ready"], i)
                dve.scalar_tensor_tensor(tf[:, :], tf[:, :], 1.0, cell[:, :], ALU.add, ALU.mult).then_inc(R["fc_ready"], 1)
                dve.wait_ge(R["tg_ready"], i + 1)
                dve.wait_ge(R["ti_ready"], i + 1)
                dve.scalar_tensor_tensor(ti[:, :], ti[:, :], 1.0, tg[:, :], ALU.add, ALU.mult).then_inc(R["ig_ready"], 1)
                dve.wait_ge(R["fc_ready"], i + 1)
                dve.wait_ge(R["ig_ready"], i + 1)
                dve.wait_ge(R["g_ps"], i + 1)
                dve.scalar_tensor_tensor(cell[:, :], tf[:, :], 0.5, ti[:, :], ALU.mult, ALU.add).then_inc(R["c_ready"], 1)

            def cell_out():
                dve.wait_ge(R["cp_ps"], 1)
                dve.wait_ge(R["res_init"], B)
                dve.tensor_tensor(view(c_out[:, :], "p (k d) -> p k d", d=D), view(P0[0][:, :], "p (k d) -> p k d", d=D),
                                  spread(w("bo").unsqueeze(1), [128, TILES, D]), ALU.add).then_inc(R["cp_ready"], 1)

            def end_add(b):
                dve.wait_ge(R["end_tanh"], b + 1)
                if b == B - 1:
                    dve.wait_ge(R["res_ready"], B)
                dve.tensor_tensor(end_hx[b], end_hx[b], end_res[b], ALU.add).then_inc(R["end_add"], 1)

            def stages(i, j):
                if j is not None:
                    norm0(j)
                else:
                    recurrence(i - 1)
                if i is not None:
                    if later(i):
                        attention_out(i - 1)
                    gates1(i)
                    if later(i) and j is not None:
                        recurrence(i - 1)
                    sums(i)
                    if later(i):
                        norm2(i - 1)
                    token_sums(i)
                    lam_sum(i)
                    level_factors(i)
                    node_lams(i)
                    node_rows(i)
                if j is not None:
                    delta(j)
                    turn_logits(j)
                if i is not None:
                    level_weights(i)
                if j is not None:
                    top1(j)
                    scan_inputs(j)
                else:
                    recurrence(i)
                    cell_out()
                if i is not None:
                    pair_exponents(i)
                if j is not None:
                    scans(j)
                if i is not None:
                    pair_weights(i, 0)
                    level_sum(i, 0)
                    pair_weights(i, 1)
                    own_heads(i, 0)
                if j is not None:
                    gate0(j, 0)
                if i is not None:
                    tile_sum(i, 0)
                    level_sum(i, 1)
                    pair_weights(i, 2)
                    own_heads(i, 1)
                if j is not None:
                    gate0(j, 1)
                if i is not None:
                    tile_sum(i, 1)
                    level_sum(i, 2)
                    pair_weights(i, 3)
                    own_heads(i, 2)
                    tile_sum(i, 2)
                    level_sum(i, 3)
                if j is None:
                    for b in range(FIRST):
                        end_add(b)
                else:
                    sum0(j)
                    norm1(j)
                if i is not None:
                    own_heads(i, 3)
                    tile_sum(i, 3)

            def after():
                attention_out(B - 1)
                norm2(B - 1)
                dve.wait_ge(R["end_loaded1"], 16 * (2 * (B - FIRST) - 1))
                for b in range(FIRST, B):
                    dve.tensor_tensor(end_hx[b], end_hx[b], c_out[:, :], ALU.add).then_inc(R["end_sum"], 1)
                    if b > FIRST:
                        end_add(b - 1)
                end_add(B - 1)
            schedule(dve, stages, before, after)

        @block.gpsimd
        def _(pool):
            def residual(j):
                pool.wait_ge(R["x1_ready"], j + 1)
                if later(j):
                    pool.wait_ge(R["res_stored"], 16 * j)
                pool.tensor_tensor(view(res[:, :], "p (k d) -> p k d", d=D), view(x1[:, :], "p (k d) -> p k d", d=D),
                                   spread(w("lnbias").unsqueeze(1), [128, TILES, D]), ALU.add).then_inc(R["res_init"], 1)

            def own_values(i):
                pool.wait_ge(R["vdw_ready"], 4 * i + 4)
                if later(i):
                    pool.wait_ge(R["y1_ps"], 4 * i)
                for n in range(TILES):
                    v = view(vdw[:, VDW * n:VDW * n + 128], "p (g v) -> p g v", g=4)
                    pool.tensor_tensor(view(tile(vbd, n, 512), "p (g c v) -> p g c v", g=4, c=4),
                                       spread(v.unsqueeze(2), [128, 4, 4, 32]),
                                       spread(k("own_chunk").unsqueeze(1).unsqueeze(3), [128, 4, 4, 32]), ALU.mult)\
                        .then_inc(R["vbd_ready"], 1)

            def own_level(i):
                pool.wait_ge(R["lam_ready"], i + 1)
                if later(i):
                    pool.wait_ge(R["lam_ps"], 4 * i)
                pool.tensor_tensor(view(self_lam[:, :], "p (m t) -> p m t", t=CHUNK),
                                   spread(view(lam[:, :], "p (m l) -> p m l", l=LEVELS)[:, :, 0:1], [128, 64, CHUNK]),
                                   spread(k("diag").unsqueeze(1), [128, 64, CHUNK]), ALU.mult).then_inc(R["self_ready"], 1)

            def level_values(i):
                pool.wait_ge(R["nodesT_ready"], i + 1)
                pool.wait_ge(R["beta_ready"], i + 1)
                at = 0
                for n, runs in enumerate((((0, 5),), ((0, 3), (4, 1)), ((0, 4),), ((0, 3),))):
                    v = view(vdw[:, VDW * n:VDW * n + 128], "p (h e) -> p h e", e=HD)
                    bt = view(beta[:, 80 * n:80 * n + 80], "p (s h) -> p s h", h=H)
                    for slot, count in runs:
                        last = pool.tensor_tensor(view(vp[:, at:at + 128 * count], "p (s h e) -> p s h e", s=count, e=HD),
                                                  spread(v.unsqueeze(1), [128, count, H, HD]),
                                                  spread(bt[:, slot:slot + count].unsqueeze(3), [128, count, H, HD]),
                                                  ALU.mult)
                        at += 128 * count
                last.then_inc(R["vp_ready"], 1)

            def keep_skip(i):
                pool.wait_ge(R["loaded"], 48)
                if later(i):
                    pool.wait_ge(R["ob_ready"], i)
                pool.tensor_copy(skip[:, :], xn1[:, :]).then_inc(R["skip_ready"], 1)

            def finish(i):
                pool.wait_ge(R["n_ready"], i + 1)
                pool.tensor_tensor(view(ob[:, :], "p (k d) -> p k d", d=D), view(ob[:, :], "p (k d) -> p k d", d=D),
                                   spread(w("lng").unsqueeze(1), [128, TILES, D]), ALU.mult).then_inc(R["ng_ready"], 1)
                pool.wait_ge(R["ng_ready"], i + 1)
                pool.tensor_tensor(res[:, :], res[:, :], ob[:, :], ALU.add).then_inc(R["res_ready"], 1)

            def end_sum(b):
                pool.tensor_tensor(end_hx[b], end_hx[b], c_out[:, :], ALU.add).then_inc(R["end_sum"], 1)

            def stages(i, j):
                if i is None:
                    return
                own_values(i)
                if later(i):
                    finish(i - 1)
                own_level(i)
                keep_skip(i)
                residual(i)
                level_values(i)
                if j is None:
                    pool.wait_ge(R["cp_ready"], 1)
                    pool.wait_ge(R["end_loaded0"], 16 * 2 * FIRST)
                    for b in range(FIRST):
                        end_sum(b)

            schedule(pool, stages, lambda: None, lambda: finish(B - 1))


def _columns_of(a, rows=128):
    n = a.shape[0] // rows
    return a.reshape(n, rows, -1).transpose(1, 0, 2).reshape(rows, -1)


def _pack(columns, parts):
    at, width = _offsets(columns)
    out = np.zeros((128, width), np.float32)
    for name, a in parts.items():
        out[:a.shape[0], at[name][0]:at[name][0] + a.shape[1]] = a
    return out


def _consts():
    p = np.arange(128)
    q, c = p % CHUNK, p // CHUNK
    ident = np.eye(128, dtype=np.float32)
    end6, end7 = 64 * (p // 64) + 31, np.full(128, 63)
    left = np.zeros((128, 128), np.float32)
    right = np.zeros((128, NODES), np.float32)
    at = 0
    for level in range(5, 0, -1):
        size = 1 << level
        for m in range(CHUNK // size):
            inside = (q // size == m)
            first = q % size < size // 2
            right[:, at] = inside & ~first
            for chunk in range(4):
                left[32 * chunk + at, :] = inside & first & (c == chunk)
            at += 1
    alpha = np.zeros((128, 4, TILES, H), np.float32)
    alpha[:, 0] = (p % 64 >= 32)[:, None, None]
    alpha[:, 1] = (p >= 64)[:, None, None]
    alpha[:, 2, 1::2] = 1
    alpha[:, 3, 2:] = 1
    beta = np.zeros((128, TILES, 5, H), np.float32)
    beta[:, :, 0] = (p < 32)[:, None, None]
    beta[:, :, 1] = ((p >= 64) & (p < 96))[:, None, None]
    beta[:, :, 2] = (p < 64)[:, None, None]
    beta[:, 0::2, 3] = 1
    beta[:, 0:2, 4] = 1
    expert = np.zeros((8, E * HID), np.float32)
    for e in range(E):
        expert[e, HID * e:HID * e + HID] = 1
    parts = {
        "ident": ident, "sel6": (p[:, None] == end6[None]).astype(np.float32),
        "sel7": (p[:, None] == end7[None]).astype(np.float32),
        "sel_last": np.repeat((p == 127)[:, None], 128, 1).astype(np.float32),
        "left": left, "right": right, "diag": (q[:, None] == np.arange(CHUNK)).astype(np.float32),
        "own_chunk": (c[:, None] == np.arange(4)).astype(np.float32),
        "own_head": (c[:, None] == np.arange(4)).astype(np.float32),
        "sum_heads": (q[:, None] == np.arange(CHUNK)).astype(np.float32),
        "alpha_mask": alpha.reshape(128, -1), "beta_mask": beta.reshape(128, -1),
        "rank": np.repeat((E - np.arange(E, dtype=np.float32))[None], 32, 0), "expert": expert,
        "b2_part": (np.arange(24)[:, None] // 8 == np.arange(3)).astype(np.float32),
    }
    return _pack(_const_columns(), parts)


def kernel(**inputs):
    import numpy as _np
    import concourse.bacc as _bacc
    from concourse import mybir as _mybir
    from concourse.bass_utils import run_bass_kernel_spmd as _run

    a = {n: _np.asarray(v) for n, v in inputs.items()}
    rows = lambda v, n=128: _np.repeat(v.reshape(1, -1), n, 0)
    w_xp = a["L0_attn_W_xp"]
    parts = {
        "Win": a["L0_attn_W_in"], "wdelta": _columns_of(w_xp[:, 0:1]), "Dskip": _columns_of(a["L0_attn_D"][:, None]),
        "A0": rows(a["L0_attn_A_log"]), "WgT": a["L0_ffn_Wg"].T,
        "W1": a["L0_ffn_W1"].transpose(1, 0, 2).reshape(D, -1), "lns": a["L0_ffn_ln_scale"].T,
        "lnb": a["L0_ffn_ln_bias"].T, "b1": _columns_of(a["L0_ffn_b1"].reshape(-1, 1)),
        "Wout0": _columns_of(a["L0_attn_W_out"]), "W2": _columns_of(a["L0_ffn_W2"].reshape(E * HID, D)),
        "b2": _np.concatenate([a["L0_ffn_b2"]] * 3, 0),
        "WinT": _columns_of(a["L0_attn_W_in"][:, :INNER].T), "WxpT": w_xp[:, 1:].T,
        "WBC": _np.concatenate([a["L0_attn_W_B"], a["L0_attn_W_C"]], 0),
        "Wvdw": _np.concatenate([a["L1_attn_Wv"].T,
                                 a["L1_attn_Wdl"].reshape(H, 12, D)[:, :LEVELS].reshape(-1, D).T,
                                 a["L1_attn_Wdt"].T, a["L1_ffn_wo"].T], 1),
        "Lp": rows(a["L1_attn_Lp"][:, :LEVELS]), "dtb": rows(a["L1_attn_dt_bias"]), "A1": rows(a["L1_attn_A_log"]),
        "lng": rows(a["L1_attn_ln_g"]), "lnbias": rows(a["L1_attn_ln_b"]), "WoutT": a["L1_attn_Wout"].T,
        "gates_x": _np.concatenate([a["L1_ffn_wf"].T, a["L1_ffn_wi"].T, a["L1_ffn_wc"].T], 1),
        "gates_c": _np.concatenate([a["L1_ffn_uf"].T, a["L1_ffn_ui"].T, a["L1_ffn_uc"].T], 1),
        "gate_b": _np.stack([a["L1_ffn_bf"], a["L1_ffn_bi"], a["L1_ffn_bc"]], 1),
        "uo": a["L1_ffn_uo"].T, "bo": rows(a["L1_ffn_bo"]), "c0": a["L1_ffn_in_c"][:, None],
        "Wq": _columns_of(a["L1_attn_Wq"], HS), "Wk": _columns_of(a["L1_attn_Wk"], HS),
    }
    arrays = {
        "in_x": _np.ascontiguousarray(a["L0_attn_x"]),
        "in_weights": _pack(_weight_columns(), parts),
        "in_consts": _consts(),
    }
    nc = _bacc.Bacc("TRN2", target_bir_lowering=False, num_devices=1)
    fp32 = _mybir.dt.float32
    args = [nc.dram_tensor(name, v.shape, fp32, kind="ExternalInput").ap() for name, v in arrays.items()]
    args.append(nc.dram_tensor("out_0", (B, T, D), fp32, kind="ExternalOutput").ap())
    build(nc, *args)
    r = _run(nc, [arrays], core_ids=[0])
    return r.results[0]["out_0"]
```

```python
import numpy as np

B, T, D = 16, 512, 128
TILES = T // 128
INNER, STATE = 256, 64
E, HID = 8, 32
H, HS, HD = 16, 64, 8
LEVELS = 10
CHUNK = 32
NODES = 32
EPS = 1e-5
BIG = 1e30


def _weight_columns():
    return {
        "Win": 2 * INNER, "wdelta": 2, "Dskip": 2, "A0": 1, "WgT": 32, "W1": E * HID,
        "lns": E, "lnb": E, "b1": 2, "Wout0": 2 * D, "W2": 2 * D, "b2": D,
        "Wvdw": 128 + 160 + 16 + 128, "dtb": H, "A1": H, "lng": D, "lnbias": D,
        "WoutT": D, "gates_c": 3 * D, "gate_b": 3, "uo": D, "bo": D, "c0": 1,
        "WinT": 2 * D, "WxpT": INNER, "WBC": INNER, "Lp": 160, "Wq": H * D // 2, "Wk": H * D // 2,
        "gates_x": 3 * D,
    }


def _const_columns():
    return {
        "ident": 128, "sel6": 128, "sel7": 128, "sel_last": 128, "left": 128, "right": NODES,
        "diag": CHUNK, "own_chunk": 4, "own_head": 4, "sum_heads": CHUNK,
        "alpha_mask": 4 * TILES, "beta_mask": TILES * 5, "rank": E, "expert": E * HID, "b2_part": 3,
    }


def _offsets(columns):
    at, out = 0, {}
    for name, width in columns.items():
        out[name] = (at, width)
        at += width
    return out, at


def build(nc, x, weights, consts, out):
    import concourse.bass as bass
    from concourse import mybir
    from contextlib import ExitStack

    fp32, bf16, fp32r = mybir.dt.float32, mybir.dt.bfloat16, mybir.dt.float32r
    ACT, ALU, AX = mybir.ActivationFunctionType, mybir.AluOpType, mybir.AxisListType
    wat, wwidth = _offsets(_weight_columns())
    cat, cwidth = _offsets(_const_columns())

    with ExitStack() as ctx:
        def sb(name, cols, dt=fp32, rows=128):
            return ctx.enter_context(nc.sbuf_tensor(name, [rows, cols], dt))

        def psum(name):
            return ctx.enter_context(nc.psum_tensor(name, [128, 512], fp32))

        def sem(name):
            return ctx.enter_context(nc.semaphore(name))

        kept = wat["WinT"][0]
        W = sb("W", kept)
        K = sb("K", cwidth)

        def w(name, a=0, b=None, rows=128):
            at, width = wat[name]
            t = W if at < kept else gx
            at -= 0 if at < kept else kept
            return t[0:rows, at + a:at + (width if b is None else b)]

        def k(name, a=0, b=None, rows=128):
            at, width = cat[name]
            return K[0:rows, at + a:at + (width if b is None else b)]

        def tile(t, n, width=128):
            return t[:, n * width:(n + 1) * width]

        ident = k("ident")
        MB = sb("MB", INNER)
        MC = sb("MC", INNER)
        Mdelta = sb("Mdelta", 128)
        Gh = sb("Gh", H * 128, fp32r)
        Gl = sb("Gl", H * 128, fp32r)
        GT = sb("GT", H * 128)
        gates_xh = sb("gates_xh", 3 * D, fp32r)
        gates_xl = sb("gates_xl", 3 * D, fp32r)
        bias_u = sb("bias_u", 2)
        neg_a0 = sb("neg_a0", 1)
        neg_a1 = sb("neg_a1", H)
        expert_b = sb("expert_b", E * HID, bf16, 32)
        b2_b = sb("b2_b", D, bf16, 32)
        ones = sb("ones", 8, fp32, 16)
        xin = sb("xin", T)
        st0 = sb("st0", TILES * 6)
        mv0 = sb("mv0", TILES * 2)
        sm0 = sb("sm0", 8 * TILES)
        xn = sb("xn", T)
        xh = sb("xh", T)
        xnT = sb("xnT", T)
        xhT = sb("xhT", T)
        sp0 = sb("sp0", T)
        decay0 = sb("decay0", T)
        xi = sb("xi", 2 * T)
        y = sb("y", 2 * T)
        th = sb("th", 2 * T)
        gelu = sb("gelu", 2 * T)
        lgT = sb("lgT", T, fp32, 32)
        oh = sb("oh", T, fp32, 32)
        ohT = lgT
        lv = sb("lv", 4 * 128 + 64)
        am = lv[0:32, :]
        mask_b = sb("mask_b", T, bf16, 32)
        oh_b = sb("oh_b", T, bf16, 32)
        x1 = sb("x1", T)
        st1 = sb("st1", TILES * 6)
        mv1 = sb("mv1", TILES * 2)
        sm1 = sb("sm1", 2 * TILES)
        st2 = sb("st2", TILES * 6)
        mv2 = sb("mv2", TILES * 2)
        sm2 = sb("sm2", 2 * TILES)
        skip = sb("skip", T)
        xn1 = sb("xn1", T)
        x1T = sb("x1T", T)
        VDW = 432
        vdw = sb("vdw", TILES * VDW)
        lam = sb("lam", TILES * 160)
        x1Th = sb("x1Th", T, fp32r)
        x1Tl = sb("x1Tl", T, fp32r)
        cgt = sb("cgt", 64)
        lev = sb("lev", 256)
        e4 = sb("e4", 256)
        alpha = sb("alpha", 256)
        beta = sb("beta", TILES * 5 * H)
        gx = sb("gx", H * T)
        pair = sb("pair", TILES * 512)
        nodesT = sb("nodesT", TILES * 512)
        self_lam = sb("self_lam", TILES * 512)
        vp = sb("vp", 2048)
        vbd = sb("vbd", TILES * 512)
        rs = sb("rs", 2048)
        ms = sb("ms", 2048)
        nodes = ms
        yt, ytT, ob = rs[:, 0:T], rs[:, T:2 * T], rs[:, 2 * T:3 * T]
        tf, ti, tg = ms[:, 0:T], ms[:, T:2 * T], rs[:, 3 * T:4 * T]
        ym = sb("ym", 2 * 512)
        cgC, dts = ym[0:16, 0:T], pair[:, 0:10 * 64]
        lvs = sb("lvs", 128)
        cell = sb("cell", T)
        hx_dram = nc.dram_tensor("hx_scratch", (B, 128, T), fp32, kind="Internal").ap()
        res_dram = nc.dram_tensor("res_scratch", (B, 128, T), fp32, kind="Internal").ap()
        res = sb("res", T)
        WQ, WK = w("Wq"), w("Wk")

        GROUPS = ((0, 7), (7, 11), (11, B))
        free = [tile(t, n, T) for t in (y, gelu, xi, th) for n in range(2)] \
            + [t[:, :] for t in (xnT, xhT, xn, xh, xin, decay0)]
        end_hx = free[0:7] + [tile(GT, n, T) for n in range(4)] + [tile(gx, n, T) for n in range(5)]
        end_res = free[7:14] + [tile(vp, n, T) for n in range(4)] + [tile(gx, n, T) for n in range(5, 9)] + [res[:, :]]
        c_out = sp0

        P0 = [psum(f"p0_{n}") for n in range(3)]
        P1 = [psum(f"p1_{n}") for n in range(5)]

        names = """loaded heads_loaded folded setup_ps setup_ev setup_done G_ps G_ready Gh_ready Gl_ready
            gates_xh_ready gates_xl_ready
            x_loaded st0_ready mv0_ready ln0_steps r0_ready vr_steps q0_ready rr_ready xn_ready xh_ready
            xnT_ps xhT_ps xnT_ready xhT_ready logit_ps top1_steps ohT_ready delta_ps sp0_steps delta_ready decay0_ready
            xi0_ps xi1_ps xi0_ready xi1_ready b0_ps b1_ps bx0_ready bx1_ready h0_ready h1_ready
            c0_ps c1_ps ch0_ready ch1_ready yd0_ready yd1_ready z0_ps z1_ps th0_ready th1_ready
            sz0_ready sz1_ready y0_ready y1_ready u0_ps u1_ps g0_ready g1_ready out0_ps x1_ready
            st1_ready mv1_ready ln1_ready r1_ready xn1_ready x1T_ps x1T_ready x1Th_ready x1Tl_ready vdw_ps vdw_ready hx_stored
            lam_steps lam_ready dt_in dt_act dt_steps g_ready gT_ps cgC_ready cgT_ps cgt_ready cgc_ps
            lev_diff lev_neg e4_ready alpha_steps beta_ready vp_ready r_ps r_copied m_ps m_copied
            gx_ps gx_copied cgrow_ready diff_ready diff_abs decay_ready nodes_ready nodesT_ready self_ready
            s_ps lam_ps dlam_ready lams_ready w_ready vbd_ready y1_ps ym_ready y2_ps lev_ps lev_ready levsum_ready
            yt_ready ytT_ps ytT_ready wo_ps ob_ready st2_ready mv2_ready ln2_ready r2_ready n_ready
            res_init skip_ready ng_ready res_ready res_stored f_ps i_ps g_ps tf_ready ti_ready tg_ready ig_ready c_ready dxi_ready
            cp_ps cp_ready end_loaded0 end_loaded1 end_loaded2 end_sum end_tanh end_add end_stored""".split()
        R = {n: sem(n) for n in names}

        def later(i, n=0):
            return not (isinstance(i, int) and i == 0 and n == 0)

        def view(ap, spec, **sizes):
            return ap.rearrange(spec, **sizes)

        def spread(ap, shape):
            return ap.broadcast_to(shape)

        def head_bank(h):
            return P1[(2 + h) % 5] if h < 4 else P1[(3, 4, 0)[(h - 4) % 3]]

        block = ctx.enter_context(nc.Block())

        def schedule(eng, stages, before, after):
            before()
            stages(None, 0)
            stages(0, 1)
            with eng.Fori(1, B - 1) as i:
                stages(i, i + 1)
            stages(B - 1, None)
            after()

        @block.sync
        def _(sp):
            def before():
                load_x(0)
                first = wat["Wq"][0]
                sp.dma_start(gx[:, 0:first - kept], weights[:, kept:first]).then_inc(R["loaded"], 16)
                sp.dma_start(K[:, :], consts).then_inc(R["loaded"], 16)
                sp.dma_start(W[:, :], weights[:, 0:kept]).then_inc(R["loaded"], 16)
                sp.dma_start(gx[:, first - kept:wwidth - kept], weights[:, first:wwidth]).then_inc(R["heads_loaded"], 16)

            def load_x(j):
                if later(j):
                    sp.wait_ge(R["x1_ready"], j)
                src = x[j:j + 1] if isinstance(j, int) else x[bass.ds(j, 1)]
                sp.dma_start(view(xin[:, :], "p (a k d) -> p a k d", a=1, d=D),
                             view(src, "a (k p) d -> p a k d", p=128)).then_inc(R["x_loaded"], 16)

            def row(dram, b):
                return view(dram[b:b + 1] if isinstance(b, int) else dram[bass.ds(b, 1)], "a p n -> p (a n)")

            def store_hx(i):
                sp.wait_ge(R["vdw_ready"], 4 * i + 4)
                sp.dma_start(view(row(hx_dram, i), "p (k d) -> p k d", d=D),
                             view(vdw[:, :], "p (k c) -> p k c", k=TILES)[:, :, 304:432]).then_inc(R["hx_stored"], 16)

            def store_res(i):
                sp.wait_ge(R["res_ready"], i + 1)
                sp.dma_start(row(res_dram, i), res[:, :]).then_inc(R["res_stored"], 16)

            def load(group):
                for b in range(*GROUPS[group]):
                    sp.dma_start(end_hx[b], row(hx_dram, b)).then_inc(R[f"end_loaded{group}"], 16)
                    if b < B - 1:
                        sp.dma_start(end_res[b], row(res_dram, b)).then_inc(R[f"end_loaded{group}"], 16)

            def stages(i, j):
                if i is not None and j is not None:
                    load_x(j)
                if j is None:
                    sp.wait_ge(R["res_stored"], 16 * (B - 2))
                    sp.wait_ge(R["hx_stored"], 16 * (B - 1))
                    sp.wait_ge(R["x1_ready"], B)
                    sp.wait_ge(R["u1_ps"], B)
                    load(0)
                if i is not None:
                    if later(i):
                        store_res(i - 1)
                    store_hx(i)

            def after():
                def store(group):
                    for b in range(*GROUPS[group]):
                        sp.wait_ge(R["end_add"], b + 1)
                        sp.dma_start(view(out[b], "(k p) d -> p k d", p=128),
                                     view(end_hx[b], "p (k d) -> p k d", d=D)).then_inc(R["end_stored"], 16)

                sp.wait_ge(R["res_stored"], 16 * (B - 1))
                sp.wait_ge(R["hx_stored"], 16 * B)
                sp.wait_ge(R["m_ps"], 4 * B)
                sp.wait_ge(R["r_ps"], 4 * B)
                load(1)
                sp.wait_ge(R["s_ps"], 4 * B)
                load(2)
                store(0)
                store(1)
                store(2)
                sp.wait_ge(R["end_stored"], 16 * B)
            schedule(sp, stages, before, after)

        @block.tensor
        def _(pe):
            def before():
                pe.wait_ge(R["loaded"], 48)
                for n, half in enumerate(("B", "C")):
                    rows = slice(64 * n, 64 * n + 64)
                    for q in range(2):
                        mm = pe.matmul(P0[n][:, 256 * q:256 * q + 256],
                                       w("WxpT", 128 * q, 128 * q + 128)[rows, :], w("WBC")[rows, :],
                                       start=True, stop=True)
                mm.then_inc(R["setup_ps"], 1)
                for e in range(E):
                    mm = pe.matmul(P1[0][32 * (e % 4):32 * (e % 4) + 32, e // 4:e // 4 + 1],
                                   w("W1", HID * e, HID * e + HID), w("lnb", e, e + 1), start=True, stop=True)
                mm.then_inc(R["setup_ps"], 1)
                for q in range(2):
                    mm = pe.matmul(P1[1][:, 0:128], w("WinT", 128 * q, 128 * q + 128),
                                   spread(w("wdelta", q, q + 1), [128, 128]), start=(q == 0), stop=(q == 1))
                mm.then_inc(R["setup_ps"], 1)
                pe.wait_ge(R["setup_ev"], 2)
                for n in range(2):
                    for q in range(2):
                        mm = pe.matmul(P1[2][:, 256 * n:256 * n + 256], w("WinT", 128 * q, 128 * q + 128),
                                       tile(xi, n, 512)[:, 256 * q:256 * q + 256], start=(q == 0), stop=(q == 1))
                mm.then_inc(R["setup_ps"], 1)
                pe.wait_ge(R["setup_done"], 3)

            def fold_heads(a, b):
                pe.wait_ge(R["heads_loaded"], 16)
                for m in range(a, b):
                    g, lhs, rhs = m // 2, (WQ, WK)[m % 2], (WK, WQ)[m % 2]
                    if m >= 5:
                        pe.wait_ge(R["G_ready"], m - 4)
                    for a in range(4):
                        h = 4 * g + a
                        rows, cols = slice(HS * (h // 8), HS * (h // 8) + HS), slice(D * (h % 8), D * (h % 8) + D)
                        mm = pe.matmul(P1[m % 5][:, 128 * a:128 * a + 128], lhs[rows, cols], rhs[rows, cols],
                                       start=True, stop=True)
                    mm.then_inc(R["G_ps"], 1)

            def turn_x(j):
                if not isinstance(j, int):
                    pe.wait_ge(R["tf_ready"], j - 1)
                elif j == 1:
                    pe.wait_ge(R["g0_ready"], 1)
                pe.wait_ge(R["xn_ready"], j + 1)
                for n in range(TILES):
                    mm = pe.transpose(tile(P0[0], n), tile(xn, n), ident)
                mm.then_inc(R["xnT_ps"], 1)
                if not isinstance(j, int):
                    pe.wait_ge(R["ti_ready"], j - 1)
                elif j == 1:
                    pe.wait_ge(R["g1_ready"], 1)
                pe.wait_ge(R["xh_ready"], j + 1)
                for n in range(TILES):
                    mm = pe.transpose(tile(P0[1], n), tile(xh, n), ident)
                mm.then_inc(R["xhT_ps"], 1)

            def logits(j):
                if not isinstance(j, int):
                    pe.wait_ge(R["tg_ready"], j - 1)
                elif j == 1:
                    pe.wait_ge(R["x1_ready"], 1)
                pe.wait_ge(R["xnT_ready"], j + 1)
                pe.matmul(P0[2][0:32, :], w("WgT"), xnT[:, :], start=True, stop=True).then_inc(R["logit_ps"], 1)
                pe.matmul(P0[0][:, :], Mdelta[:, :], xnT[:, :], start=True, stop=True).then_inc(R["delta_ps"], 1)

            def project(j, bank, free, value, lhs, done):
                pe.wait_ge(R[free], value)
                pe.matmul(P0[bank][:, :], lhs, xnT[:, :], start=True, stop=True).then_inc(R[done], 1)

            def scan_x(j):
                project(j, 1, "xhT_ready", j + 1, w("Win", 0, 128), "xi0_ps")
                project(j, 2, "top1_steps", 7 * j + 1, w("Win", 128, 256), "xi1_ps")

            def scan_b(j):
                project(j, 0, "delta_ready", j + 1, MB[:, 0:128], "b0_ps")
                project(j, 1, "xi0_ready", j + 1, MB[:, 128:256], "b1_ps")

            def scan_c(j):
                project(j, 2, "xi1_ready", j + 1, MC[:, 0:128], "c0_ps")
                project(j, 0, "bx0_ready", j + 1, MC[:, 128:256], "c1_ps")

            def gate_z(j, q):
                if q == 0:
                    project(j, 1, "bx1_ready", j + 1, w("Win", 256, 384), "z0_ps")
                else:
                    project(j, 2, "ch0_ready", j + 1, w("Win", 384, 512), "z1_ps")

            def gate_u(j, q):
                pe.wait_ge(R["top1_steps"], 7 * j + 7)
                if q == 0:
                    pe.wait_ge(R["ch1_ready"], j + 1)
                else:
                    pe.wait_ge(R["sz0_ready"], j + 1)
                pe.matmul(P0[q][:, :], expert_b[0:8, 128 * q:128 * q + 128], mask_b[0:8, :],
                          start=True, stop=False)
                pe.matmul(P0[q][:, :], w("W1", 128 * q, 128 * q + 128), xhT[:, :],
                          start=False, stop=True).then_inc(R[f"u{q}_ps"], 1)

            def out0(j):
                pe.wait_ge(R["sz1_ready"], j + 1)
                for name in ("y0_ready", "y1_ready", "g0_ready", "g1_ready"):
                    pe.wait_ge(R[name], j + 1)
                for n in range(TILES):
                    o, t = tile(P0[2], n), slice(128 * n, 128 * n + 128)
                    pe.matmul(o, y[:, t], w("Wout0", 0, D), start=True, stop=False)
                    pe.matmul(o, y[:, 128 * n + T:128 * n + T + 128], w("Wout0", D), start=False, stop=False)
                    pe.matmul(o, gelu[:, t], w("W2", 0, D), start=False, stop=False)
                    pe.matmul(o, gelu[:, 128 * n + T:128 * n + T + 128], w("W2", D), start=False, stop=False)
                    mm = pe.matmul(o, oh_b[0:24, t], b2_b[0:24, :], start=False, stop=True)
                mm.then_inc(R["out0_ps"], 1)

            def turn_x1(j):
                if later(j):
                    pe.wait_ge(R["lev_ready"], 4 * j)
                else:
                    pe.wait_ge(R["G_ready"], 8)
                pe.wait_ge(R["xn1_ready"], j + 1)
                for n in range(TILES):
                    mm = pe.transpose(tile(P1[0], n), tile(xn1, n), ident)
                mm.then_inc(R["x1T_ps"], 1)

            def values(j):
                pe.wait_ge(R["x1T_ready"], j + 1)
                for n, free in enumerate(("dlam_ready", "ym_ready", "yt_ready", "x1Th_ready")):
                    if n == 0 and not later(j):
                        pe.wait_ge(R["G_ready"], 8)
                    if n == 3:
                        pe.wait_ge(R[free], j + 1)
                    elif later(j):
                        pe.wait_ge(R[free], 4 * j)
                    pe.matmul(P1[(2 + n) % 5][:, 0:VDW], tile(x1T, n), w("Wvdw"), start=True, stop=True)\
                        .then_inc(R["vdw_ps"], 1)

            def heads(i, a, b):
                for h in range(a, b):
                    if h < 4:
                        pe.wait_ge(R["vdw_ready"], 4 * i + h + 1)
                    else:
                        pe.wait_ge(R["gx_copied"], 16 * i + h - 2)
                    if h == 0:
                        pe.wait_ge(R["x1Tl_ready"], i + 1)
                        if not later(i):
                            pe.wait_ge(R["Gl_ready"], 1)
                    pe.matmul(head_bank(h)[:, :], tile(Gl, h), x1Th[:, :], start=True, stop=False)
                    pe.matmul(head_bank(h)[:, :], tile(Gh, h), x1Tl[:, :], start=False, stop=False)
                    pe.matmul(head_bank(h)[:, :], tile(Gh, h), x1Th[:, :], start=False, stop=True).then_inc(R["gx_ps"], 1)

            def gates_to_rows(i):
                if later(i):
                    pe.wait_ge(R["ob_ready"], i)
                pe.wait_ge(R["g_ready"], i + 1)
                for n in range(TILES):
                    mm = pe.transpose(P1[1][0:16, 128 * n:128 * n + 128],
                                      dts[:, 576 + 16 * n:576 + 16 * n + 16], ident)
                mm.then_inc(R["gT_ps"], 1)

            def sums_to_tokens(i):
                pe.wait_ge(R["loaded"], 48)
                pe.wait_ge(R["cgC_ready"], i + 1)
                for n in range(TILES):
                    mm = pe.transpose(P1[2][:, 16 * n:16 * n + 16], cgC[:, 128 * n:128 * n + 128], k("ident", 0, 16, 16))
                mm.then_inc(R["cgT_ps"], 1)

            def left_ends(i):
                pe.wait_ge(R["cgt_ready"], i + 1)
                pe.matmul(P1[2][:, 64:128], k("sel6"), cgt[:, :], start=True, stop=True)
                pe.matmul(P1[2][:, 128:192], k("sel7"), cgt[:, :], start=True, stop=True)
                pe.matmul(P1[2][:, 192:224], k("sel_last"),
                          view(cgt[:, :], "p (a b h) -> p a b h", a=2, b=2)[:, :, 0, :], start=True, stop=True)
                pe.matmul(P1[2][:, 224:240], k("sel_last"), cgt[:, 16:32], start=True, stop=True)\
                    .then_inc(R["cgc_ps"], 1)

            def left_halves(i):
                pe.wait_ge(R["vp_ready"], i + 1)
                for n in range(TILES):
                    if n < 3:
                        pe.wait_ge(R["gx_copied"], 16 * i + 14 + n)
                    else:
                        pe.wait_ge(R["r_copied"], 4 * i + 1)
                    bank = P1[(3, 4, 0, 3)[n]]
                    if n == 1:
                        pe.matmul(bank[:, 384:512], tile(xn1, 0), vp[:, 512:640], start=True, stop=False)
                        pe.matmul(bank[:, 384:512], tile(xn1, 1), vp[:, 1024:1152], start=False, stop=True)
                    at = (0, 640, 1152, 1664)[n]
                    cols = 512 if n in (0, 2) else 384
                    pe.matmul(bank[:, 0:cols], tile(xn1, n), vp[:, at:at + cols], start=True, stop=True)\
                        .then_inc(R["r_ps"], 1)

            def node_matrices(i):
                pe.wait_ge(R["r_copied"], 4 * i + 4)
                if not later(i):
                    pe.wait_ge(R["G_ready"], 8)
                for g in range(4):
                    if g == 3:
                        pe.wait_ge(R["m_copied"], 4 * i + 1)
                    bank = P1[(4, 0, 3, 4)[g]]
                    for a in range(4):
                        h = 4 * g + a
                        mm = pe.matmul(bank[:, 120 * a:120 * a + 120], tile(GT, h),
                                       view(rs[:, 0:1920], "p (n c) -> p n c", c=128)[:, :, HD * h:HD * h + HD],
                                       start=True, stop=True)
                    mm.then_inc(R["m_ps"], 1)

            def pair_scores(i, n):
                if n == 0:
                    pe.wait_ge(R["cgC_ready"], i + 1)
                    pe.wait_ge(R["gx_copied"], 16 * i + 16)
                else:
                    pe.wait_ge(R["w_ready"], 4 * i + n)
                for c in range(4):
                    mm = pe.matmul(P1[1][32 * c:32 * c + 32, :], x1T[:, 128 * n + 32 * c:128 * n + 32 * c + 32],
                                   view(gx[:, :], "p (h t) -> p h t", h=H)[:, :, 128 * n + 32 * c:128 * n + 32 * c + 32],
                                   start=True, stop=True)
                mm.then_inc(R["s_ps"], 1)

            def pair_levels(i, n):
                if n == 0:
                    pe.wait_ge(R["lev_diff"], i + 1)
                    pe.wait_ge(R["nodesT_ready"], i + 1)
                else:
                    pe.wait_ge(R["dlam_ready"], 4 * i + n)
                pe.matmul(P1[2][:, :], k("left"), tile(nodesT, n, 512), start=True, stop=True).then_inc(R["lam_ps"], 1)

            def levels(i, n):
                pe.wait_ge(R["m_copied"], 4 * i + 4)
                if n > 0:
                    pe.wait_ge(R["lev_ready"], 4 * i + n)
                node = lambda a: tile(ms, a)
                bank = P1[0]
                for c in range(2):
                    pe.matmul(bank[64 * c:64 * c + 64, 0:128], x1T[:, 128 * n + 64 * c:128 * n + 64 * c + 64],
                              node(4 * n + c), start=True, stop=True)
                full = [4 * n + 2] + [[], [3], [7], [11, 7]][n]
                for a, m in enumerate(full):
                    mm = pe.matmul(bank[:, 128 * (a + 1):128 * (a + 2)], tile(x1T, n), node(m), start=True, stop=True)
                mm.then_inc(R["lev_ps"], 1)

            def chunk_values(i, n):
                if n > 0:
                    pe.wait_ge(R["ym_ready"], 4 * i + n)
                pe.wait_ge(R["m_copied"], 4 * i + 4)
                pe.wait_ge(R["w_ready"], 4 * i + n + 1)
                pe.wait_ge(R["vbd_ready"], 4 * i + n + 1)
                for g in range(4):
                    at = 512 * n + 128 * g
                    mm = pe.matmul(tile(P1[3], g), pair[:, at:at + 128], vbd[:, at:at + 128], start=True, stop=True)
                mm.then_inc(R["y1_ps"], 1)

            def chunk_sums(i, n):
                if n > 0:
                    pe.wait_ge(R["yt_ready"], 4 * i + n)
                pe.wait_ge(R["ym_ready"], 4 * i + n + 1)
                for c in range(4):
                    mm = pe.matmul(P1[4][32 * c:32 * c + 32, 0:128], k("sum_heads"),
                                   view(tile(ym, n % 2, 512), "p (g c v) -> p g c v", g=4, c=4)[:, :, c, :],
                                   start=True, stop=True)
                mm.then_inc(R["y2_ps"], 1)

            def turn_out(i):
                pe.wait_ge(R["w_ready"], 4 * i + 4)
                pe.wait_ge(R["yt_ready"], 4 * i + 4)
                for n in range(TILES):
                    mm = pe.transpose(tile(P1[1], n), tile(yt, n), ident)
                mm.then_inc(R["ytT_ps"], 1)

            def project_out(i):
                pe.wait_ge(R["ytT_ready"], i + 1)
                for n in range(TILES):
                    mm = pe.matmul(tile(P1[1], n), tile(ytT, n), w("WoutT"), start=True, stop=True)
                mm.then_inc(R["wo_ps"], 1)

            def recurrence(i, j, n):
                if n == 0:
                    if later(i):
                        pe.wait_ge(R["c_ready"], i)
                    else:
                        pe.wait_ge(R["gates_xl_ready"], 1)
                    if j is None:
                        pe.wait_ge(R["x1Tl_ready"], i + 1)
                free, done = ("g0_ready", "g1_ready", "x1_ready")[n], ("f_ps", "i_ps", "g_ps")[n]
                pe.wait_ge(R[free], B if j is None else j + 1)
                pe.matmul(P0[n][:, :], tile(gates_xl, n), x1Th[:, :], start=True, stop=False)
                pe.matmul(P0[n][:, :], tile(gates_xh, n), x1Tl[:, :], start=False, stop=False)
                pe.matmul(P0[n][:, :], tile(gates_xh, n), x1Th[:, :], start=False, stop=False)
                pe.matmul(P0[n][:, :], w("gates_c", 128 * n, 128 * n + 128), cell[:, :],
                          start=False, stop=True).then_inc(R[done], 1)

            def stages(i, j):
                if j is None:
                    for n in range(3):
                        recurrence(i, j, n)
                if i is not None:
                    heads(i, 0, 4)
                if j is not None:
                    turn_x(j)
                if i is not None:
                    heads(i, 4, 6)
                    heads(i, 6, 7)
                    gates_to_rows(i)
                    heads(i, 7, 8)
                    sums_to_tokens(i)
                if j is not None:
                    logits(j)
                if i is not None:
                    left_ends(i)
                    heads(i, 8, 12)
                else:
                    fold_heads(0, 5)
                if j is not None:
                    scan_x(j)
                else:
                    cell_out()
                if i is not None:
                    heads(i, 12, 14)
                if j is not None:
                    scan_b(j)
                if i is not None:
                    heads(i, 14, H)
                else:
                    fold_heads(5, 8)
                if j is not None:
                    scan_c(j)
                if i is not None:
                    pair_scores(i, 0)
                    left_halves(i)
                    pair_levels(i, 0)
                    node_matrices(i)
                    pair_scores(i, 1)
                    chunk_values(i, 0)
                    pair_levels(i, 1)
                    levels(i, 0)
                if j is not None:
                    gate_z(j, 0)
                if i is not None:
                    chunk_sums(i, 0)
                if j is not None:
                    gate_z(j, 1)
                if i is not None:
                    pair_scores(i, 2)
                    chunk_values(i, 1)
                    pair_levels(i, 2)
                    levels(i, 1)
                if j is not None:
                    gate_u(j, 0)
                if i is not None:
                    chunk_sums(i, 1)
                    pair_scores(i, 3)
                    chunk_values(i, 2)
                    pair_levels(i, 3)
                    levels(i, 2)
                if j is not None:
                    gate_u(j, 1)
                if i is not None:
                    chunk_sums(i, 2)
                    levels(i, 3)
                if j is not None:
                    out0(j)
                if i is not None:
                    chunk_values(i, 3)
                    if j is not None:
                        for n in range(3):
                            recurrence(i, j, n)
                if j is not None:
                    turn_x1(j)
                if i is not None:
                    chunk_sums(i, 3)
                    turn_out(i)
                if j is not None:
                    values(j)
                if i is not None:
                    project_out(i)

            def cell_out():
                pe.wait_ge(R["c_ready"], B)
                pe.wait_ge(R["tf_ready"], B)
                for n in range(TILES):
                    mm = pe.matmul(tile(P0[0], n), tile(cell, n), w("uo"), start=True, stop=True)
                mm.then_inc(R["cp_ps"], 1)
            schedule(pe, stages, before, lambda: None)

        @block.scalar
        def _(act):
            def logs():
                act.preload_act_table_set("natural_log_exp_and_others")

            def gelus():
                act.preload_act_table_set("gelu_and_others")

            def before():
                logs()
                rstd0(0)
                act.wait_ge(R["loaded"], 48)
                act.activation(neg_a0[:, :], w("A0"), ACT.Exp).then_inc(R["setup_ev"], 1)
                act.activation(neg_a1[:, :], w("A1"), ACT.Exp).then_inc(R["setup_done"], 1)
                act.wait_ge(R["setup_ps"], 1)
                for n in range(2):
                    cp = act.activation(tile(xi, n, 512), P0[n][:, :], ACT.Copy)
                cp.then_inc(R["setup_ev"], 1)
                act.wait_ge(R["setup_ps"], 3)
                act.activation(Mdelta[:, :], P1[1][:, 0:128], ACT.Copy).then_inc(R["setup_ev"], 1)
                act.wait_ge(R["setup_ps"], 4)
                act.activation(MB[:, :], P1[2][:, 0:256], ACT.Copy).then_inc(R["setup_ev"], 1)
                act.activation(MC[:, :], P1[2][:, 256:512], ACT.Copy).then_inc(R["setup_ev"], 1)
                act.mul(w("uo"), w("uo"), 0.5).then_inc(R["setup_ev"], 1)
                act.wait_ge(R["setup_ev"], 6)
                act.mul(neg_a0[:, :], neg_a0[:, :], -1.0).then_inc(R["setup_done"], 1)

            def fold_heads(a, b):
                if a == 0:
                    act.wait_ge(R["heads_loaded"], 16)
                    act.activation(gates_xh[:, :], w("gates_x"), ACT.Copy).then_inc(R["gates_xh_ready"], 1)
                for m in range(a, b):
                    act.wait_ge(R["G_ps"], m + 1)
                    act.activation(tile((pair, GT)[m % 2], m // 2, 512), P1[m % 5][:, :], ACT.Copy, scale=HS ** -0.5)\
                        .then_inc(R["G_ready"], 1)
                if b == 8:
                    act.wait_ge(R["G_ready"], 8)
                    act.activation(Gh[:, :], pair[:, :], ACT.Copy).then_inc(R["Gh_ready"], 1)

            def rstd0(j):
                act.wait_ge(R["mv0_ready"], j + 1)
                act.activation(sm0[:, 0:4], view(mv0[:, :], "p (k s) -> p k s", s=2)[:, :, 1], ACT.Ln, bias=EPS)\
                    .then_inc(R["ln0_steps"], 1)
                act.wait_ge(R["ln0_steps"], 2 * j + 1)
                act.activation(sm0[:, 4:8], sm0[:, 0:4], ACT.Exp, scale=-0.5).then_inc(R["r0_ready"], 1)
                act.wait_ge(R["vr_steps"], 2 * j + 2)
                act.activation(sm0[:, 16:20], sm0[:, 12:16], ACT.Ln, bias=EPS).then_inc(R["ln0_steps"], 1)
                act.wait_ge(R["ln0_steps"], 2 * j + 2)
                act.activation(sm0[:, 20:24], sm0[:, 16:20], ACT.Exp, scale=-0.5).then_inc(R["q0_ready"], 1)

            def turned(j):
                if later(j):
                    act.wait_ge(R["z1_ps"], j)
                act.wait_ge(R["xnT_ps"], j + 1)
                act.activation(xnT[:, :], P0[0][:, :], ACT.Copy).then_inc(R["xnT_ready"], 1)
                if later(j):
                    act.wait_ge(R["u1_ps"], j)
                act.wait_ge(R["xhT_ps"], j + 1)
                act.activation(xhT[:, :], P0[1][:, :], ACT.Copy).then_inc(R["xhT_ready"], 1)

            def delta(j):
                act.wait_ge(R["delta_ps"], j + 1)
                if later(j):
                    act.wait_ge(R["delta_ready"], j)
                act.activation(sp0[:, :], P0[0][:, :], ACT.Abs).then_inc(R["sp0_steps"], 1)
                act.wait_ge(R["sp0_steps"], 3 * j + 1)
                act.activation(sp0[:, :], sp0[:, :], ACT.Exp, scale=-1.0).then_inc(R["sp0_steps"], 1)
                act.wait_ge(R["sp0_steps"], 3 * j + 2)
                act.activation(sp0[:, :], sp0[:, :], ACT.Ln, bias=1.0).then_inc(R["sp0_steps"], 1)

            def decay(j):
                act.wait_ge(R["delta_ready"], j + 1)
                act.activation(decay0[:, :], decay0[:, :], ACT.Exp, scale=neg_a0[:, 0:1]).then_inc(R["decay0_ready"], 1)

            def xi_copy(j):
                if later(j):
                    act.wait_ge(R["yd1_ready"], j)
                for q, bank in ((0, 1), (1, 2)):
                    act.wait_ge(R[f"xi{q}_ps"], j + 1)
                    act.activation(tile(xi, q, T), P0[bank][:, :], ACT.Copy).then_inc(R[f"xi{q}_ready"], 1)

            def gates0(j):
                for q, bank in ((0, 1), (1, 2)):
                    if later(j):
                        act.wait_ge(R[f"y{q}_ready"], j)
                    act.wait_ge(R[f"z{q}_ps"], j + 1)
                    act.activation(tile(th, q, T), P0[bank][:, :], ACT.Tanh, scale=0.5).then_inc(R[f"th{q}_ready"], 1)
                if later(j):
                    act.wait_ge(R["out0_ps"], j)
                for q in range(2):
                    act.wait_ge(R[f"u{q}_ps"], j + 1)
                    act.activation(tile(gelu, q, T), P0[q][:, :], ACT.Gelu, bias=bias_u[:, q:q + 1])\
                        .then_inc(R[f"g{q}_ready"], 1)

            def rstd(i, mv, sm, ready, ln, done):
                act.wait_ge(R[ready], i + 1)
                act.activation(sm[:, 0:4], view(mv, "p (k s) -> p k s", s=2)[:, :, 1], ACT.Ln, bias=EPS)\
                    .then_inc(R[ln], 1)
                act.wait_ge(R[ln], i + 1)
                act.activation(sm[:, 4:8], sm[:, 0:4], ACT.Exp, scale=-0.5).then_inc(R[done], 1)

            def rstd2(i):
                rstd(i, mv2[:, :], sm2, "mv2_ready", "ln2_ready", "r2_ready")

            def turned1(i):
                if later(i):
                    act.wait_ge(R["lev_ps"], 4 * i)
                    act.wait_ge(R["g_ps"], i)
                act.wait_ge(R["x1T_ps"], i + 1)
                act.activation(x1T[:, :], P1[0][:, :], ACT.Copy).then_inc(R["x1T_ready"], 1)
                act.activation(x1Th[:, :], P1[0][:, :], ACT.Copy).then_inc(R["x1Th_ready"], 1)

            def values(i):
                if later(i):
                    act.wait_ge(R["vbd_ready"], 4 * i)
                if later(i):
                    act.wait_ge(R["vp_ready"], i)
                if later(i):
                    act.wait_ge(R["hx_stored"], 16 * i)
                for n in range(TILES):
                    act.wait_ge(R["vdw_ps"], 4 * i + n + 1)
                    act.activation(tile(vdw, n, VDW), P1[(2 + n) % 5][:, 0:VDW], ACT.Copy)\
                        .then_inc(R["vdw_ready"], 1)

            def heads(i, a, b):
                for h in range(a, b):
                    if h == 0:
                        if later(i):
                            act.wait_ge(R["s_ps"], 4 * i)
                    act.wait_ge(R["gx_ps"], 16 * i + h + 1)
                    act.activation(tile(gx, h, T), head_bank(h)[:, :], ACT.Copy).then_inc(R["gx_copied"], 1)

            def gate_logs(i):
                act.wait_ge(R["dt_in"], i + 1)
                act.activation(dts[:, 64:128], dts[:, 0:64], ACT.Abs).then_inc(R["dt_act"], 1)
                act.wait_ge(R["dt_act"], 3 * i + 1)
                act.activation(dts[:, 128:192], dts[:, 64:128], ACT.Exp, scale=-1.0).then_inc(R["dt_act"], 1)
                act.wait_ge(R["dt_act"], 3 * i + 2)
                act.activation(dts[:, 192:256], dts[:, 128:192], ACT.Ln, bias=1.0).then_inc(R["dt_act"], 1)

            def lam_logs(i):
                if later(i):
                    act.wait_ge(R["nodes_ready"], i)
                if later(i):
                    act.wait_ge(R["self_ready"], i)
                if later(i):
                    act.wait_ge(R["alpha_steps"], 2 * i)
                act.wait_ge(R["vdw_ready"], 4 * i + 4)
                act.activation(view(lam[:, :], "p (k c) -> p k c", k=TILES),
                               view(vdw[:, :], "p (k c) -> p k c", k=TILES)[:, :, 128:288], ACT.Abs)\
                    .then_inc(R["lam_steps"], 1)
                act.wait_ge(R["lam_steps"], 3 * i + 1)
                act.activation(lam[:, :], lam[:, :], ACT.Exp, scale=-1.0).then_inc(R["lam_steps"], 1)
                act.wait_ge(R["lam_steps"], 3 * i + 2)
                act.activation(lam[:, :], lam[:, :], ACT.Ln, bias=1.0).then_inc(R["lam_steps"], 1)

            def level_decay(i):
                act.wait_ge(R["lev_neg"], i + 1)
                act.activation(e4[:, :], lev[:, :], ACT.Exp).then_inc(R["e4_ready"], 1)

            def pair_decay(i):
                act.wait_ge(R["diff_ready"], i + 1)
                act.activation(pair[:, :], pair[:, :], ACT.Abs).then_inc(R["diff_abs"], 1)
                act.wait_ge(R["diff_abs"], i + 1)
                act.activation(pair[:, :], pair[:, :], ACT.Exp, scale=-1.0).then_inc(R["decay_ready"], 1)

            def left_halves(i):
                if later(i):
                    act.wait_ge(R["m_ps"], 4 * i)
                if later(i):
                    act.wait_ge(R["n_ready"], i)
                for n in range(TILES):
                    cols = 384 if n == 3 else 512
                    act.wait_ge(R["r_ps"], 4 * i + n + 1)
                    act.activation(rs[:, 512 * n:512 * n + cols], P1[(3, 4, 0, 3)[n]][:, 0:cols], ACT.Copy)\
                        .then_inc(R["r_copied"], 1)

            def node_matrices(i):
                act.wait_ge(R["nodesT_ready"], i + 1)
                for g in range(4):
                    act.wait_ge(R["m_ps"], 4 * i + g + 1)
                    src = view(P1[(4, 0, 3, 4)[g]][:, 0:480], "p (a n e) -> p a n e", a=4, e=HD)
                    dst = view(ms[:, 0:1920], "p (n g a e) -> p g a n e", g=4, a=4, e=HD)[:, g]
                    for a in range(4):
                        cp = act.activation(dst[:, a], src[:, a], ACT.Copy)
                    cp.then_inc(R["m_copied"], 1)

            def project_out(i):
                act.wait_ge(R["ytT_ps"], i + 1)
                act.activation(ytT[:, :], P1[1][:, :], ACT.Copy).then_inc(R["ytT_ready"], 1)

            def recurrence(i, n):
                ps, done = (("f_ps", "tf_ready"), ("i_ps", "ti_ready"), ("g_ps", "tg_ready"))[n]
                act.wait_ge(R[ps], i + 1)
                act.activation((tf, ti, tg)[n][:, :], P0[n][:, :], ACT.Tanh, bias=w("gate_b", n, n + 1),
                               scale=(0.5, 0.5, 1.0)[n]).then_inc(R[done], 1)

            def end_tanh(b):
                act.wait_ge(R["end_sum"], b + 1)
                act.activation(end_hx[b], end_hx[b], ACT.Tanh).then_inc(R["end_tanh"], 1)

            def stages(i, j):
                if i is not None:
                    values(i)
                if i is not None and j is not None:
                    rstd0(j)
                if i is not None:
                    if j is None:
                        gate_logs(i)
                    heads(i, 0, 2)
                    if j is not None:
                        gate_logs(i)
                    heads(i, 2, 4)
                if j is not None:
                    turned(j)
                if i is not None:
                    heads(i, 4, 6)
                    lam_logs(i)
                if j is None:
                    gelus()
                    for n in range(3):
                        recurrence(i, n)
                    logs()
                if i is not None:
                    heads(i, 6, 8)
                if j is not None:
                    delta(j)
                if i is not None:
                    heads(i, 8, 10)
                    level_decay(i)
                    heads(i, 10, 12)
                else:
                    fold_heads(0, 5)
                if j is not None:
                    xi_copy(j)
                if i is not None:
                    heads(i, 12, 14)
                    if later(i):
                        rstd2(i - 1)
                if j is not None:
                    decay(j)
                if i is None:
                    fold_heads(5, 8)
                if i is not None:
                    heads(i, 14, H)
                    pair_decay(i)
                    left_halves(i)
                    node_matrices(i)
                gelus()
                if j is not None:
                    gates0(j)
                    logs()
                else:
                    for b in range(GROUPS[2][0]):
                        end_tanh(b)
                if j is not None:
                    rstd(j, mv1[:, :], sm1, "mv1_ready", "ln1_ready", "r1_ready")
                    if i is not None:
                        gelus()
                        for n in range(3):
                            recurrence(i, n)
                    turned1(j)
                    if i is not None:
                        logs()
                if i is not None:
                    project_out(i)

            def after():
                for b in range(*GROUPS[2]):
                    end_tanh(b)
                logs()
                rstd2(B - 1)
            schedule(act, stages, before, after)

        @block.vector
        def _(dve):
            def before():
                norm0(0)
                second_norm0(0)
                dve.wait_ge(R["loaded"], 48)
                b2 = w("b2", rows=32)
                steps = [0]

                def step(ins):
                    steps[0] += 1
                    ins.then_inc(R["folded"], 1)
                    dve.wait_ge(R["folded"], steps[0])

                part, rest = am[:, 0:128], am[:, 128:256]
                step(dve.memset(am[:, 256:384], 0.0))
                for n in range(3):
                    step(dve.tensor_copy(b2_b[:, :], b2 if n == 0 else rest))
                    step(dve.tensor_copy(part, b2_b[:, :]))
                    step(dve.tensor_tensor(rest, b2 if n == 0 else rest, part, ALU.subtract))
                    step(dve.scalar_tensor_tensor(am[:, 256:384], part, k("b2_part", n, n + 1, 32), am[:, 256:384],
                                                  ALU.mult, ALU.add))
                step(dve.tensor_copy(b2_b[:, :], am[:, 256:384]))
                step(dve.tensor_copy(expert_b[:, :], k("expert", rows=32)))
                step(dve.memset(oh[:, :], 0.0))
                step(dve.memset(ones[:, :], 1.0))
                dve.wait_ge(R["setup_ps"], 2)
                step(dve.tensor_tensor(bias_u[:, :], P1[0][:, 0:2], w("b1"), ALU.add))
                w1 = view(w("W1"), "p (e h) -> p e h", e=E)
                step(dve.tensor_tensor(w1, w1, spread(w("lns").unsqueeze(2), [128, E, HID]), ALU.mult))
                dl = w("Wvdw", 128, 288)
                step(dve.tensor_tensor(dl, dl, w("Lp"), ALU.mult))
                step(dve.tensor_scalar(w("Wout0"), w("Wout0"), 0.5, None, ALU.mult))
                step(dve.tensor_scalar(w("gates_c"), w("gates_c"), 0.5, None, ALU.mult))
                step(dve.tensor_scalar(w("gate_b", 0, 2), w("gate_b", 0, 2), 0.5, None, ALU.mult))
                step(dve.tensor_scalar(cell[:, :], spread(w("c0"), [128, T]), 2.0, None, ALU.mult))
                dve.wait_ge(R["setup_done"], 1)
                step(dve.tensor_scalar(neg_a1[:, :], neg_a1[:, :], -1.0, None, ALU.mult))
                dve.sem_inc(R["setup_done"], 1)
                dve.wait_ge(R["setup_done"], 3)

            def heads_low_part():
                dve.wait_ge(R["gates_xh_ready"], 1)
                dve.tensor_tensor(gates_xl[:, :], w("gates_x"), gates_xh[:, :], ALU.subtract).then_inc(R["gates_xl_ready"], 1)
                dve.wait_ge(R["Gh_ready"], 1)
                dve.tensor_tensor(Gl[:, :], pair[:, :], Gh[:, :], ALU.subtract).then_inc(R["Gl_ready"], 1)

            def stats(src, st, mv, st_ready, mv_ready, i):
                for n in range(TILES):
                    last = dve.bn_stats(st[:, 6 * n:6 * n + 6], tile(src, n))
                last.then_inc(R[st_ready], 1)
                if not isinstance(i, int):
                    dve.wait_ge(R["loaded"], 48)
                dve.wait_ge(R[st_ready], i + 1)
                for n in range(TILES):
                    last = dve.bn_aggr(mv[:, 2 * n:2 * n + 2], st[:, 6 * n:6 * n + 6])
                last.then_inc(R[mv_ready], 1)

            def normalise(dst, src, mv, r):
                for n in range(TILES):
                    last = dve.tensor_scalar(tile(dst, n), tile(src, n), mv[:, 2 * n:2 * n + 1], r[:, n:n + 1],
                                             ALU.subtract, ALU.mult)
                return last

            def norm0(j):
                dve.wait_ge(R["x_loaded"], 16 * (j + 1))
                stats(xin, st0, mv0, "st0_ready", "mv0_ready", j)
                dve.wait_ge(R["r0_ready"], j + 1)
                var, r = view(mv0[:, :], "p (k s) -> p k s", s=2)[:, :, 1], sm0[:, 4:8]
                dve.tensor_tensor(sm0[:, 8:12], var, r, ALU.mult).then_inc(R["vr_steps"], 1)
                if later(j):
                    dve.wait_ge(R["xnT_ps"], j)
                dve.wait_ge(R["vr_steps"], 2 * j + 1)
                dve.tensor_tensor(sm0[:, 12:16], sm0[:, 8:12], r, ALU.mult).then_inc(R["vr_steps"], 1)
                normalise(xn, xin, mv0, r).then_inc(R["xn_ready"], 1)

            def second_norm0(j):
                dve.wait_ge(R["q0_ready"], j + 1)
                dve.tensor_tensor(sm0[:, 24:28], sm0[:, 20:24], sm0[:, 4:8], ALU.mult).then_inc(R["rr_ready"], 1)
                if later(j):
                    dve.wait_ge(R["xhT_ps"], j)
                dve.wait_ge(R["rr_ready"], j + 1)
                normalise(xh, xin, mv0, sm0[:, 24:28]).then_inc(R["xh_ready"], 1)

            def turn_logits(j):
                dve.wait_ge(R["logit_ps"], j + 1)
                dve.transpose(lgT[:, :], P0[2][0:32, :]).then_inc(R["top1_steps"], 1)

            def top1(j):
                lg = view(lgT[:, :], "p (c e) -> p c e", e=32)[:, :, 0:E]
                eq = view(am[:, 0:128], "p (c e) -> p c e", e=E)
                val = view(am[:, 128:256], "p (c e) -> p c e", e=E)
                mx, mx2 = am[:, 512:528], am[:, 528:544]
                dve.wait_ge(R["top1_steps"], 7 * j + 1)
                dve.tensor_reduce(mx, lg, AX.X, ALU.max).then_inc(R["top1_steps"], 1)
                dve.wait_ge(R["top1_steps"], 7 * j + 2)
                dve.tensor_tensor(eq, lg, spread(mx.unsqueeze(2), [32, 16, E]), ALU.is_ge).then_inc(R["top1_steps"], 1)
                dve.wait_ge(R["top1_steps"], 7 * j + 3)
                dve.tensor_tensor(val, eq, spread(k("rank", rows=32).unsqueeze(1), [32, 16, E]), ALU.mult)\
                    .then_inc(R["top1_steps"], 1)
                dve.wait_ge(R["top1_steps"], 7 * j + 4)
                dve.tensor_reduce(mx2, val, AX.X, ALU.max).then_inc(R["top1_steps"], 1)
                dve.wait_ge(R["top1_steps"], 7 * j + 5)
                rows = view(oh[:, :], "p (c r e) -> p c r e", c=16, e=E)
                for r in range(3):
                    last = dve.tensor_tensor(rows[:, :, r], val, spread(mx2.unsqueeze(2), [32, 16, E]), ALU.is_equal)
                last.then_inc(R["top1_steps"], 1)
                dve.wait_ge(R["top1_steps"], 7 * j + 6)
                dve.transpose(ohT[:, :], oh[:, :]).then_inc(R["ohT_ready"], 1)
                dve.wait_ge(R["ohT_ready"], j + 1)
                if later(j):
                    dve.wait_ge(R["out0_ps"], j)
                dve.tensor_copy(oh_b[:, :], ohT[:, :])
                dve.tensor_scalar(mask_b[:, :], ohT[:, :], 1.0, BIG, ALU.subtract, ALU.mult)\
                    .then_inc(R["top1_steps"], 1)

            def delta(j):
                dve.wait_ge(R["sp0_steps"], 3 * j + 3)
                if later(j):
                    dve.wait_ge(R["h1_ready"], j)
                dve.scalar_tensor_tensor(decay0[:, :], P0[0][:, :], 0.0, sp0[:, :], ALU.max, ALU.add)\
                    .then_inc(R["delta_ready"], 1)

            def scan_inputs(j):
                if later(j):
                    dve.wait_ge(R["out0_ps"], j)
                for q, bank in ((0, 0), (1, 1)):
                    dve.wait_ge(R[f"b{q}_ps"], j + 1)
                    dve.wait_ge(R[f"xi{q}_ready"], j + 1)
                    dve.tensor_tensor(tile(y, q, T), P0[bank][:, :], tile(xi, q, T), ALU.mult)\
                        .then_inc(R[f"bx{q}_ready"], 1)

            def scans(j):
                dve.wait_ge(R["decay0_ready"], j + 1)
                for q in range(2):
                    dve.wait_ge(R[f"bx{q}_ready"], j + 1)
                    dve.tensor_tensor_scan(tile(y, q, T), decay0[:, :], tile(y, q, T), 0.0, ALU.mult, ALU.add)\
                        .then_inc(R[f"h{q}_ready"], 1)
                for q, bank in ((0, 2), (1, 0)):
                    dve.wait_ge(R[f"c{q}_ps"], j + 1)
                    dve.wait_ge(R[f"h{q}_ready"], j + 1)
                    dve.tensor_tensor(tile(y, q, T), P0[bank][:, :], tile(y, q, T), ALU.mult)\
                        .then_inc(R[f"ch{q}_ready"], 1)

            def gate0(j, q):
                dve.wait_ge(R[f"th{q}_ready"], j + 1)
                dve.scalar_tensor_tensor(tile(th, q, T), tile(th, q, T), 1.0, P0[1 + q][:, :], ALU.add, ALU.mult)\
                    .then_inc(R[f"sz{q}_ready"], 1)
                dve.wait_ge(R[f"sz{q}_ready"], j + 1)
                dve.wait_ge(R[f"yd{q}_ready"], j + 1)
                dve.tensor_tensor(tile(y, q, T), tile(y, q, T), tile(th, q, T), ALU.mult)\
                    .then_inc(R[f"y{q}_ready"], 1)

            def sum0(j):
                dve.wait_ge(R["out0_ps"], j + 1)
                if later(j):
                    dve.wait_ge(R["res_init"], j)
                dve.tensor_tensor(x1[:, :], P0[2][:, :], xin[:, :], ALU.add).then_inc(R["x1_ready"], 1)

            def norm1(i):
                dve.wait_ge(R["x1_ready"], i + 1)
                stats(x1, st1, mv1, "st1_ready", "mv1_ready", i)
                dve.wait_ge(R["r1_ready"], i + 1)
                if later(i):
                    dve.wait_ge(R["skip_ready"], i)
                    dve.wait_ge(R["r_ps"], 4 * i)
                normalise(xn1, x1, mv1, sm1[:, 4:8]).then_inc(R["xn1_ready"], 1)

            def gate_inputs(i):
                c = lambda n: dts[:, 64 * n:64 * n + 64]
                heads = lambda ap: view(ap, "p (k h) -> p k h", k=TILES)
                if later(i):
                    dve.wait_ge(R["y1_ps"], 4 * i)
                dve.wait_ge(R["vdw_ready"], 4 * i + 4)
                dve.tensor_tensor(heads(c(0)), view(vdw[:, :], "p (k c) -> p k c", k=TILES)[:, :, 288:304],
                                  spread(w("dtb").unsqueeze(1), [128, TILES, H]), ALU.add).then_inc(R["dt_in"], 1)

            def gates1(i):
                c = lambda n: dts[:, 64 * n:64 * n + 64]
                heads = lambda ap: view(ap, "p (k h) -> p k h", k=TILES)
                dve.wait_ge(R["dt_act"], 3 * i + 2)
                dve.tensor_scalar(c(4), c(2), 1.0, 1.0, ALU.add, ALU.subtract).then_inc(R["dt_steps"], 1)
                dve.wait_ge(R["dt_act"], 3 * i + 3)
                dve.wait_ge(R["dt_steps"], 6 * i + 1)
                dve.scalar_tensor_tensor(c(5), c(4), 0.0, c(4), ALU.is_equal, ALU.add).then_inc(R["dt_steps"], 1)
                dve.scalar_tensor_tensor(c(6), c(4), 0.0, c(3), ALU.is_equal, ALU.add)
                dve.wait_ge(R["dt_steps"], 6 * i + 2)
                dve.reciprocal(c(7), c(5)).then_inc(R["dt_steps"], 1)
                dve.wait_ge(R["dt_steps"], 6 * i + 3)
                dve.tensor_tensor(c(7), c(7), c(2), ALU.mult).then_inc(R["dt_steps"], 1)
                dve.wait_ge(R["dt_steps"], 6 * i + 4)
                dve.tensor_tensor(c(7), c(7), c(6), ALU.mult).then_inc(R["dt_steps"], 1)
                dve.wait_ge(R["dt_steps"], 6 * i + 5)
                dve.scalar_tensor_tensor(c(8), c(0), 0.0, c(7), ALU.max, ALU.add).then_inc(R["dt_steps"], 1)
                dve.wait_ge(R["dt_steps"], 6 * i + 6)
                dve.tensor_tensor(heads(c(9)), heads(c(8)), spread(neg_a1[:, :].unsqueeze(1), [128, TILES, H]), ALU.mult)\
                    .then_inc(R["g_ready"], 1)

            def lam_sum(i):
                dve.wait_ge(R["lam_steps"], 3 * i + 3)
                l = view(lam[:, :], "p (k c) -> p k c", k=TILES)
                dve.scalar_tensor_tensor(l, view(vdw[:, :], "p (k c) -> p k c", k=TILES)[:, :, 128:288], 0.0, l,
                                         ALU.max, ALU.add).then_inc(R["lam_ready"], 1)

            def node_lams(i):
                dve.wait_ge(R["lam_ready"], i + 1)
                if later(i):
                    dve.wait_ge(R["lev_ps"], 4 * i)
                l = view(lam[:, :], "p (m l) -> p m l", l=LEVELS)
                nd = view(nodes[:, :], "p (m n) -> p m n", n=NODES)
                at = 0
                for level in range(5, 0, -1):
                    count = (CHUNK >> level) + (level == 1)
                    last = dve.tensor_tensor(nd[:, :, at:at + count], spread(l[:, :, level:level + 1], [128, 64, count]),
                                             spread(k("right", at, at + count).unsqueeze(1), [128, 64, count]), ALU.mult)
                    at += count
                last.then_inc(R["nodes_ready"], 1)

            def node_rows(i):
                dve.wait_ge(R["nodes_ready"], i + 1)
                if later(i):
                    dve.wait_ge(R["lam_ps"], 4 * i)
                dve.transpose(nodesT[:, :], nodes[:, :]).then_inc(R["nodesT_ready"], 1)

            def sums(i):
                if later(i):
                    dve.wait_ge(R["y2_ps"], 4 * i)
                dve.wait_ge(R["gT_ps"], i + 1)
                dve.tensor_tensor_scan(cgC[:, :], spread(ones[:, 0:1], [16, T]), P1[1][0:16, :], 0.0, ALU.mult, ALU.add)\
                    .then_inc(R["cgC_ready"], 1)

            def token_sums(i):
                dve.wait_ge(R["cgT_ps"], i + 1)
                if later(i):
                    dve.wait_ge(R["diff_ready"], i)
                dve.tensor_copy(cgt[:, :], P1[2][:, 0:64]).then_inc(R["cgt_ready"], 1)

            def level_factors(i):
                dve.wait_ge(R["cgc_ps"], i + 1)
                P = P1[2]
                dve.tensor_tensor(view(lev[:, 0:128], "p (a m) -> p a m", a=2), view(P[:, 64:192], "p (a m) -> p a m", a=2),
                                  spread(cgt[:, :].unsqueeze(1), [128, 2, 64]), ALU.subtract)
                dve.tensor_tensor(view(lev[:, 128:192], "p (a b h) -> p a b h", a=2, b=2),
                                  spread(view(P[:, 192:224], "p (a h) -> p a h", a=2).unsqueeze(2), [128, 2, 2, H]),
                                  view(cgt[:, :], "p (a b h) -> p a b h", a=2, b=2), ALU.subtract)
                dve.tensor_tensor(view(lev[:, 192:256], "p (a h) -> p a h", a=TILES),
                                  spread(P[:, 224:240].unsqueeze(1), [128, TILES, H]),
                                  view(cgt[:, :], "p (a h) -> p a h", a=TILES), ALU.subtract).then_inc(R["lev_diff"], 1)
                dve.wait_ge(R["lev_diff"], i + 1)
                dve.scalar_tensor_tensor(lev[:, :], lev[:, :], -1.0, lev[:, :], ALU.mult, ALU.min)\
                    .then_inc(R["lev_neg"], 1)

            def level_weights(i):
                dve.wait_ge(R["lam_ready"], i + 1)
                for n in range(TILES):
                    last = dve.tensor_tensor(view(alpha[:, :], "p (l k h) -> p l k h", l=4, k=TILES)[:, :, n],
                                             view(lam[:, :], "p (k h l) -> p k l h", k=TILES, l=LEVELS)[:, n, 6:10],
                                             spread(view(k("alpha_mask"), "p (l k) -> p l k", l=4)[:, :, n:n + 1], [128, 4, H]),
                                             ALU.mult)
                last.then_inc(R["alpha_steps"], 1)
                dve.wait_ge(R["e4_ready"], i + 1)
                dve.wait_ge(R["alpha_steps"], 2 * i + 1)
                dve.tensor_tensor(alpha[:, :], alpha[:, :], e4[:, :], ALU.mult).then_inc(R["alpha_steps"], 1)
                bt = view(beta[:, :], "p (k s h) -> p k s h", k=TILES, s=5)
                bm = view(k("beta_mask"), "p (k s) -> p k s", k=TILES)
                e = view(e4[:, :], "p (l k h) -> p k l h", l=4, k=TILES)
                if later(i):
                    dve.wait_ge(R["vp_ready"], i)
                dve.tensor_tensor(bt[:, :, 0:2], spread(e[:, :, 0:1], [128, TILES, 2, H]),
                                  spread(bm[:, :, 0:2].unsqueeze(3), [128, TILES, 2, H]), ALU.mult)
                dve.tensor_tensor(bt[:, :, 2:5], e[:, :, 1:4],
                                  spread(bm[:, :, 2:5].unsqueeze(3), [128, TILES, 3, H]), ALU.mult).then_inc(R["beta_ready"], 1)

            def token_rows(i):
                dve.wait_ge(R["cgt_ready"], i + 1)
                if later(i):
                    dve.wait_ge(R["y1_ps"], 4 * i)
                dve.transpose(view(pair[:, :], "p (m t) -> p m t", t=CHUNK), spread(cgt[:, :].unsqueeze(2), [128, 64, CHUNK]))\
                    .then_inc(R["cgrow_ready"], 1)

            def pair_weights(i, n):
                if n == 0:
                    dve.wait_ge(R["decay_ready"], i + 1)
                dve.wait_ge(R["lam_ps"], 4 * i + n + 1)
                dve.tensor_tensor(tile(pair, n, 512), tile(pair, n, 512), P1[2][:, :], ALU.mult)\
                    .then_inc(R["dlam_ready"], 1)
                if n == 0:
                    dve.wait_ge(R["self_ready"], i + 1)
                dve.wait_ge(R["dlam_ready"], 4 * i + n + 1)
                dve.tensor_tensor(tile(pair, n, 512), tile(pair, n, 512), tile(self_lam, n, 512), ALU.add)\
                    .then_inc(R["lams_ready"], 1)
                dve.wait_ge(R["s_ps"], 4 * i + n + 1)
                dve.wait_ge(R["lams_ready"], 4 * i + n + 1)
                dve.tensor_tensor(tile(pair, n, 512), tile(pair, n, 512), P1[1][:, :], ALU.mult)\
                    .then_inc(R["w_ready"], 1)

            def level_sum(i, n):
                dve.wait_ge(R["lev_ps"], 4 * i + n + 1)
                al = view(alpha[:, :], "p (l k h) -> p k l h", l=4, k=TILES)[:, n]
                runs = [[(0, 0, 2)], [(0, 0, 3)], [(0, 0, 2), (2, 3, 1)], [(0, 0, 4)]][n]
                for at, level, count in runs:
                    o = view(lv[:, 128 * at:128 * (at + count)], "p (l h e) -> p l h e", l=count, e=HD)
                    p = view(P1[0][:, 128 * at:128 * (at + count)], "p (l h e) -> p l h e", l=count, e=HD)
                    last = dve.tensor_tensor(o, p, spread(al[:, level:level + count].unsqueeze(3), [128, count, H, HD]),
                                             ALU.mult)
                last.then_inc(R["lev_ready"], 1)
                dve.wait_ge(R["lev_ready"], 4 * i + n + 1)
                count = sum(r[2] for r in runs)
                dve.tensor_reduce(lvs[:, :], view(lv[:, 0:128 * count], "p (l v) -> p v l", l=count), AX.X, ALU.add)\
                    .then_inc(R["levsum_ready"], 1)

            def own_heads(i, n):
                dve.wait_ge(R["y1_ps"], 4 * i + n + 1)
                if later(i, n // 2):
                    dve.wait_ge(R["y2_ps"], 4 * i + n - 1)
                dve.tensor_tensor(view(tile(ym, n % 2, 512), "p (m a e) -> p m a e", m=16, a=4),
                                  view(P1[3][:, :], "p (m a e) -> p m a e", m=16, a=4),
                                  spread(k("own_head").unsqueeze(1).unsqueeze(3), [128, 16, 4, HD]), ALU.mult)\
                    .then_inc(R["ym_ready"], 1)

            def tile_sum(i, n):
                dve.wait_ge(R["y2_ps"], 4 * i + n + 1)
                dve.wait_ge(R["levsum_ready"], 4 * i + n + 1)
                if n == 0:
                    if later(i):
                        dve.wait_ge(R["ytT_ps"], i)
                dve.tensor_tensor(tile(yt, n), lvs[:, :], P1[4][:, 0:128], ALU.add).then_inc(R["yt_ready"], 1)

            def attention_out(i):
                dve.wait_ge(R["wo_ps"], i + 1)
                if later(i):
                    dve.wait_ge(R["n_ready"], i)
                dve.tensor_tensor(ob[:, :], P1[1][:, :], skip[:, :], ALU.add).then_inc(R["ob_ready"], 1)

            def stats2(i):
                dve.wait_ge(R["ob_ready"], i + 1)
                stats(ob, st2, mv2, "st2_ready", "mv2_ready", i)

            def norm2(i):
                dve.wait_ge(R["r2_ready"], i + 1)
                normalise(skip, ob, mv2, sm2[:, 4:8]).then_inc(R["n_ready"], 1)

            def recurrence(i):
                dve.wait_ge(R["tf_ready"], i + 1)
                if later(i):
                    dve.wait_ge(R["c_ready"], i)
                dve.scalar_tensor_tensor(tf[:, :], tf[:, :], 1.0, cell[:, :], ALU.add, ALU.mult)
                dve.wait_ge(R["tg_ready"], i + 1)
                dve.wait_ge(R["ti_ready"], i + 1)
                dve.scalar_tensor_tensor(ti[:, :], ti[:, :], 1.0, tg[:, :], ALU.add, ALU.mult).then_inc(R["ig_ready"], 1)
                dve.wait_ge(R["ig_ready"], i + 1)
                dve.wait_ge(R["g_ps"], i + 1)
                dve.scalar_tensor_tensor(cell[:, :], tf[:, :], 0.5, ti[:, :], ALU.mult, ALU.add).then_inc(R["c_ready"], 1)

            def cell_out():
                dve.wait_ge(R["cp_ps"], 1)
                dve.tensor_tensor(view(c_out[:, :], "p (k d) -> p k d", d=D), view(P0[0][:, :], "p (k d) -> p k d", d=D),
                                  spread(w("bo").unsqueeze(1), [128, TILES, D]), ALU.add).then_inc(R["cp_ready"], 1)

            def end_add(b):
                dve.wait_ge(R["end_tanh"], b + 1)
                if b == B - 1:
                    dve.wait_ge(R["res_ready"], B)
                dve.tensor_tensor(end_hx[b], end_hx[b], end_res[b], ALU.add).then_inc(R["end_add"], 1)

            def stages(i, j):
                if i is not None and j is not None:
                    norm0(j)
                if i is not None:
                    gate_inputs(i)
                if i is not None and j is not None:
                    second_norm0(j)
                if i is not None:
                    gates1(i)
                    if later(i):
                        attention_out(i - 1)
                    sums(i)
                    token_sums(i)
                    token_rows(i)
                if j is not None:
                    turn_logits(j)
                if i is not None:
                    level_factors(i)
                    lam_sum(i)
                if j is not None:
                    delta(j)
                else:
                    recurrence(i)
                if i is not None:
                    level_weights(i)
                    if later(i):
                        stats2(i - 1)
                    node_lams(i)
                if j is not None:
                    scan_inputs(j)
                if i is not None:
                    if later(i):
                        norm2(i - 1)
                    node_rows(i)
                if j is not None:
                    scans(j)
                else:
                    cell_out()
                if i is not None:
                    pair_weights(i, 0)
                if j is not None:
                    top1(j)
                if i is not None:
                    own_heads(i, 0)
                    pair_weights(i, 1)
                    level_sum(i, 0)
                    tile_sum(i, 0)
                if j is not None:
                    gate0(j, 0)
                if i is not None:
                    own_heads(i, 1)
                    pair_weights(i, 2)
                    level_sum(i, 1)
                    tile_sum(i, 1)
                if j is not None:
                    gate0(j, 1)
                if i is not None:
                    own_heads(i, 2)
                    level_sum(i, 2)
                    pair_weights(i, 3)
                    tile_sum(i, 2)
                    level_sum(i, 3)
                if i is None:
                    heads_low_part()
                if j is not None:
                    sum0(j)
                    norm1(j)
                if i is not None:
                    own_heads(i, 3)
                    tile_sum(i, 3)
                    if j is not None:
                        recurrence(i)

            def after():
                for b in range(GROUPS[2][0]):
                    end_add(b)
                attention_out(B - 1)
                stats2(B - 1)
                for b in range(GROUPS[2][0], B - 1):
                    end_add(b)
                norm2(B - 1)
                end_add(B - 1)
            schedule(dve, stages, before, after)

        @block.gpsimd
        def _(pool):
            def residual(j):
                pool.wait_ge(R["x1_ready"], j + 1)
                if later(j):
                    pool.wait_ge(R["res_stored"], 16 * j)
                pool.tensor_tensor(view(res[:, :], "p (k d) -> p k d", d=D), view(x1[:, :], "p (k d) -> p k d", d=D),
                                   spread(w("lnbias").unsqueeze(1), [128, TILES, D]), ALU.add).then_inc(R["res_init"], 1)

            def low_part(i):
                pool.wait_ge(R["loaded"], 48)
                pool.wait_ge(R["x1Th_ready"], i + 1)
                pool.tensor_tensor(x1Tl[:, :], x1T[:, :], x1Th[:, :], ALU.subtract).then_inc(R["x1Tl_ready"], 1)

            def own_values(i):
                pool.wait_ge(R["vdw_ready"], 4 * i + 4)
                if later(i):
                    pool.wait_ge(R["y1_ps"], 4 * i)
                for n in range(TILES):
                    v = view(vdw[:, VDW * n:VDW * n + 128], "p (g v) -> p g v", g=4)
                    pool.tensor_tensor(view(tile(vbd, n, 512), "p (g c v) -> p g c v", g=4, c=4),
                                       spread(v.unsqueeze(2), [128, 4, 4, 32]),
                                       spread(k("own_chunk").unsqueeze(1).unsqueeze(3), [128, 4, 4, 32]), ALU.mult)\
                        .then_inc(R["vbd_ready"], 1)

            def own_level(i):
                pool.wait_ge(R["lam_ready"], i + 1)
                if later(i):
                    pool.wait_ge(R["lams_ready"], 4 * i)
                pool.tensor_tensor(view(self_lam[:, :], "p (m t) -> p m t", t=CHUNK),
                                   spread(view(lam[:, :], "p (m l) -> p m l", l=LEVELS)[:, :, 0:1], [128, 64, CHUNK]),
                                   spread(k("diag").unsqueeze(1), [128, 64, CHUNK]), ALU.mult).then_inc(R["self_ready"], 1)

            def skip_terms(j):
                pool.wait_ge(R["bx1_ready"], j + 1)
                xq = view(xi[:, :], "p (q t) -> p q t", q=2)
                pool.tensor_tensor(xq, xq, spread(w("Dskip").unsqueeze(2), [128, 2, T]), ALU.mult).then_inc(R["dxi_ready"], 1)

            def scan_skip(j):
                for q in range(2):
                    pool.wait_ge(R[f"ch{q}_ready"], j + 1)
                    pool.wait_ge(R["dxi_ready"], j + 1)
                    pool.tensor_tensor(tile(y, q, T), tile(xi, q, T), tile(y, q, T), ALU.add)\
                        .then_inc(R[f"yd{q}_ready"], 1)

            def pair_differences(i):
                pool.wait_ge(R["loaded"], 48)
                pool.wait_ge(R["cgrow_ready"], i + 1)
                pw = view(pair[:, :], "p (m t) -> p m t", t=CHUNK)
                pool.tensor_tensor(pw, pw, spread(cgt[:, :].unsqueeze(2), [128, 64, CHUNK]), ALU.subtract)\
                    .then_inc(R["diff_ready"], 1)

            def level_values(i):
                if later(i):
                    pool.wait_ge(R["r_ps"], 4 * i)
                pool.wait_ge(R["beta_ready"], i + 1)
                at = 0
                for n, runs in enumerate((((0, 5),), ((0, 3), (4, 1)), ((0, 4),), ((0, 3),))):
                    v = view(vdw[:, VDW * n:VDW * n + 128], "p (h e) -> p h e", e=HD)
                    bt = view(beta[:, 80 * n:80 * n + 80], "p (s h) -> p s h", h=H)
                    for slot, count in runs:
                        last = pool.tensor_tensor(view(vp[:, at:at + 128 * count], "p (s h e) -> p s h e", s=count, e=HD),
                                                  spread(v.unsqueeze(1), [128, count, H, HD]),
                                                  spread(bt[:, slot:slot + count].unsqueeze(3), [128, count, H, HD]),
                                                  ALU.mult)
                        at += 128 * count
                last.then_inc(R["vp_ready"], 1)

            def keep_skip(i):
                pool.wait_ge(R["loaded"], 48)
                if later(i):
                    pool.wait_ge(R["ob_ready"], i)
                pool.tensor_copy(skip[:, :], xn1[:, :]).then_inc(R["skip_ready"], 1)

            def finish(i):
                pool.wait_ge(R["n_ready"], i + 1)
                pool.tensor_tensor(view(skip[:, :], "p (k d) -> p k d", d=D), view(skip[:, :], "p (k d) -> p k d", d=D),
                                   spread(w("lng").unsqueeze(1), [128, TILES, D]), ALU.mult).then_inc(R["ng_ready"], 1)
                pool.wait_ge(R["ng_ready"], i + 1)
                pool.tensor_tensor(res[:, :], res[:, :], skip[:, :], ALU.add).then_inc(R["res_ready"], 1)

            def end_sum(b):
                pool.tensor_tensor(end_hx[b], end_hx[b], c_out[:, :], ALU.add).then_inc(R["end_sum"], 1)

            def stages(i, j):
                if i is None:
                    skip_terms(j)
                    scan_skip(j)
                    return
                low_part(i)
                own_values(i)
                pair_differences(i)
                level_values(i)
                own_level(i)
                if j is not None:
                    skip_terms(j)
                if later(i):
                    finish(i - 1)
                if j is not None:
                    scan_skip(j)
                residual(i)
                keep_skip(i)
                if j is None:
                    pool.wait_ge(R["cp_ready"], 1)
                    for group, (a, b) in enumerate(GROUPS):
                        pool.wait_ge(R[f"end_loaded{group}"], 16 * (2 * (b - a) - (b == B)))
                        for n in range(a, b):
                            end_sum(n)

            schedule(pool, stages, lambda: None, lambda: finish(B - 1))


def _columns_of(a, rows=128):
    n = a.shape[0] // rows
    return a.reshape(n, rows, -1).transpose(1, 0, 2).reshape(rows, -1)


def _pack(columns, parts):
    at, width = _offsets(columns)
    out = np.zeros((128, width), np.float32)
    for name, a in parts.items():
        out[:a.shape[0], at[name][0]:at[name][0] + a.shape[1]] = a
    return out


def _consts():
    p = np.arange(128)
    q, c = p % CHUNK, p // CHUNK
    ident = np.eye(128, dtype=np.float32)
    end6, end7 = 64 * (p // 64) + 31, np.full(128, 63)
    left = np.zeros((128, 128), np.float32)
    right = np.zeros((128, NODES), np.float32)
    at = 0
    for level in range(5, 0, -1):
        size = 1 << level
        for m in range(CHUNK // size):
            inside = (q // size == m)
            first = q % size < size // 2
            right[:, at] = inside & ~first
            for chunk in range(4):
                left[32 * chunk + at, :] = inside & first & (c == chunk)
            at += 1
    alpha = np.zeros((128, 4, TILES), np.float32)
    alpha[:, 0] = (p % 64 >= 32)[:, None]
    alpha[:, 1] = (p >= 64)[:, None]
    alpha[:, 2, 1::2] = 1
    alpha[:, 3, 2:] = 1
    beta = np.zeros((128, TILES, 5), np.float32)
    beta[:, :, 0] = (p < 32)[:, None]
    beta[:, :, 1] = ((p >= 64) & (p < 96))[:, None]
    beta[:, :, 2] = (p < 64)[:, None]
    beta[:, 0::2, 3] = 1
    beta[:, 0:2, 4] = 1
    expert = np.zeros((8, E * HID), np.float32)
    for e in range(E):
        expert[e, HID * e:HID * e + HID] = 1
    parts = {
        "ident": ident, "sel6": (p[:, None] == end6[None]).astype(np.float32),
        "sel7": (p[:, None] == end7[None]).astype(np.float32),
        "sel_last": np.repeat((p == 127)[:, None], 128, 1).astype(np.float32),
        "left": left, "right": right, "diag": (q[:, None] == np.arange(CHUNK)).astype(np.float32),
        "own_chunk": (c[:, None] == np.arange(4)).astype(np.float32),
        "own_head": (c[:, None] == np.arange(4)).astype(np.float32),
        "sum_heads": (q[:, None] == np.arange(CHUNK)).astype(np.float32),
        "alpha_mask": alpha.reshape(128, -1), "beta_mask": beta.reshape(128, -1),
        "rank": np.repeat((E - np.arange(E, dtype=np.float32))[None], 32, 0), "expert": expert,
        "b2_part": (np.arange(24)[:, None] // 8 == np.arange(3)).astype(np.float32),
    }
    return _pack(_const_columns(), parts)


def kernel(**inputs):
    import numpy as _np
    import concourse.bacc as _bacc
    from concourse import mybir as _mybir
    from concourse.bass_utils import run_bass_kernel_spmd as _run

    a = {n: _np.asarray(v) for n, v in inputs.items()}
    rows = lambda v, n=128: _np.repeat(v.reshape(1, -1), n, 0)
    heads = lambda v: _np.concatenate([_columns_of(v[:H * HS // 2], HS), _columns_of(v[H * HS // 2:], HS)], 0)
    w_xp = a["L0_attn_W_xp"]
    parts = {
        "Win": a["L0_attn_W_in"], "wdelta": _columns_of(w_xp[:, 0:1]), "Dskip": _columns_of(a["L0_attn_D"][:, None]),
        "A0": rows(a["L0_attn_A_log"]), "WgT": a["L0_ffn_Wg"].T,
        "W1": a["L0_ffn_W1"].transpose(1, 0, 2).reshape(D, -1), "lns": a["L0_ffn_ln_scale"].T,
        "lnb": a["L0_ffn_ln_bias"].T, "b1": _columns_of(a["L0_ffn_b1"].reshape(-1, 1)),
        "Wout0": _columns_of(a["L0_attn_W_out"]), "W2": _columns_of(a["L0_ffn_W2"].reshape(E * HID, D)),
        "b2": _np.concatenate([a["L0_ffn_b2"]] * 3, 0),
        "WinT": _columns_of(a["L0_attn_W_in"][:, :INNER].T), "WxpT": w_xp[:, 1:].T,
        "WBC": _np.concatenate([a["L0_attn_W_B"], a["L0_attn_W_C"]], 0),
        "Wvdw": _np.concatenate([a["L1_attn_Wv"].T,
                                 a["L1_attn_Wdl"].reshape(H, 12, D)[:, :LEVELS].reshape(-1, D).T,
                                 a["L1_attn_Wdt"].T, a["L1_ffn_wo"].T], 1),
        "Lp": rows(a["L1_attn_Lp"][:, :LEVELS]), "dtb": rows(a["L1_attn_dt_bias"]), "A1": rows(a["L1_attn_A_log"]),
        "lng": rows(a["L1_attn_ln_g"]), "lnbias": rows(a["L1_attn_ln_b"]), "WoutT": a["L1_attn_Wout"].T,
        "gates_x": _np.concatenate([a["L1_ffn_wf"].T, a["L1_ffn_wi"].T, a["L1_ffn_wc"].T], 1),
        "gates_c": _np.concatenate([a["L1_ffn_uf"].T, a["L1_ffn_ui"].T, a["L1_ffn_uc"].T], 1),
        "gate_b": _np.stack([a["L1_ffn_bf"], a["L1_ffn_bi"], a["L1_ffn_bc"]], 1),
        "uo": a["L1_ffn_uo"].T, "bo": rows(a["L1_ffn_bo"]), "c0": a["L1_ffn_in_c"][:, None],
        "Wq": heads(a["L1_attn_Wq"]), "Wk": heads(a["L1_attn_Wk"]),
    }
    arrays = {
        "in_x": _np.ascontiguousarray(a["L0_attn_x"]),
        "in_weights": _pack(_weight_columns(), parts),
        "in_consts": _consts(),
    }
    nc = _bacc.Bacc("TRN2", target_bir_lowering=False, num_devices=1)
    fp32 = _mybir.dt.float32
    args = [nc.dram_tensor(name, v.shape, fp32, kind="ExternalInput").ap() for name, v in arrays.items()]
    args.append(nc.dram_tensor("out_0", (B, T, D), fp32, kind="ExternalOutput").ap())
    build(nc, *args)
    r = _run(nc, [arrays], core_ids=[0])
    return r.results[0]["out_0"]
```
